# Optimizing a Trainium2 kernel written in Bass

```python
import numpy as np
import jax
import jax.numpy as jnp

def _softmax(x, axis=-1):
    return jax.nn.softmax(x, axis=axis)

def _gelu(x):
    return jax.nn.gelu(x, approximate=True)

def _silu(x):
    return jax.nn.silu(x)

def _sigmoid(x):
    return jax.nn.sigmoid(x)

def _layernorm(x, axis=-1, eps=1e-05):
    m = jnp.mean(x, axis=axis, keepdims=True)
    v = jnp.var(x, axis=axis, keepdims=True)
    return (x - m) / jnp.sqrt(v + eps)

def _scatter_add(tgt, idx, src, axis=0):
    return tgt.at[idx].add(src)

def _segment_sum(src, seg, n):
    return jax.ops.segment_sum(src, seg, n)
kernel_name = 'mk_flamingo_gated_d1_seqx_r4_779fe4'

def setup_inputs(seed: int=0):
    np.random.seed(seed)
    _w = jnp.asarray

    def _rec_inputs():
        import jax
        import jax.numpy as jnp
        _rk = jax.random.key(seed)
        x = -0.0003929 + 0.9999 * jax.random.normal(jax.random.fold_in(_rk, 1), (1, 2048, 256), jnp.float32)
        _lenS = 2048 - jax.random.randint(jax.random.fold_in(_rk, 7), (1,), 0, max(1, 2048 // 4) + 1, jnp.int32)
        _lenS2 = 1601 - jax.random.randint(jax.random.fold_in(_rk, 8), (1,), 0, max(1, 1601 // 4) + 1, jnp.int32)
        _ctx_1024P = jax.random.normal(jax.random.fold_in(_rk, 11), (1, 16, 256), jnp.float32)
        _ctx_1024c = jax.random.dirichlet(jax.random.fold_in(_rk, 511), 0.3 * jnp.ones((16,), jnp.float32), (1, 1601))
        _ctx_1024t = jnp.einsum('bsk,bkd->bsd', _ctx_1024c, _ctx_1024P)
        _ctx_1024t = _ctx_1024t * jax.lax.rsqrt(jnp.mean(jnp.square(_ctx_1024t)) + 1e-12) * 0.953939
        ctx_1024 = 4.13588e-05 + 0.999923 * (_ctx_1024t + 0.3 * jax.random.normal(jax.random.fold_in(_rk, 611), (1, 1601, 256), jnp.float32))
        _g = jax.random.normal(jax.random.fold_in(_rk, 9001), (2, 1), jnp.float32)
        _g = jnp.sign(_g) * jnp.maximum(jnp.abs(_g), 1.0) + (_g == 0) * 1.0
        g_xattn = _g[0]
        g_ffn = _g[1]
        return (x, ctx_1024, g_xattn, g_ffn)
    x, ctx_1024, g_xattn, g_ffn = _rec_inputs()

    def _L0_xattn_setup():
        import jax, jax.numpy as jnp
        import numpy as np
        H = 256
        B = 8
        L_CHAR = 512
        L_SUB = 256

        def _linear(x, W, b):
            return jnp.einsum('blh,oh->blo', x, W) + b

        def _interp_linear(x, out_len):
            L_in = x.shape[1]
            pos = (jnp.arange(out_len, dtype=x.dtype) + 0.5) * (L_in / out_len) - 0.5
            pos = jnp.clip(pos, 0.0, L_in - 1)
            lo = jnp.floor(pos).astype(jnp.int32)
            hi = jnp.minimum(lo + 1, L_in - 1)
            w = (pos - lo.astype(x.dtype))[None, :, None]
            return x[:, lo] * (1 - w) + x[:, hi] * w
        key = jax.random.key(seed)
        ks = jax.random.split(key, 18)
        s = 0.02
        inp = {'char_emb': jax.random.normal(ks[0], (B, L_CHAR, H), jnp.float32), 'subword_emb': jax.random.normal(ks[1], (B, L_SUB, H), jnp.float32)}
        names = ['Wq_c', 'Wk_s', 'Wv_s', 'Wq_s', 'Wk_c', 'Wv_c']
        for i, n in enumerate(names):
            inp[n] = jax.random.normal(ks[2 + 2 * i], (H, H), jnp.float32) * s
            inp['b' + n[1:]] = jax.random.normal(ks[3 + 2 * i], (H,), jnp.float32) * s
        inp['Wg'] = jax.random.normal(ks[14], (H, 2 * H), jnp.float32) * s
        inp['bg'] = jax.random.normal(ks[15], (H,), jnp.float32) * s
        return inp
    _L0_xattn_all = _L0_xattn_setup()
    _L0_xattn_in = {k: v for k, v in _L0_xattn_all.items() if k in ('Wq_c', 'bq_c', 'Wk_s', 'bk_s', 'Wv_s', 'bv_s', 'Wq_s', 'bq_s', 'Wk_c', 'bk_c', 'Wv_c', 'bv_c', 'Wg', 'bg')}
    del _L0_xattn_all

    def _L0_ffn_setup():
        import jax, jax.numpy as jnp
        import numpy as np
        E = 8
        TOP_K = 2
        B, S, D = (2, 1024, 256)
        H = 1024
        CAPACITY = 512

        def _moe(x, Wg, W1, b1, W2, b2):
            b, s, d = x.shape
            xf = x.reshape(b * s, d)
            logits = xf.astype(jnp.float32) @ Wg.astype(jnp.float32)
            probs = jax.nn.softmax(logits, axis=-1)
            vals, idx = jax.lax.top_k(probs, TOP_K)
            w = vals / (jnp.sum(vals, axis=-1, keepdims=True) + 1e-09)
            counts = jnp.zeros((E,), dtype=jnp.int32)
            combine = jnp.zeros((b * s, E), dtype=jnp.float32)
            for k in range(TOP_K):
                oh = jax.nn.one_hot(idx[:, k], E, dtype=jnp.int32)
                pos = jnp.cumsum(oh, axis=0) - 1 + counts[None, :]
                keep = (oh == 1) & (pos < CAPACITY)
                counts = counts + jnp.sum(keep.astype(jnp.int32), axis=0)
                combine = combine + w[:, k][:, None] * keep.astype(jnp.float32)
            out = jnp.zeros_like(xf)
            for e in range(E):
                h = jax.nn.gelu(xf @ W1[e] + b1[e])
                ye = h @ W2[e] + b2[e]
                out = out + combine[:, e][:, None].astype(xf.dtype) * ye
            return out.reshape(b, s, d)
        key = jax.random.key(seed)
        k0, k1, k2, k3 = jax.random.split(key, 4)
        return {'x': jax.random.normal(k0, (B, S, D), dtype=jnp.float32), 'Wg': jax.random.normal(k1, (D, E), dtype=jnp.float32) * 0.02, 'W1': jax.random.normal(k2, (E, D, H), dtype=jnp.float32) * 0.02, 'b1': jnp.zeros((E, H), dtype=jnp.float32), 'W2': jax.random.normal(k3, (E, H, D), dtype=jnp.float32) * 0.02, 'b2': jnp.zeros((E, D), dtype=jnp.float32)}
    _L0_ffn_all = _L0_ffn_setup()
    _L0_ffn_in = {k: v for k, v in _L0_ffn_all.items() if k in ('Wg', 'W1', 'b1', 'W2', 'b2')}
    del _L0_ffn_all
    return {'x': x, 'ctx_1024': ctx_1024, 'g_xattn': g_xattn, 'g_ffn': g_ffn, 'L0_xattn_Wq_c': _L0_xattn_in['Wq_c'], 'L0_xattn_bq_c': _L0_xattn_in['bq_c'], 'L0_xattn_Wk_s': _L0_xattn_in['Wk_s'], 'L0_xattn_bk_s': _L0_xattn_in['bk_s'], 'L0_xattn_Wv_s': _L0_xattn_in['Wv_s'], 'L0_xattn_bv_s': _L0_xattn_in['bv_s'], 'L0_xattn_Wq_s': _L0_xattn_in['Wq_s'], 'L0_xattn_bq_s': _L0_xattn_in['bq_s'], 'L0_xattn_Wk_c': _L0_xattn_in['Wk_c'], 'L0_xattn_bk_c': _L0_xattn_in['bk_c'], 'L0_xattn_Wv_c': _L0_xattn_in['Wv_c'], 'L0_xattn_bv_c': _L0_xattn_in['bv_c'], 'L0_xattn_Wg': _L0_xattn_in['Wg'], 'L0_xattn_bg': _L0_xattn_in['bg'], 'L0_ffn_Wg': _L0_ffn_in['Wg'], 'L0_ffn_W1': _L0_ffn_in['W1'], 'L0_ffn_b1': _L0_ffn_in['b1'], 'L0_ffn_W2': _L0_ffn_in['W2'], 'L0_ffn_b2': _L0_ffn_in['b2']}

def reference(x, ctx_1024, g_xattn, g_ffn, L0_xattn_Wq_c, L0_xattn_bq_c, L0_xattn_Wk_s, L0_xattn_bk_s, L0_xattn_Wv_s, L0_xattn_bv_s, L0_xattn_Wq_s, L0_xattn_bq_s, L0_xattn_Wk_c, L0_xattn_bk_c, L0_xattn_Wv_c, L0_xattn_bv_c, L0_xattn_Wg, L0_xattn_bg, L0_ffn_Wg, L0_ffn_W1, L0_ffn_b1, L0_ffn_W2, L0_ffn_b2):
    import jax
    import jax.numpy as jnp

    def _L0_xattn_ref(char_emb, subword_emb, Wq_c, bq_c, Wk_s, bk_s, Wv_s, bv_s, Wq_s, bq_s, Wk_c, bk_c, Wv_c, bv_c, Wg, bg):
        import jax, jax.numpy as jnp
        import numpy as np
        H = 256
        B = 8
        L_CHAR = 512
        L_SUB = 256

        def _linear(x, W, b):
            return jnp.einsum('blh,oh->blo', x, W) + b

        def _interp_linear(x, out_len):
            L_in = x.shape[1]
            pos = (jnp.arange(out_len, dtype=x.dtype) + 0.5) * (L_in / out_len) - 0.5
            pos = jnp.clip(pos, 0.0, L_in - 1)
            lo = jnp.floor(pos).astype(jnp.int32)
            hi = jnp.minimum(lo + 1, L_in - 1)
            w = (pos - lo.astype(x.dtype))[None, :, None]
            return x[:, lo] * (1 - w) + x[:, hi] * w
        h = char_emb.shape[-1]
        scale = 1.0 / jnp.sqrt(jnp.asarray(h, char_emb.dtype))
        Q_char = _linear(char_emb, Wq_c, bq_c)
        K_sub = _linear(subword_emb, Wk_s, bk_s)
        V_sub = _linear(subword_emb, Wv_s, bv_s)
        scores = jnp.einsum('bqh,bkh->bqk', Q_char, K_sub) * scale
        char2sub = jnp.einsum('bqk,bkh->bqh', jax.nn.softmax(scores, axis=-1), V_sub)
        Q_sub = _linear(subword_emb, Wq_s, bq_s)
        K_char = _linear(char_emb, Wk_c, bk_c)
        V_char = _linear(char_emb, Wv_c, bv_c)
        scores2 = jnp.einsum('bqh,bkh->bqk', Q_sub, K_char) * scale
        sub2char = jnp.einsum('bqk,bkh->bqh', jax.nn.softmax(scores2, axis=-1), V_char)
        L_char = char_emb.shape[1]
        if sub2char.shape[1] != L_char:
            sub2char = _interp_linear(sub2char, L_char)
        gate_in = jnp.concatenate([char2sub, sub2char], axis=-1)
        gate = jax.nn.sigmoid(jnp.einsum('blh,oh->blo', gate_in, Wg) + bg)
        return gate * char2sub + (1 - gate) * sub2char

    def _L0_ffn_ref(x, Wg, W1, b1, W2, b2):
        import jax, jax.numpy as jnp
        import numpy as np
        E = 8
        TOP_K = 2
        B, S, D = (2, 1024, 256)
        H = 1024
        CAPACITY = 512

        def _moe(x, Wg, W1, b1, W2, b2):
            b, s, d = x.shape
            xf = x.reshape(b * s, d)
            logits = xf.astype(jnp.float32) @ Wg.astype(jnp.float32)
            probs = jax.nn.softmax(logits, axis=-1)
            vals, idx = jax.lax.top_k(probs, TOP_K)
            w = vals / (jnp.sum(vals, axis=-1, keepdims=True) + 1e-09)
            counts = jnp.zeros((E,), dtype=jnp.int32)
            combine = jnp.zeros((b * s, E), dtype=jnp.float32)
            for k in range(TOP_K):
                oh = jax.nn.one_hot(idx[:, k], E, dtype=jnp.int32)
                pos = jnp.cumsum(oh, axis=0) - 1 + counts[None, :]
                keep = (oh == 1) & (pos < CAPACITY)
                counts = counts + jnp.sum(keep.astype(jnp.int32), axis=0)
                combine = combine + w[:, k][:, None] * keep.astype(jnp.float32)
            out = jnp.zeros_like(xf)
            for e in range(E):
                h = jax.nn.gelu(xf @ W1[e] + b1[e])
                ye = h @ W2[e] + b2[e]
                out = out + combine[:, e][:, None].astype(xf.dtype) * ye
            return out.reshape(b, s, d)
        return _moe(x, Wg, W1, b1, W2, b2)
    x = x + jnp.tanh(g_xattn[0]) * _L0_xattn_ref(_layernorm(x, axis=-1), ctx_1024, L0_xattn_Wq_c, L0_xattn_bq_c, L0_xattn_Wk_s, L0_xattn_bk_s, L0_xattn_Wv_s, L0_xattn_bv_s, L0_xattn_Wq_s, L0_xattn_bq_s, L0_xattn_Wk_c, L0_xattn_bk_c, L0_xattn_Wv_c, L0_xattn_bv_c, L0_xattn_Wg, L0_xattn_bg)
    x = x + jnp.tanh(g_ffn[0]) * _L0_ffn_ref(_layernorm(x, axis=-1), L0_ffn_Wg, L0_ffn_W1, L0_ffn_b1, L0_ffn_W2, L0_ffn_b2)
    return x

_drawn_inputs = setup_inputs


def setup_inputs(seed=0):
    import zlib

    import numpy as np

    out = dict(_drawn_inputs(seed))
    spreads = {'L0_ffn_b1': (0.0, 0.328), 'L0_ffn_b2': (0.0, 0.1)}
    factors = {'L0_xattn_Wq_c': 8.0,
     'L0_xattn_bq_c': 21.384,
     'L0_xattn_Wk_s': 8.0,
     'L0_xattn_bk_s': 200.0,
     'L0_xattn_bv_s': 5.732,
     'L0_xattn_Wq_s': 8.0,
     'L0_xattn_bq_s': 8.0,
     'L0_xattn_Wk_c': 8.0,
     'L0_xattn_bk_c': 200.0,
     'L0_xattn_Wv_c': 8.0,
     'L0_xattn_bv_c': 4.448,
     'L0_xattn_Wg': 8.0,
     'L0_xattn_bg': 21.359}
    for name, (base, spread) in spreads.items():
        noise = np.random.default_rng([zlib.crc32(name.encode()), seed]).standard_normal(out[name].shape)
        drawn = base * np.exp(spread * noise) if base else spread * noise
        out[name] = jnp.asarray(drawn.astype(out[name].dtype))
    for name, factor in factors.items():
        out[name] = (out[name] * factor).astype(out[name].dtype)
    return out
```

```python
import concourse.bass as bass
from concourse import mybir
from contextlib import ExitStack, contextmanager

P = 128
D = 256
DC = D // P
E = 8
HID = 1024
HC = HID // P
CAP = 512
CT = CAP // P
L = 2048
LT = L // P
C = 1601
CTX = -(-C // P)
CREM = C - (CTX - 1) * P
CKEYS = C + 1
BANK = 512
ROW = D + 3
SKIP = 1 << 20
SCALE = 1.0 / 16
STEP = L // P
LN_EPS = 1e-5


class Tile:

    def __init__(self, i, half, p):
        self.i, self.half, self.p = i, half, p

    def ahead(self, d):
        p = (self.p + d) % 2
        return Tile(self.i + d, self.half + (self.p + d - p) // 2, p)

    def back(self, d):
        p = (self.p - d) % 2
        return Tile(self.i - d, self.half - (d + p - self.p) // 2, p)


def tiles(eng, first, last, body):
    i = first
    if i % 2:
        body(Tile(i, i // 2, 1))
        i += 1
    pairs = (last - i) // 2
    if pairs >= 2:
        with eng.Fori(i // 2, i // 2 + pairs) as half:
            body(Tile(half * 2, half, 0))
            body(Tile(half * 2 + 1, half, 1))
        i += 2 * pairs
    while i < last:
        body(Tile(i, i // 2, i % 2))
        i += 1


def wait(eng, sem, count):
    if isinstance(count, int) and count <= 0:
        return
    eng.wait_ge(sem, count)


def program(nc, x, ctx_in, g_xattn, g_ffn, Wq_c, bq_c, Wk_s, bk_s, Wv_s, bv_s, Wq_s, bq_s, Wk_c, bk_c,
            Wv_c, bv_c, Wgate, bgate, Wroute, W1, b1, W2, b2, out):
    f32, f32r = mybir.dt.float32, mybir.dt.float32r
    i32, u32 = mybir.dt.int32, mybir.dt.uint32
    ALU, ACT, AX = mybir.AluOpType, mybir.ActivationFunctionType, mybir.AxisListType
    stack = ExitStack()
    with stack:
        top = [(nc.sbuf_base + 63) // 64 * 64]

        def size(shape):
            n = 4
            for v in shape[1:]:
                n *= v
            return (n + 31) // 32 * 32

        def at(name, offset, shape, dt=f32):
            return nc.alloc_sbuf_tensor_at(name, shape, dt, offset=offset)

        def region(n):
            top[0] += n
            assert top[0] <= nc.sbuf_usable_end, top[0]
            return top[0] - n

        def sb(name, shape, dt=f32):
            return at(name, region(size(shape)), shape, dt)

        def inside(start, end):
            used = [start]

            def place(name, shape, dt=f32):
                used[0] += size(shape)
                assert used[0] <= end, (name, used[0] - end)
                return at(name, used[0] - size(shape), shape, dt)
            return place

        def sem(name):
            return stack.enter_context(nc.semaphore(name))

        r_kchar = region(2 * DC * L * 4)
        kchar = [at(f"kchar_{s}", r_kchar + n * DC * L * 4, [P, DC, L], f32r) for n, s in enumerate(("high", "low"))]
        r_vchar = region(LT * 2 * D * 4)
        vchar = at("vchar", r_vchar, [P, LT, 2 * D], f32r)
        r_ksub = region(2 * DC * CTX * P * 4)
        ksub = [at(f"ksub_{s}", r_ksub + n * DC * CTX * P * 4, [P, DC, CTX * P], f32r) for n, s in enumerate(("high", "low"))]
        r_vsub = region(CTX * 2 * D * 4)
        vsub = at("vsub", r_vsub, [P, CTX, 2 * D], f32r)
        r_qchar = region(LT * D * 4)
        qchar = at("qchar", r_qchar, [P, LT, DC, P], f32)
        r_qsub = region(CTX * D * 4)
        qsub = at("qsub", r_qsub, [P, CTX, DC, P], f32)

        r_work = region(2 * L * 4 + 2 * LT * P * 4)
        probs = [at(f"probs{p}", r_work + p * L * 4, [P, L], f32) for p in range(2)]
        r_pt = r_work + 2 * L * 4
        pt = [at(f"probsT_{s}", r_pt + n * LT * P * 4, [P, LT, P], f32r) for n, s in enumerate(("high", "low"))]
        wT = [at(f"wT_{n}", r_work + n * DC * 2 * D * 4, [P, DC, 2, D], f32r) for n in range(6)]
        o = r_work + 6 * DC * 2 * D * 4
        tin = [at(f"tin{p}", o + p * D * 4, [P, D], f32) for p in range(2)]
        tT = [[at(f"tT_{s}{p}", o + (2 + 2 * p + n) * D * 4, [P, DC, P], f32r) for n, s in enumerate(("high", "low"))] for p in range(2)]
        assert o + 6 * D * 4 <= r_work + 2 * L * 4 + 2 * LT * P * 4
        x_all = at("x_all", r_vsub, [P, LT, D], f32)
        w_raw = at("w_raw", r_ksub, [P, 6, DC, D], f32)
        wg_raw = at("wg_raw", r_ksub + 6 * DC * D * 4, [P, DC, 2 * D], f32)

        wgT = sb("wgT", [P, 2 * DC, 2, D], f32r)
        ident = sb("ident", [P, P])
        before = sb("before", [P, P])
        ones = sb("ones", [P, P])
        tent = sb("tent", [P, P])
        tdist = sb("tdist", [P, P])
        tabs = sb("tabs", [P, P])
        tidx = at("tidx", r_vchar, [P, P], i32)
        VECS = E * HC + 4 * DC
        vec_rows = at("vec_rows", r_qsub + 1024, [VECS, P])
        vec_cols = sb("vec_cols", [P, VECS])
        b1c = vec_cols[:, 0:E * HC].rearrange("p (e c) -> p e c", c=HC)
        bias_cols = vec_cols[:, E * HC:VECS].rearrange("p (n c) -> p n c", c=DC)
        bias_rows = sb("bias_rows", [P, 3, D])
        gains = sb("gains", [P, 2])
        tgains = sb("tgains", [P, 2])
        mhalf = sb("mhalf", [P, LT])
        iota_e = sb("iota_e", [P, E])
        base_e = sb("base_e", [P, 2, E])
        full_e = sb("full_e", [P, 2, E])
        ie = sb("ie", [P, 2 * E], i32)
        wroute = sb("wroute", [P, DC, E])
        token = sb("token", [P, 1])
        prow = sb("prow", [P, 1])
        tok_i = sb("tok_i", [P, 1], i32)
        zrow = at("zrow", r_ksub + 16 * D * 4, [P, CT, ROW], f32)
        ztok = sb("ztok", [P, CT], i32)
        stats = at("stats", r_qsub, [P, LT, 6], f32)
        mv = at("mv", r_qsub + LT * 24, [P, LT, 2], f32)
        rstd = at("rstd", r_qsub + LT * 32, [P, LT], f32)
        vpe = at("vpe", r_qsub + LT * 36, [P, LT], f32)

        qs = [[sb(f"q_{s}{p}", [P, DC, P], f32r) for s in ("high", "low")] for p in range(2)]
        mx = sb("mx", [P, 2, 4])
        nmx = sb("nmx", [P, 2])
        nbias = sb("nbias", [P, 2])
        esum = sb("esum", [P, 2, 4])
        zsum = sb("zsum", [P, 2])
        rz = sb("rz", [P, 2])
        osb = sb("osb", [P, D])
        onorm = sb("onorm", [P, D])
        att = [sb(f"att{p}", [P, D]) for p in range(2)]

        in_qsub = inside(r_qsub, r_work)
        xres = [sb(f"xres{p}", [P, D]) for p in range(2)]
        subwin = sb("subwin", [P, D])
        sub = in_qsub("sub", [P, D])
        ginT = [in_qsub(f"ginT_{s}", [P, 2 * DC, P], f32r) for s in ("high", "low")]
        ga = in_qsub("ga", [P, D])
        gb = in_qsub("gb", [P, D])
        gd = in_qsub("gd", [P, D])
        gdt = in_qsub("gdt", [P, D])
        subt = in_qsub("subt", [P, D])
        base = in_qsub("base", [P, D])
        x1 = [in_qsub(f"x1_{p}", [P, D]) for p in range(2)]
        row = [sb(f"row{p}", [P, ROW]) for p in range(2)]
        st1 = sb("st1", [P, 6])
        mv1 = sb("mv1", [P, 2])
        rs1 = sb("rs1", [P, 2])
        xn2T = sb("xn2T", [P, DC, P])
        lg = sb("lg", [P, E])
        lmax = sb("lmax", [P, 2])
        pe_ = sb("pe_", [P, E])
        psm = sb("psm", [P, 2])
        prob = sb("prob", [P, E])
        best = sb("best", [P, 8])
        besti = sb("besti", [P, 8], u32)
        bestf = sb("bestf", [P, 8])
        wsum = sb("wsum", [P, 2])
        oneh = sb("oneh", [P, 2, E])
        counts = sb("counts", [P, 2, E])
        rank = sb("rank", [P, 2, E])
        over = sb("over", [P, 2, E])
        slotf = sb("slotf", [P, 2])
        sloti = [sb(f"sloti{p}", [P, 2], u32) for p in range(2)]

        place = inside(r_kchar, r_ksub)
        w1_raw = place("w1_raw", [P, DC, HID])
        w2_raw = place("w2_raw", [P, HC, D])
        w1s = [place(f"w1_{h}", [P, DC, HID], f32r) for h in ("high", "low")]
        w2s = place("w2s", [P, HC, 2, D], f32r)
        b2r = place("b2r", [P, 2, D])
        place = inside(r_ksub, r_qchar)
        xg = [place(f"xg{p}", [P, CT, ROW]) for p in range(2)]
        xgT = [place(f"xgT_{h}", [P, DC, CAP], f32r) for h in ("high", "low")]
        hid = [place(f"hid{p}", [P, CAP]) for p in range(2)]
        hs = [[place(f"hid_{h}{p}", [P, CAP], f32r) for h in ("high", "low")] for p in range(2)]
        wt = place("wt", [P, 2, CT])
        wd = place("wd", [P, CT])
        tok = [place(f"tok{p}", [P, CT], u32) for p in range(2)]
        gcur = [place(f"gcur{p}", [P, CT], u32) for p in range(2)]
        yb = place("yb", [P, 2, D])
        yu = place("yu", [P, 2, D])
        yo = place("yo", [P, CT, D])
        cfill = place("cfill", [P, E])
        slot = place("slot", [P, E, CT])
        first_free = place("first_free", [P, E, CT])
        smask = place("smask", [P, E, CT])
        shift = place("shift", [P, E, CT])

        sub_rows = nc.dram_tensor("sub_rows", [CTX * P + 1, D], f32, kind="Internal").ap()
        routed = nc.dram_tensor("routed", [2 * E * CAP, ROW], f32, kind="Internal").ap()
        acc = nc.dram_tensor("acc", [L + CAP, D], f32, kind="Internal").ap()

        bank = [stack.enter_context(nc.psum_tensor(f"bank{b}", [P, BANK], f32)) for b in range(8)]
        scores, ptb, obank, misc = bank[0:4], bank[4:6], bank[6], bank[7]

        names = {}

        def s(name):
            if name not in names:
                names[name] = sem(name)
            return names[name]

        def then_wait(eng, ins, name, count):
            ins.then_inc(s(name), 1)
            eng.wait_ge(s(name), count)

        RANK_STEPS, CHOICE_STEPS, NORM_STEPS = 5, 6, 3

        xv = x[0].rearrange("(t p) d -> p t d", p=P)
        ov = out[0]
        block = stack.enter_context(nc.Block())

        W6 = (Wq_c, Wk_c, Wv_c, Wq_s, Wk_s, Wv_s)
        UNITS = 8
        CONSTS = 11

        def unit_in(u):
            return bank[u][:].rearrange("p (c o) -> p c o", c=DC)

        def unit_out(u, part):
            return wT[u][:, :, part] if u < 6 else wgT[:, (u - 6) * DC:(u - 5) * DC, part]

        GROUPS_A = [range(4 * g, 4 * g + 4) for g in range(4)]
        GROUPS_B = [range(4 * g, min(4 * g + 4, CTX)) for g in range(4)]
        CHUNKS_A = [(BANK * c, BANK) for c in range(4)]
        CHUNKS_B = [(BANK * c, min(BANK, CKEYS - BANK * c)) for c in range(4)]

        def row_bcast(v):
            return v.rearrange("(a n) -> a n", a=1).broadcast_to([P, v.shape[0]])

        @block.sync
        def _(sp):
            for n, w in enumerate(W6):
                sp.dma_start(w_raw[:, n], w.rearrange("(c p) i -> p c i", p=P)).then_inc(s("weights_in"), 16)
            sp.dma_start(wg_raw[:], Wgate.rearrange("(c p) i -> p c i", p=P)).then_inc(s("weights_in"), 16)

            def load_context(t, rows=P):
                if isinstance(t.i, int) and t.i < 2:
                    sp.wait_ge(s("x_T"), LT)
                else:
                    sp.wait_ge(s("c_T"), t.i - 1)
                sp.dma_start(tin[t.p][0:rows], ctx_in[0, bass.ds(t.i * P, rows)]).then_inc(s(f"tin_in{t.p}"), 16)
            tiles(sp, 0, 2, load_context)
            tiles(sp, 2, CTX - 1, load_context)
            load_context(Tile(CTX - 1, (CTX - 1) // 2, (CTX - 1) % 2), CREM)

            def store_sub(t):
                sp.wait_ge(s("a_att"), t.i + 1)
                sp.dma_start(sub_rows[bass.ds(t.i * P + 1, P)], att[t.p][:]).then_inc(s(f"sub_out{t.p}"), 16)
            store_sub(Tile(0, 0, 0))
            sp.dma_start(sub_rows[0:1], att[0][0:1]).then_inc(s("sub_first"), 16)
            tiles(sp, 1, CTX - 1, store_sub)
            last = (CTX - 1) % 2
            sp.wait_ge(s("a_att"), CTX)
            sp.dma_start(sub_rows[(CTX - 1) * P + 1:C + 1], att[last][0:CREM]).then_inc(s("sub_edge"), 16)
            sp.dma_start(sub_rows[C + 1:C + 2], att[last][CREM - 1:CREM]).then_inc(s("sub_edge"), 16)
            sp.dma_start(sub_rows[C + 2:CTX * P + 1], att[last][CREM + 1:P]).then_inc(s("sub_edge"), 16)

            sp.wait_ge(s("a_pv"), CTX)
            sp.dma_start(w1_raw[:], W1[0].rearrange("(c p) h -> p c h", p=P)).then_inc(s("w1_in"), 16)
            sp.dma_start(w2_raw[:], W2[0].rearrange("(c p) d -> p c d", p=P)).then_inc(s("w2_in"), 16)
            sp.dma_start(b2r[:, 0], b2[0:1].broadcast_to([P, D])).then_inc(s("b2_in0"), 16)
            sp.wait_ge(s("sub_first"), 16)
            sp.wait_ge(s("sub_edge"), 48)
            sp.wait_ge(s("sub_out0"), 16 * ((CTX - 1) // 2))
            sp.wait_ge(s("sub_out1"), 16 * ((CTX - 1) // 2))

            def load_tile(t):
                wait(sp, s("base"), t.i - 1)
                sp.dma_start(xres[t.p][:], x[0, bass.ds(t.i * P, P)]).then_inc(s(f"xres_in{t.p}"), 16)
                wait(sp, s("interp"), t.i)
                sp.dma_start(subwin[:], sub_rows[bass.ds(t.i * (C // STEP), P)]).then_inc(s("subwin_in"), 16)
            tiles(sp, 0, 2, load_tile)
            tiles(sp, 2, LT, load_tile)

            def load_expert(t):
                sp.wait_ge(s("w_split"), t.i * HC)
                sp.dma_start(w1_raw[:], W1[bass.ds(t.i, 1)].rearrange("a (c p) h -> p (a c) h", p=P)).then_inc(s("w1_in"), 16)
                sp.dma_start(w2_raw[:], W2[bass.ds(t.i, 1)].rearrange("a (c p) d -> p (a c) d", p=P)).then_inc(s("w2_in"), 16)
                wait(sp, s("yo"), CT * (t.i - 1))
                sp.dma_start(b2r[:, t.p], b2[bass.ds(t.i, 1)].broadcast_to([P, D])).then_inc(s(f"b2_in{t.p}"), 16)
            tiles(sp, 1, 2, load_expert)
            tiles(sp, 2, E, load_expert)

            for p in range(2):
                sp.wait_ge(s(f"y_out{p}"), 16 * CT * E // 2)
            sp.dma_start(ov, acc[0:L]).then_inc(s("out_done"), 16)
            sp.wait_ge(s("out_done"), 16)

        @block.gpsimd
        def _(gp):
            def apart(name, count):
                gp.wait_ge(s(name), count)
                gp.sem_inc(s("g_passed"), 1)

            gp.memset(ident[:], 0.0)
            gp.memset(zrow[:], 0.0)
            gp.memset(ones[:], 1.0).then_inc(s("g_fill"), 1)
            gp.wait_ge(s("g_fill"), 1)
            gp.affine_select(out=ident[:], in_=ident[:], compare_op=ALU.not_equal, fill=1.0, base=0,
                             pattern=[[-1, P]], channel_multiplier=1)
            gp.affine_select(out=before[:], in_=ones[:], compare_op=ALU.is_gt, fill=0.0, base=0,
                             pattern=[[1, P]], channel_multiplier=-1).then_inc(s("ident"), 1)
            gp.memset(mhalf[:], -0.5)
            gp.iota(ztok[:], pattern=[[1, CT]], base=L, channel_multiplier=CT)
            gp.iota(tidx[:], pattern=[[2 * C, P]], base=C + L, channel_multiplier=-2 * L)
            gp.iota(ie[:, 0:E], pattern=[[1, E]], base=0, channel_multiplier=0)
            gp.iota(ie[:, E:2 * E], pattern=[[CAP, E]], base=0, channel_multiplier=0)
            gp.iota(tok_i[:], pattern=[[0, 1]], base=0, channel_multiplier=1).then_inc(s("g_iota"), 1)
            gp.wait_ge(s("g_iota"), 1)
            gp.tensor_copy(zrow[:, :, ROW - 1], ztok[:]).then_inc(s("zrow"), 1)
            for v in (0, 1):
                gp.tensor_scalar(base_e[:, v], ie[:, E:2 * E], float(v * E * CAP), None, ALU.add)
                gp.tensor_scalar(full_e[:, v], ie[:, E:2 * E], float(v * E * CAP + CAP), None, ALU.add)
                gp.tensor_scalar(counts[:, v], ie[:, E:2 * E], float(v * E * CAP), None, ALU.add)
            gp.tensor_copy(iota_e[:], ie[:, 0:E])
            gp.tensor_copy(token[:], tok_i[:])
            gp.tensor_copy(prow[:], tok_i[:])
            gp.tensor_scalar(tdist[:], tidx[:], 1.0 / (2 * L), None, ALU.mult).then_inc(s("g_consts"), 1)
            gp.wait_ge(s("vpe"), 1)
            gp.tensor_tensor(rstd[:], vpe[:], mhalf[:], ALU.pow).then_inc(s("rstd"), 1)

            def split_queries(src, t, ph):
                q = src[:, bass.ds(t.i, 1)].rearrange("p a c l -> p (a c) l")
                if not (isinstance(t.i, int) and t.i < 2):
                    apart(f"{ph}_scores", 4 * (t.i - 1))
                gp.tensor_copy(qs[t.p][0][:], q).then_inc(s(f"{ph}_qh"), 1)
                apart(f"{ph}_qh", t.i + 1)
                gp.tensor_tensor(qs[t.p][1][:], q, qs[t.p][0][:].bitcast(f32), ALU.subtract).then_inc(s(f"{ph}_q"), 1)

            def add_value_bias(t, ph, n):
                gp.wait_ge(s(f"{ph}_norm"), t.i + 1)
                if ph == "a" and not (isinstance(t.i, int) and t.i < 2):
                    gp.wait_ge(s(f"sub_out{t.p}"), 16 * t.half)
                if ph == "b" and not (isinstance(t.i, int) and t.i < 2):
                    gp.wait_ge(s("gate_T"), t.i - 1)
                gp.tensor_tensor(att[t.p][:], onorm[:], bias_rows[:, n], ALU.add).then_inc(s(f"{ph}_att"), 1)

            gp.wait_ge(s("consts_in"), CONSTS * 16)
            def a_step(t, cur=True, old=True):
                if cur:
                    split_queries(qsub, t.ahead(1), "a")
                if old:
                    add_value_bias(t.back(2), "a", 1)
            for name in ("c_high_kqv", "c_low_v"):
                gp.wait_ge(s(name), CTX)
            split_queries(qsub, Tile(0, 0, 0), "a")
            tiles(gp, 0, 2, lambda t: a_step(t, old=False))
            tiles(gp, 2, 4, a_step)
            gp.wait_ge(s("sub_first"), 16)
            tiles(gp, 4, CTX - 1, a_step)
            tiles(gp, CTX - 1, CTX + 2, lambda t: a_step(t, cur=False))

            def gate_parts(j):
                gp.wait_ge(s("sub"), j.i + 1)
                gp.wait_ge(s("b_att"), j.i + 1)
                if not (isinstance(j.i, int) and j.i < 1):
                    gp.wait_ge(s("x1"), j.i)
                gp.tensor_tensor(gd[:], att[j.p][:], sub[:], ALU.subtract).then_inc(s("gd"), 1)
                apart("gd", j.i + 1)
                gp.tensor_scalar(gdt[:], gd[:], tgains[:, 0:1], None, ALU.mult)
                gp.tensor_scalar(subt[:], sub[:], tgains[:, 0:1], None, ALU.mult).then_inc(s("gdt"), 1)
                gp.wait_ge(s(f"xres_in{j.p}"), 16 * (j.half + 1))
                gp.wait_ge(s("gdt"), j.i + 1)
                gp.tensor_tensor(base[:], subt[:], xres[j.p][:], ALU.add).then_inc(s("base"), 1)
                gp.wait_ge(s("vpe1"), j.i + 1)
                gp.tensor_tensor(rs1[:, 1:2], rs1[:, 0:1], mhalf[:, 0:1], ALU.pow).then_inc(s("rs1"), 1)

            def route(j):
                apart("slots", j.i + 1)
                for v in range(2):
                    gp.indirect_dma_start(out=routed, out_offset=bass.IndirectOffsetOnAxis(ap=sloti[j.p][:, v:v + 1], axis=0),
                                          in_=row[j.p][:], in_offset=None,
                                          bounds_check=2 * E * CAP - 1, oob_is_err=False).then_inc(s(f"routed_out{j.p}"), 16)

            def b_step(t, cur=True, old=True, older=True):
                if cur:
                    split_queries(qchar, t.ahead(1), "b")
                if old:
                    add_value_bias(t.back(2), "b", 0)
                if older:
                    route(t.back(3))
                if old:
                    gate_parts(t.back(2))

            def split_weights(e, hc):
                cols = slice(hc * P, hc * P + P)
                if not (isinstance(e, int) and e == 0):
                    gp.wait_ge(s("h_mm"), HC * (e - 1) + hc + 1)
                    gp.wait_ge(s("y_mm"), HC * (e - 1) + hc + 1)
                    gp.sem_inc(s("g_passed"), 1)
                gp.tensor_copy(w1s[0][:, :, cols], w1_raw[:, :, cols])
                gp.tensor_copy(w2s[:, hc, 0], w2_raw[:, hc]).then_inc(s("w_high"), 1)
                gp.wait_ge(s("w_high"), e * HC + hc + 1)
                gp.tensor_tensor(w1s[1][:, :, cols], w1_raw[:, :, cols], w1s[0][:, :, cols].bitcast(f32), ALU.subtract)
                gp.tensor_tensor(w2s[:, hc, 1], w2_raw[:, hc], w2s[:, hc, 0].bitcast(f32), ALU.subtract).then_inc(s("w_split"), 1)

            gp.wait_ge(s("empty_in"), 16 * (2 * E + CT))
            gp.wait_ge(s("a_scores"), 4 * CTX)
            gp.wait_ge(s("sub_edge"), 48)
            gp.wait_ge(s("sub_out1"), 16 * ((CTX - 1) // 2))
            split_queries(qchar, Tile(0, 0, 0), "b")
            tiles(gp, 0, 2, lambda t: b_step(t, old=False, older=False))
            tiles(gp, 2, 3, lambda t: b_step(t, older=False))
            gp.wait_ge(s("w1_in"), 16)
            gp.wait_ge(s("w2_in"), 16)
            for hc in range(HC):
                split_weights(0, hc)
            tiles(gp, 3, LT - 1, b_step)
            tiles(gp, LT - 1, LT + 2, lambda t: b_step(t, cur=False))
            route(Tile(LT - 1, (LT - 1) // 2, (LT - 1) % 2))

            def gather(t):
                apart("gcur", t.i + 1)
                for c in range(CT):
                    gp.indirect_dma_start(out=xg[t.p][:, c], out_offset=None, in_=routed,
                                          in_offset=bass.IndirectOffsetOnAxis(ap=gcur[t.p][:, c:c + 1], axis=0),
                                          bounds_check=2 * E * CAP - 1, oob_is_err=False).then_inc(s(f"xg_in{t.p}"), 16)

            def add_rows(t):
                for c in range(CT):
                    apart("yo", CT * t.i + c + 1)
                    if c == 0 and not (isinstance(t.i, int) and t.i == 0):
                        b = t.back(1)
                        apart(f"y_out{b.p}", 16 * CT * (b.half + 1))
                    gp.indirect_dma_start(out=acc, out_offset=bass.IndirectOffsetOnAxis(ap=tok[t.p][:, c:c + 1], axis=0),
                                          in_=yo[:, c], in_offset=None, bounds_check=L + CAP - 1, oob_is_err=True,
                                          compute_op=ALU.add).then_inc(s(f"y_out{t.p}"), 16)

            def expert(t, first=False, last=False):
                if not first:
                    add_rows(t.back(1))
                if not last:
                    n = t.ahead(1)
                    gather(n)
                    apart("w1_in", 16 * (n.i + 1))
                    apart("w2_in", 16 * (n.i + 1))
                    for hc in range(HC):
                        split_weights(n.i, hc)

            for p in range(2):
                gp.wait_ge(s(f"routed_out{p}"), 16 * LT)
            gather(Tile(0, 0, 0))
            for p in range(2):
                gp.wait_ge(s(f"x1_out{p}"), 16 * LT // 2)
            expert(Tile(0, 0, 0), first=True)
            tiles(gp, 1, 2, expert)
            tiles(gp, 2, E - 2, expert)
            expert(Tile(E - 2, E // 2 - 1, 0))
            expert(Tile(E - 1, E // 2 - 1, 1), last=True)
            add_rows(Tile(E - 1, E // 2 - 1, 1))

        @block.scalar
        def _(act):
            act.dma_start(x_all[:], xv).then_inc(s("x_in"), 16)
            for n, b in enumerate((bq_c, bk_c, bq_s, bk_s)):
                act.dma_start(vec_rows[E * HC + n * DC:E * HC + (n + 1) * DC], b.rearrange("(c p) -> c p", p=P)).then_inc(s("consts_in"), 16)
            act.dma_start(vec_rows[0:E * HC], b1.rearrange("e (c p) -> (e c) p", p=P)).then_inc(s("consts_in"), 16)
            for n, b in enumerate((bv_s, bv_c, bgate)):
                act.dma_start(bias_rows[:, n], row_bcast(b)).then_inc(s("consts_in"), 16)
            for n, g in enumerate((g_xattn, g_ffn)):
                act.dma_start(gains[:, n:n + 1], row_bcast(g)).then_inc(s("consts_in"), 16)
            act.dma_start(wroute[:], Wroute.rearrange("(c p) e -> p c e", p=P)).then_inc(s("consts_in"), 16)
            act.wait_ge(s("zrow"), 1)
            for e in range(2 * E):
                act.dma_start(routed[e * CAP:(e + 1) * CAP].rearrange("(p r) n -> p r n", p=P), zrow[:]).then_inc(s("empty_in"), 16)
            for c in range(CT):
                act.dma_start(acc[L + c * P:L + (c + 1) * P], zrow[:, c, 0:D]).then_inc(s("empty_in"), 16)
            act.wait_ge(s("consts_in"), CONSTS * 16)
            act.wait_ge(s("g_consts"), 1)
            act.activation(tgains[:], gains[:], ACT.Tanh).then_inc(s("tgains"), 1)

            for u in range(UNITS):
                act.wait_ge(s("wt_T"), u + 1)
                act.activation(unit_out(u, 0), unit_in(u), ACT.Copy).then_inc(s("wt_high"), 1)

            act.wait_ge(s("vec_T"), 1)
            act.activation(vec_cols[:], bank[6][:, 0:VECS], ACT.Copy).then_inc(s("vec_cols"), 1)
            act.wait_ge(s("vec_cols"), 1)

            def proj_step(t, ph, cur=True, old=True):
                if cur:
                    act.wait_ge(s(f"{ph}_T"), t.i + 1)
                    act.activation(tT[t.p][0][:], bank[t.p][:, 0:D].rearrange("p (c l) -> p c l", c=DC), ACT.Copy).then_inc(s(f"{ph}_tT_high"), 1)
                if old:
                    j = t.back(1)
                    kd, vd, qd, bn = (kchar, vchar, qchar, 0) if ph == "x" else (ksub, vsub, qsub, 2)
                    kq, v = bank[2 + j.p], bank[4 + j.p]
                    act.wait_ge(s(f"{ph}_mm"), j.i + 1)
                    if ph == "c" and isinstance(j.i, int) and j.i == 0:
                        act.wait_ge(s("empty_in"), 16 * (2 * E + CT))
                    for oc in range(DC):
                        act.activation(kd[0][:, oc, bass.ds(j.i * P, P)], kq[:, oc * P:(oc + 1) * P], ACT.Identity,
                                       bias=bias_cols[:, bn + 1, oc:oc + 1])
                    for oc in range(DC):
                        act.activation(qd[:, bass.ds(j.i, 1), oc].rearrange("p a l -> p (a l)"), kq[:, D + oc * P:D + (oc + 1) * P], ACT.Identity,
                                       bias=bias_cols[:, bn, oc:oc + 1])
                    act.activation(vd[:, bass.ds(j.i, 1), 0:D].rearrange("p a d -> p (a d)"), v[:, 0:D], ACT.Copy).then_inc(s(f"{ph}_high_kqv"), 1)

            def proj(ph, n):
                proj_step(Tile(0, 0, 0), ph, old=False)
                tiles(act, 1, n, lambda t: proj_step(t, ph))
                proj_step(Tile(n, n // 2, n % 2), ph, cur=False)
            proj("x", LT)
            proj("c", CTX)

            def high(t, g, ph, groups):
                n = len(groups[g])
                act.wait_ge(s(f"{ph}_T{g % 2}"), 2 * t.i + g // 2 + 1)
                act.activation(pt[0][:, groups[g][0]:groups[g][0] + n], ptb[g % 2][:, 0:n * P].rearrange("p (k l) -> p k l", k=n),
                               ACT.Copy).then_inc(s(f"{ph}_high{g % 2}"), 1)

            def exps(t, c, ph, chunks, keys):
                act.wait_ge(s(f"{ph}_bias"), t.i + 1)
                o, w = chunks[c][0], min(chunks[c][1], keys - chunks[c][0])
                act.activation(probs[t.p][:, o:o + w], scores[c][:, 0:w], ACT.Exp, bias=nbias[:, t.p:t.p + 1], scale=SCALE,
                               accum_out=esum[:, t.p, c:c + 1]).then_inc(s(f"{ph}_exp"), 1)

            def a_step(t, cur=True, prev=True):
                b = t.back(1)
                for g in range(2):
                    if prev:
                        high(b, g, "a", GROUPS_A)
                for g in range(2):
                    if cur:
                        exps(t, 2 * g, "a", CHUNKS_A, L)
                        exps(t, 2 * g + 1, "a", CHUNKS_A, L)
                    if prev:
                        high(b, 2 + g, "a", GROUPS_A)
            a_step(Tile(0, 0, 0), prev=False)
            tiles(act, 1, CTX, a_step)
            a_step(Tile(CTX, CTX // 2, CTX % 2), cur=False)

            def tent_weights(j):
                if isinstance(j.i, int) and j.i == 0:
                    act.wait_ge(s("g_consts"), 1)
                else:
                    act.wait_ge(s("interp"), j.i)
                    act.wait_ge(s("tdist"), j.i)
                act.activation(tabs[:], tdist[:], ACT.Abs).then_inc(s("tabs"), 1)
                act.wait_ge(s("tabs"), j.i + 1)
                act.activation(tent[:], tabs[:], ACT.Relu, scale=-1.0, bias=ones[:, 0:1]).then_inc(s("tent"), 1)

            def b_step(t, cur=True, prev=True, old=True):
                b, j = t.back(1), t.back(2)
                if old:
                    act.wait_ge(s("interp"), j.i + 1)
                    if not (isinstance(j.i, int) and j.i < 1):
                        act.wait_ge(s("base"), j.i)
                    act.activation(sub[:], misc[:, 0:D], ACT.Copy).then_inc(s("sub"), 1)
                    act.wait_ge(s("gate_T"), j.i + 1)
                    act.activation(ginT[0][:], misc[:].rearrange("p (c l) -> p c l", c=2 * DC), ACT.Copy).then_inc(s("gin_high"), 1)
                if prev:
                    high(b, 0, "b", GROUPS_B)
                    high(b, 1, "b", GROUPS_B)
                if cur:
                    exps(t, 0, "b", CHUNKS_B, C)
                    exps(t, 1, "b", CHUNKS_B, C)
                if old:
                    act.wait_ge(s("z"), j.i + 1)
                    act.activation(gb[:], ga[:], ACT.Exp, scale=-1.0).then_inc(s("gexp"), 1)
                if prev:
                    high(b, 2, "b", GROUPS_B)
                if cur:
                    exps(t, 2, "b", CHUNKS_B, C)
                    exps(t, 3, "b", CHUNKS_B, C)
                if prev:
                    high(b, 3, "b", GROUPS_B)
                if old:
                    act.wait_ge(s("xn2_T"), j.i + 1)
                    act.activation(xn2T[:], misc[:, 0:D].rearrange("p (c l) -> p c l", c=DC), ACT.Copy).then_inc(s("xn2T"), 1)
                    act.wait_ge(s("lmax"), j.i + 1)
                    act.activation(pe_[:], misc[:, 0:E], ACT.Exp, bias=lmax[:, 0:1], accum_out=psm[:, 0:1]).then_inc(s("lexp"), 1)
                if old:
                    act.wait_ge(s("x1"), j.i + 1)
                    act.dma_start(acc[bass.ds(j.i * P, P)], x1[j.p][:]).then_inc(s(f"x1_out{j.p}"), 16)
                if prev:
                    tent_weights(b)
            tiles(act, 0, 1, lambda t: b_step(t, prev=False, old=False))
            tiles(act, 1, 2, lambda t: b_step(t, old=False))
            tiles(act, 2, LT, b_step)
            tiles(act, LT, LT + 1, lambda t: b_step(t, cur=False))
            tiles(act, LT + 1, LT + 2, lambda t: b_step(t, cur=False, prev=False))

            def rows_high(t):
                for dc in range(DC):
                    act.wait_ge(s("xg_T"), DC * t.i + dc + 1)
                    act.activation(xgT[0][:, dc], bank[4 + dc][:], ACT.Copy).then_inc(s("xgT_high"), 1)

            def weighted(t, c):
                act.wait_ge(s("y_mm"), HC * (t.i + 1))
                if not (isinstance(t.i, int) and t.i == 0 and c < 2):
                    act.wait_ge(s("yu"), CT * t.i + c - 1)
                act.activation(yb[:, c % 2], bank[c][:, D:2 * D], ACT.Copy, scale=wt[:, t.p, c:c + 1]).then_inc(s("yb"), 1)

            def gelu(t, hc):
                act.wait_ge(s("h_mm"), HC * t.i + hc + 1)
                if not (isinstance(t.i, int) and t.i == 0 and hc < 2):
                    act.wait_ge(s("hid_low"), HC * t.i + hc - 1)
                act.activation(hid[hc % 2][:], bank[6 + hc % 2][:], ACT.Gelu_apprx_tanh,
                               bias=b1c[:, bass.ds(t.i, 1), hc].rearrange("p a -> p a")).then_inc(s("gelu"), 1)

            def expert(t, first=False, last=False):
                for hc in range(HC):
                    if hc < 2 and not first:
                        weighted(t.back(1), 2 * hc)
                        weighted(t.back(1), 2 * hc + 1)
                    gelu(t, hc)
                if not last:
                    rows_high(t.ahead(1))
            rows_high(Tile(0, 0, 0))
            expert(Tile(0, 0, 0), first=True)
            tiles(act, 1, 2, expert)
            tiles(act, 2, E - 2, expert)
            expert(Tile(E - 2, E // 2 - 1, 0))
            t = Tile(E - 1, E // 2 - 1, 1)
            expert(t, last=True)
            for c in range(CT):
                weighted(t, c)

        @block.vector
        def _(dve):
            dve.wait_ge(s("x_in"), 16)
            for t in range(LT):
                dve.bn_stats(stats[:, t], x_all[:, t]).then_inc(s("stats"), 1)
            for t in range(LT):
                dve.wait_ge(s("stats"), t + 1)
                dve.bn_aggr(mv[:, t], stats[:, t]).then_inc(s("aggr"), 1)
            dve.wait_ge(s("aggr"), LT)
            dve.tensor_scalar(vpe[:], mv[:, :, 1], LN_EPS, None, ALU.add).then_inc(s("vpe"), 1)

            for u in range(UNITS):
                dve.wait_ge(s("wt_high"), u + 1)
                dve.tensor_tensor(unit_out(u, 1), unit_in(u), unit_out(u, 0).bitcast(f32), ALU.subtract).then_inc(s("wt_low"), 1)

            def norm(t):
                if not (isinstance(t.i, int) and t.i < 2):
                    dve.wait_ge(s("x_T"), t.i - 1)
                dve.tensor_scalar(tin[t.p][:], x_all[:, bass.ds(t.i, 1)].rearrange("p a d -> p (a d)"),
                                  mv[:, bass.ds(t.i, 1), 0], rstd[:, bass.ds(t.i, 1)],
                                  ALU.subtract, ALU.mult).then_inc(s("tin_norm"), 1)

            def proj_step(t, ph, cur=True, nxt=True, old=True):
                if cur:
                    dve.wait_ge(s(f"{ph}_tT_high"), t.i + 1)
                    dve.tensor_tensor(tT[t.p][1][:], bank[t.p][:, 0:D].rearrange("p (c l) -> p c l", c=DC), tT[t.p][0][:].bitcast(f32),
                                      ALU.subtract).then_inc(s(f"{ph}_tT_low"), 1)
                if nxt and ph == "x":
                    norm(t.ahead(1))
                if old:
                    j = t.back(1)
                    kd, vd, bn = (kchar, vchar, 0) if ph == "x" else (ksub, vsub, 2)
                    kq, v = bank[2 + j.p], bank[4 + j.p]
                    dve.wait_ge(s(f"{ph}_high_kqv"), j.i + 1)
                    for oc in range(DC):
                        at_ = bass.ds(j.i * P, P)
                        dve.scalar_tensor_tensor(kd[1][:, oc, at_], kq[:, oc * P:(oc + 1) * P], bias_cols[:, bn + 1, oc:oc + 1],
                                                 kd[0][:, oc, at_].bitcast(f32), ALU.add, ALU.subtract)
                    dve.tensor_tensor(vd[:, bass.ds(j.i, 1), D:2 * D].rearrange("p a d -> p (a d)"), v[:, 0:D],
                                      vd[:, bass.ds(j.i, 1), 0:D].rearrange("p a d -> p (a d)").bitcast(f32),
                                      ALU.subtract).then_inc(s(f"{ph}_low_v"), 1)

            def proj(ph, n):
                proj_step(Tile(0, 0, 0), ph, old=False)
                tiles(dve, 1, n - 1, lambda t: proj_step(t, ph))
                proj_step(Tile(n - 1, (n - 1) // 2, (n - 1) % 2), ph, nxt=False)
                proj_step(Tile(n, n // 2, n % 2), ph, cur=False, nxt=False)
            dve.wait_ge(s("rstd"), 1)
            dve.wait_ge(s("vec_cols"), 1)
            dve.wait_ge(s("aggr"), LT)
            norm(Tile(0, 0, 0))
            proj("x", LT)
            proj("c", CTX)

            def maxima(t, c, ph, chunks, keys):
                w = min(chunks[c][1], keys - chunks[c][0])
                dve.wait_ge(s(f"{ph}_scores"), 4 * t.i + c + 1)
                dve.reduce_max(mx[:, t.p, c:c + 1], scores[c][:, 0:w], AX.X).then_inc(s(f"{ph}_max"), 1)

            def softmax_bias(t, ph):
                dve.wait_ge(s(f"{ph}_max"), 4 * t.i + 4)
                dve.tensor_reduce(nmx[:, t.p:t.p + 1], mx[:, t.p], AX.X, ALU.max, negate=True).then_inc(s(f"{ph}_nmx"), 1)
                dve.wait_ge(s(f"{ph}_nmx"), t.i + 1)
                dve.tensor_scalar(nbias[:, t.p:t.p + 1], nmx[:, t.p:t.p + 1], SCALE, None, ALU.mult).then_inc(s(f"{ph}_bias"), 1)

            def low(t, g, ph, groups):
                n, k = len(groups[g]), groups[g][0]
                dve.wait_ge(s(f"{ph}_high{g % 2}"), 2 * t.i + g // 2 + 1)
                dve.tensor_tensor(pt[1][:, k:k + n], ptb[g % 2][:, 0:n * P].rearrange("p (k l) -> p k l", k=n),
                                  pt[0][:, k:k + n].bitcast(f32), ALU.subtract).then_inc(s(f"{ph}_low{g % 2}"), 1)

            def normalise(t, ph):
                dve.wait_ge(s(f"{ph}_exp"), 4 * t.i + 4)
                then_wait(dve, dve.reduce_sum(zsum[:, 0:1], esum[:, t.p], AX.X), f"{ph}_norm_chain", NORM_STEPS * t.i + 1)
                then_wait(dve, dve.reciprocal(rz[:, 0:1], zsum[:, 0:1]), f"{ph}_norm_chain", NORM_STEPS * t.i + 2)
                dve.wait_ge(s(f"{ph}_pv"), t.i + 1)
                then_wait(dve, dve.tensor_scalar(osb[:], obank[:, D:2 * D], rz[:, 0:1], None, ALU.mult), f"{ph}_norm_chain", NORM_STEPS * t.i + 3)
                wait(dve, s(f"{ph}_att"), t.i)
                dve.scalar_tensor_tensor(onorm[:], obank[:, 0:D], rz[:, 0:1], osb[:], ALU.mult, ALU.add).then_inc(s(f"{ph}_norm"), 1)

            def a_step(t, cur=True, prev=True, old=True):
                b = t.back(1)
                if old:
                    normalise(t.back(2), "a")
                if cur:
                    for c in range(3):
                        maxima(t, c, "a", CHUNKS_A, L)
                if prev:
                    low(b, 0, "a", GROUPS_A)
                if cur:
                    maxima(t, 3, "a", CHUNKS_A, L)
                    softmax_bias(t, "a")
                if prev:
                    for g in (1, 2, 3):
                        low(b, g, "a", GROUPS_A)
            a_step(Tile(0, 0, 0), prev=False, old=False)
            a_step(Tile(1, 0, 1), old=False)
            tiles(dve, 2, CTX, a_step)
            tiles(dve, CTX, CTX + 1, lambda t: a_step(t, cur=False))
            tiles(dve, CTX + 1, CTX + 2, lambda t: a_step(t, cur=False, prev=False))

            dve.wait_ge(s("a_pv"), CTX)
            for p in range(2):
                dve.memset(probs[p][:, C:CTX * P], 0.0).then_inc(s("b_pad"), 1)

            def rank_rows(j):
                dve.wait_ge(s("rank_mm"), j.i + 1)
                then_wait(dve, dve.tensor_tensor(rank[:], misc[:, 0:2 * E].rearrange("p (v e) -> p v e", v=2), counts[:], ALU.add), "rank_chain", RANK_STEPS * j.i + 1)
                then_wait(dve, dve.tensor_tensor(over[:], rank[:], full_e[:], ALU.is_ge), "rank_chain", RANK_STEPS * j.i + 2)
                then_wait(dve, dve.tensor_tensor(counts[:], misc[:, 2 * E:4 * E].rearrange("p (v e) -> p v e", v=2), counts[:], ALU.add), "counts", j.i + 1)
                then_wait(dve, dve.scalar_tensor_tensor(rank[:], over[:], float(SKIP), rank[:], ALU.mult, ALU.add), "rank_chain", RANK_STEPS * j.i + 3)
                then_wait(dve, dve.tensor_tensor(rank[:], rank[:], oneh[:], ALU.mult), "rank_chain", RANK_STEPS * j.i + 4)
                then_wait(dve, dve.reduce_sum(slotf[:], rank[:], AX.X), "rank_chain", RANK_STEPS * j.i + 5)
                dve.tensor_copy(sloti[j.p][:], slotf[:]).then_inc(s("slots"), 1)

            def gate_low(j):
                dve.wait_ge(s("gin_high"), j.i + 1)
                dve.tensor_tensor(ginT[1][:], misc[:].rearrange("p (c l) -> p c l", c=2 * DC), ginT[0][:].bitcast(f32), ALU.subtract).then_inc(s("gin_low"), 1)

            def gate_sum(j):
                dve.wait_ge(s("gate_mm"), j.i + 1)
                then_wait(dve, dve.tensor_tensor(gb[:], misc[:, D:2 * D], bias_rows[:, 2], ALU.add), "zb", j.i + 1)
                dve.tensor_tensor(ga[:], misc[:, 0:D], gb[:], ALU.add).then_inc(s("z"), 1)

            def gate_inverse(j):
                dve.wait_ge(s("gexp"), j.i + 1)
                then_wait(dve, dve.tensor_scalar(gb[:], gb[:], 1.0, None, ALU.add), "gden", j.i + 1)
                dve.reciprocal(ga[:], gb[:]).then_inc(s("gate"), 1)

            def mix_and_norm(j):
                dve.wait_ge(s("base"), j.i + 1)
                dve.wait_ge(s("gate"), j.i + 1)
                then_wait(dve, dve.tensor_tensor(ga[:], ga[:], gdt[:], ALU.mult), "gmix", j.i + 1)
                if not (isinstance(j.i, int) and j.i < 2):
                    dve.wait_ge(s(f"x1_out{j.p}"), 16 * j.half)
                then_wait(dve, dve.tensor_tensor(x1[j.p][:], ga[:], base[:], ALU.add), "x1", j.i + 1)
                then_wait(dve, dve.bn_stats(st1[:], x1[j.p][:]), "st1", j.i + 1)
                dve.sem_inc(s("v_passed"), 1)
                then_wait(dve, dve.bn_aggr(mv1[:], st1[:]), "mv1", j.i + 1)
                dve.tensor_scalar(rs1[:, 0:1], mv1[:, 1:2], LN_EPS, None, ALU.add).then_inc(s("vpe1"), 1)

            def norm_rows(j):
                dve.wait_ge(s("rs1"), j.i + 1)
                if not (isinstance(j.i, int) and j.i < 2):
                    dve.wait_ge(s(f"routed_out{j.p}"), 32 * j.half)
                dve.tensor_scalar(row[j.p][:, 0:D], x1[j.p][:], mv1[:, 0:1], rs1[:, 1:2], ALU.subtract, ALU.mult).then_inc(s("xn2"), 1)

            def choose(j):
                dve.wait_ge(s("logits"), j.i + 1)
                dve.tensor_reduce(lmax[:, 0:1], misc[:, 0:E], AX.X, ALU.max, negate=True).then_inc(s("lmax"), 1)
                dve.wait_ge(s("lexp"), j.i + 1)
                then_wait(dve, dve.reciprocal(psm[:, 1:2], psm[:, 0:1]), "choice_chain", CHOICE_STEPS * j.i + 1)
                then_wait(dve, dve.tensor_scalar(prob[:], pe_[:], psm[:, 1:2], None, ALU.mult), "choice_chain", CHOICE_STEPS * j.i + 2)
                dve.sem_inc(s("v_passed"), 1)
                then_wait(dve, dve.max(best[:], prob[:]), "choice_chain", CHOICE_STEPS * j.i + 3)
                dve.sem_inc(s("v_passed"), 1)
                dve.max_index(besti[:], best[:], prob[:]).then_inc(s("besti"), 1)
                then_wait(dve, dve.tensor_scalar(wsum[:, 0:1], best[:, 0:1], best[:, 1:2], 1e-9, ALU.add, ALU.add), "choice_chain", CHOICE_STEPS * j.i + 4)
                then_wait(dve, dve.reciprocal(wsum[:, 1:2], wsum[:, 0:1]), "choice_chain", CHOICE_STEPS * j.i + 5)
                dve.tensor_scalar(row[j.p][:, D:D + 2], best[:, 0:2], wsum[:, 1:2], tgains[:, 1:2], ALU.mult, ALU.mult)
                dve.wait_ge(s("besti"), j.i + 1)
                then_wait(dve, dve.tensor_copy(bestf[:, 0:2], besti[:, 0:2]), "choice_chain", CHOICE_STEPS * j.i + 6)
                for v in range(2):
                    dve.tensor_scalar(oneh[:, v], iota_e[:], bestf[:, v:v + 1], None, ALU.is_equal).then_inc(s("oneh"), 1)
                wait(dve, s("token"), j.i)
                dve.tensor_copy(row[j.p][:, D + 2:D + 3], token[:])
                dve.tensor_scalar(token[:], token[:], float(P), None, ALU.add).then_inc(s("token"), 1)

            def b_step(t, cur=True, prev=True, old=True, older=True):
                b, j = t.back(1), t.back(2)
                if old:
                    dve.wait_ge(s("tabs"), j.i + 1)
                    dve.tensor_scalar(tdist[:], tdist[:], C / STEP - C // STEP, None, ALU.add).then_inc(s("tdist"), 1)
                    normalise(j, "b")
                if cur:
                    maxima(t, 0, "b", CHUNKS_B, C)
                if older:
                    rank_rows(t.back(3))
                if cur:
                    maxima(t, 1, "b", CHUNKS_B, C)
                if old:
                    gate_low(j)
                if cur:
                    maxima(t, 2, "b", CHUNKS_B, C)
                if prev:
                    low(b, 0, "b", GROUPS_B)
                if cur:
                    maxima(t, 3, "b", CHUNKS_B, C)
                    softmax_bias(t, "b")
                if old:
                    gate_sum(j)
                if prev:
                    low(b, 1, "b", GROUPS_B)
                if old:
                    gate_inverse(j)
                if prev:
                    low(b, 2, "b", GROUPS_B)
                if old:
                    mix_and_norm(j)
                if prev:
                    low(b, 3, "b", GROUPS_B)
                if old:
                    norm_rows(j)
                if old:
                    choose(j)
            dve.wait_ge(s("g_consts"), 1)
            dve.wait_ge(s("tgains"), 1)
            dve.wait_ge(s("a_att"), CTX)
            tiles(dve, 0, 1, lambda t: b_step(t, prev=False, old=False, older=False))
            tiles(dve, 1, 2, lambda t: b_step(t, old=False, older=False))
            tiles(dve, 2, 3, lambda t: b_step(t, older=False))
            tiles(dve, 3, LT, b_step)
            tiles(dve, LT, LT + 1, lambda t: b_step(t, cur=False))
            tiles(dve, LT + 1, LT + 2, lambda t: b_step(t, cur=False, prev=False))
            rank_rows(Tile(LT - 1, (LT - 1) // 2, (LT - 1) % 2))

            dve.wait_ge(s("b_pv"), LT)
            dve.wait_ge(s("counts"), LT)
            then_wait(dve, dve.tensor_tensor(cfill[:], counts[:, 0], base_e[:, 0], ALU.subtract), "e_chain", 1)
            then_wait(dve, dve.tensor_scalar(cfill[:], cfill[:], float(CAP), None, ALU.min), "e_chain", 2)
            for c in range(CT):
                dve.tensor_scalar(slot[:, :, c], base_e[:, 0], prow[:], float(c * P), ALU.add, ALU.add)
                then_wait(dve, dve.tensor_tensor(first_free[:, :, c], base_e[:, 0], cfill[:], ALU.add), "e_chain", 3 + c)
            then_wait(dve, dve.tensor_tensor(smask[:], slot[:], first_free[:], ALU.is_lt), "e_chain", 3 + CT)
            for c in range(CT):
                then_wait(dve, dve.tensor_scalar(shift[:, :, c], cfill[:], -1.0, float(E * CAP), ALU.mult, ALU.add), "e_chain", 4 + CT + c)
            then_wait(dve, dve.tensor_tensor(slot[:], slot[:], shift[:], ALU.add), "e_chain", 4 + 2 * CT)
            then_wait(dve, dve.tensor_tensor(shift[:], shift[:], smask[:], ALU.mult), "e_chain", 5 + 2 * CT)
            then_wait(dve, dve.tensor_tensor(slot[:], slot[:], shift[:], ALU.subtract), "e_chain", 6 + 2 * CT)

            def places(t):
                if not (isinstance(t.i, int) and t.i < 2):
                    dve.wait_ge(s(f"xg_in{t.p}"), 16 * CT * t.half)
                dve.tensor_copy(gcur[t.p][:], slot[:, bass.ds(t.i, 1)].rearrange("p a c -> p (a c)")).then_inc(s("gcur"), 1)

            def rows_low(t):
                for dc in range(DC):
                    dve.wait_ge(s("xgT_high"), DC * t.i + dc + 1)
                    dve.tensor_tensor(xgT[1][:, dc], bank[4 + dc][:], xgT[0][:, dc].bitcast(f32), ALU.subtract).then_inc(s("xgT_low"), 1)

            def weights_and_tokens(t):
                dve.wait_ge(s(f"xg_in{t.p}"), 16 * CT * (t.half + 1))
                m = smask[:, bass.ds(t.i, 1)].rearrange("p a c -> p (a c)")
                then_wait(dve, dve.tensor_tensor(wd[:], xg[t.p][:, :, D], xg[t.p][:, :, D + 1], ALU.subtract), "wd", 2 * t.i + 1)
                then_wait(dve, dve.tensor_tensor(wd[:], wd[:], m, ALU.mult), "wd", 2 * t.i + 2)
                dve.tensor_tensor(wt[:, t.p], wd[:], xg[t.p][:, :, D + 1], ALU.add)
                if not (isinstance(t.i, int) and t.i < 2):
                    dve.wait_ge(s(f"y_out{t.p}"), 16 * CT * t.half)
                dve.tensor_copy(tok[t.p][:], xg[t.p][:, :, D + 2]).then_inc(s("wt"), 1)

            def output_rows(t, c):
                dve.wait_ge(s("yb"), CT * t.i + c + 1)
                then_wait(dve, dve.scalar_tensor_tensor(yu[:, c % 2], bank[c][:, 0:D], wt[:, t.p, c:c + 1], yb[:, c % 2], ALU.mult, ALU.add),
                          "yu", CT * t.i + c + 1)
                if c == 0:
                    dve.wait_ge(s(f"b2_in{t.p}"), 16 * (t.half + 1))
                    if not (isinstance(t.i, int) and t.i == 0):
                        b = t.back(1)
                        dve.wait_ge(s(f"y_out{b.p}"), 16 * CT * (b.half + 1))
                dve.scalar_tensor_tensor(yo[:, c], b2r[:, t.p], wt[:, t.p, c:c + 1], yu[:, c % 2], ALU.mult, ALU.add).then_inc(s("yo"), 1)

            def split_hidden(t, hc):
                dve.wait_ge(s("gelu"), HC * t.i + hc + 1)
                if not (isinstance(t.i, int) and t.i == 0 and hc < 2):
                    dve.wait_ge(s("y_mm"), HC * t.i + hc - 1)
                dve.tensor_copy(hs[hc % 2][0][:], hid[hc % 2][:]).then_inc(s("hid_high"), 1)
                dve.wait_ge(s("hid_high"), HC * t.i + hc + 1)
                dve.tensor_tensor(hs[hc % 2][1][:], hid[hc % 2][:], hs[hc % 2][0][:].bitcast(f32), ALU.subtract).then_inc(s("hid_low"), 1)

            def expert(t, first=False, last=False):
                if not last:
                    places(t.ahead(1))
                for hc in range(HC):
                    if hc < 2 and not first:
                        output_rows(t.back(1), 2 * hc)
                        output_rows(t.back(1), 2 * hc + 1)
                    split_hidden(t, hc)
                if not last:
                    rows_low(t.ahead(1))
                    weights_and_tokens(t.ahead(1))
            places(Tile(0, 0, 0))
            rows_low(Tile(0, 0, 0))
            weights_and_tokens(Tile(0, 0, 0))
            expert(Tile(0, 0, 0), first=True)
            tiles(dve, 1, 2, expert)
            tiles(dve, 2, E - 2, expert)
            expert(Tile(E - 2, E // 2 - 1, 0))
            t = Tile(E - 1, E // 2 - 1, 1)
            expert(t, last=True)
            for c in range(CT):
                output_rows(t, c)

        @block.tensor
        def _(pe):
            def three(dst, lhs, rhs, start, stop):
                pe.matmul(dst, lhs[0], rhs[0], start=start, stop=False)
                pe.matmul(dst, lhs[0], rhs[1], start=False, stop=False)
                return pe.matmul(dst, lhs[1], rhs[0], start=False, stop=stop)

            pe.wait_ge(s("ident"), 1)
            pe.wait_ge(s("weights_in"), 7 * 16)
            for u in range(UNITS):
                for ic in range(DC):
                    for oc in range(DC):
                        raw = w_raw[:, u, oc, ic * P:(ic + 1) * P] if u < 6 else wg_raw[:, oc, ((u - 6) * DC + ic) * P:((u - 6) * DC + ic + 1) * P]
                        m = pe.transpose(bank[u][:, ic * D + oc * P:ic * D + (oc + 1) * P], raw, ident[:])
                m.then_inc(s("wt_T"), 1)
            pe.wait_ge(s("wt_low"), UNITS)
            pe.wait_ge(s("consts_in"), CONSTS * 16)
            pe.transpose(bank[6][:, 0:VECS], vec_rows[:], ident[0:VECS, 0:VECS]).then_inc(s("vec_T"), 1)

            def proj_step(t, ph, cur=True, old=True):
                if cur:
                    if ph == "x":
                        pe.wait_ge(s("tin_norm"), t.i + 1)
                    else:
                        pe.wait_ge(s(f"tin_in{t.p}"), 16 * (t.half + 1))
                        if isinstance(t.i, int) and t.i < 2:
                            pe.wait_ge(s("x_tT_low"), LT)
                    if not (isinstance(t.i, int) and t.i < 2):
                        pe.wait_ge(s(f"{ph}_tT_low"), t.i - 1)
                    for dc in range(DC):
                        m = pe.transpose(bank[t.p][:, dc * P:(dc + 1) * P], tin[t.p][:, dc * P:(dc + 1) * P], ident[:])
                    m.then_inc(s(f"{ph}_T"), 1)
                if old:
                    j = t.back(1)
                    w0 = 0 if ph == "x" else 3
                    kq, v = bank[2 + j.p], bank[4 + j.p]
                    pe.wait_ge(s(f"{ph}_tT_low"), j.i + 1)
                    if isinstance(j.i, int) and j.i < 2:
                        if ph == "c":
                            pe.wait_ge(s("x_low_v"), LT)
                    else:
                        pe.wait_ge(s(f"{ph}_low_v"), j.i - 1)
                    for n, w in enumerate((wT[w0 + 1], wT[w0])):
                        for oc in range(DC):
                            for dc in range(DC):
                                three(kq[:, n * D + oc * P:n * D + (oc + 1) * P],
                                      [w[:, dc, h, oc * P:(oc + 1) * P] for h in range(2)],
                                      [tT[j.p][h][:, dc] for h in range(2)], dc == 0, dc == DC - 1)
                    for dc in range(DC):
                        m = three(v[:, 0:D], [tT[j.p][h][:, dc] for h in range(2)],
                                  [wT[w0 + 2][:, dc, h] for h in range(2)], dc == 0, dc == DC - 1)
                    m.then_inc(s(f"{ph}_mm"), 1)

            def proj(ph, n):
                proj_step(Tile(0, 0, 0), ph, old=False)
                tiles(pe, 1, 3, lambda t: proj_step(t, ph))
                tiles(pe, 3, n - 1, lambda t: proj_step(t, ph))
                proj_step(Tile(n - 1, (n - 1) // 2, (n - 1) % 2), ph)
                proj_step(Tile(n, n // 2, n % 2), ph, cur=False)
            proj("x", LT)
            proj("c", CTX)

            def score(t, c, ph, k, chunks):
                if c == 0:
                    pe.wait_ge(s(f"{ph}_q"), t.i + 1)
                if not (isinstance(t.i, int) and t.i == 0):
                    pe.wait_ge(s(f"{ph}_exp"), 4 * (t.i - 1) + c + 1)
                o, w = chunks[c]
                for dc in range(DC):
                    m = three(scores[c][:, 0:w], [qs[t.p][h][:, dc] for h in range(2)],
                              [k[h][:, dc, o:o + w] for h in range(2)], dc == 0, dc == DC - 1)
                m.then_inc(s(f"{ph}_scores"), 1)

            def transpose_probs(t, g, ph, groups):
                pe.wait_ge(s(f"{ph}_exp"), 4 * t.i + g + 1)
                if not (isinstance(t.i, int) and t.i == 0 and g < 2):
                    pe.wait_ge(s(f"{ph}_low{g % 2}"), 2 * t.i + g // 2)
                for n, k in enumerate(groups[g]):
                    m = pe.transpose(ptb[g % 2][:, n * P:(n + 1) * P], probs[t.p][:, k * P:(k + 1) * P], ident[:])
                m.then_inc(s(f"{ph}_T{g % 2}"), 1)

            def values(t, g, ph, v, groups):
                pe.wait_ge(s(f"{ph}_low{g % 2}"), 2 * t.i + g // 2 + 1)
                if g == 0 and not (isinstance(t.i, int) and t.i == 0):
                    pe.wait_ge(s(f"{ph}_norm"), t.i)
                end = groups[-1][-1]
                for k in groups[g]:
                    pe.matmul(obank[:, 0:2 * D], pt[0][:, k], v[:, k], start=k == 0, stop=False, skip_group_check=True)
                    m = pe.matmul(obank[:, 0:D], pt[1][:, k], v[:, k, 0:D], start=False, stop=k == end, skip_group_check=True)
                if g == 3:
                    m.then_inc(s(f"{ph}_pv"), 1)

            def a_step(t, cur=True, prev=True):
                b = t.back(1)
                if cur:
                    for c in range(3):
                        score(t, c, "a", kchar, CHUNKS_A)
                if prev:
                    transpose_probs(b, 0, "a", GROUPS_A)
                if cur:
                    score(t, 3, "a", kchar, CHUNKS_A)
                if prev:
                    transpose_probs(b, 1, "a", GROUPS_A)
                    values(b, 0, "a", vchar, GROUPS_A)
                    transpose_probs(b, 2, "a", GROUPS_A)
                    values(b, 1, "a", vchar, GROUPS_A)
                    transpose_probs(b, 3, "a", GROUPS_A)
                    values(b, 2, "a", vchar, GROUPS_A)
                    values(b, 3, "a", vchar, GROUPS_A)
            pe.wait_ge(s("c_low_v"), CTX)
            a_step(Tile(0, 0, 0), prev=False)
            tiles(pe, 1, 2, a_step)
            tiles(pe, 2, CTX, a_step)
            tiles(pe, CTX, CTX + 1, lambda t: a_step(t, cur=False))

            def interpolate(j):
                pe.wait_ge(s("tent"), j.i + 1)
                pe.wait_ge(s("subwin_in"), 16 * (j.i + 1))
                if not (isinstance(j.i, int) and j.i == 0):
                    pe.wait_ge(s("lexp"), j.i)
                pe.matmul(misc[:, 0:D], tent[:], subwin[:], start=True, stop=True).then_inc(s("interp"), 1)

            def rank_products(j):
                pe.wait_ge(s("oneh"), 2 * (j.i + 1))
                if isinstance(j.i, int) and j.i == LT - 1:
                    pe.wait_ge(s("lexp"), LT)
                else:
                    pe.wait_ge(s("sub"), j.i + 2)
                pe.matmul(misc[:, 0:2 * E], before[:], oneh[:].rearrange("p v e -> p (v e)"), start=True, stop=True)
                pe.matmul(misc[:, 2 * E:4 * E], ones[:], oneh[:].rearrange("p v e -> p (v e)"), start=True, stop=True).then_inc(s("rank_mm"), 1)

            def gate_transposes(j):
                pe.wait_ge(s("b_att"), j.i + 1)
                pe.wait_ge(s("sub"), j.i + 1)
                if not (isinstance(j.i, int) and j.i == 0):
                    pe.wait_ge(s("counts"), j.i)
                for n, part in enumerate((att[j.p], sub)):
                    for dc in range(DC):
                        m = pe.transpose(misc[:, (n * DC + dc) * P:(n * DC + dc + 1) * P], part[:, dc * P:(dc + 1) * P], ident[:])
                m.then_inc(s("gate_T"), 1)

            def gate_products(j):
                pe.wait_ge(s("gin_low"), j.i + 1)
                for k in range(2 * DC):
                    pe.matmul(misc[:, 0:2 * D], ginT[0][:, k], wgT[:, k].rearrange("p h d -> p (h d)"), start=k == 0, stop=False, skip_group_check=True)
                    m = pe.matmul(misc[:, 0:D], ginT[1][:, k], wgT[:, k, 0], start=False, stop=k == 2 * DC - 1, skip_group_check=True)
                m.then_inc(s("gate_mm"), 1)

            def norm_transposes(j):
                pe.wait_ge(s("xn2"), j.i + 1)
                pe.wait_ge(s("z"), j.i + 1)
                for dc in range(DC):
                    m = pe.transpose(misc[:, dc * P:(dc + 1) * P], row[j.p][:, dc * P:(dc + 1) * P], ident[:])
                m.then_inc(s("xn2_T"), 1)

            def logit_products(j):
                pe.wait_ge(s("xn2T"), j.i + 1)
                for dc in range(DC):
                    m = pe.matmul(misc[:, 0:E], xn2T[:, dc], wroute[:, dc], start=dc == 0, stop=dc == DC - 1)
                m.then_inc(s("logits"), 1)

            def b_step(t, cur=True, prev=True, old=True, older=True):
                b, j = t.back(1), t.back(2)
                if old:
                    interpolate(j)
                if cur:
                    score(t, 0, "b", ksub, CHUNKS_B)
                if older:
                    rank_products(t.back(3))
                if cur:
                    score(t, 1, "b", ksub, CHUNKS_B)
                if old:
                    gate_transposes(j)
                if cur:
                    score(t, 2, "b", ksub, CHUNKS_B)
                if prev:
                    transpose_probs(b, 0, "b", GROUPS_B)
                if old:
                    gate_products(j)
                if cur:
                    score(t, 3, "b", ksub, CHUNKS_B)
                if prev:
                    transpose_probs(b, 1, "b", GROUPS_B)
                    values(b, 0, "b", vsub, GROUPS_B)
                    transpose_probs(b, 2, "b", GROUPS_B)
                    values(b, 1, "b", vsub, GROUPS_B)
                    transpose_probs(b, 3, "b", GROUPS_B)
                    values(b, 2, "b", vsub, GROUPS_B)
                if old:
                    norm_transposes(j)
                if prev:
                    values(b, 3, "b", vsub, GROUPS_B)
                if old:
                    logit_products(j)
            pe.wait_ge(s("a_low0"), 2 * CTX)
            pe.wait_ge(s("a_low1"), 2 * CTX)
            pe.wait_ge(s("a_norm"), CTX)
            pe.wait_ge(s("b_pad"), 2)
            tiles(pe, 0, 1, lambda t: b_step(t, prev=False, old=False, older=False))
            tiles(pe, 1, 2, lambda t: b_step(t, old=False, older=False))
            tiles(pe, 2, 3, lambda t: b_step(t, older=False))
            tiles(pe, 3, LT, b_step)
            tiles(pe, LT, LT + 1, lambda t: b_step(t, cur=False))
            tiles(pe, LT + 1, LT + 2, lambda t: b_step(t, cur=False, prev=False))
            rank_products(Tile(LT - 1, (LT - 1) // 2, (LT - 1) % 2))

            def transpose_rows(t):
                pe.wait_ge(s(f"xg_in{t.p}"), 16 * CT * (t.half + 1))
                if not (isinstance(t.i, int) and t.i == 0):
                    pe.wait_ge(s("xgT_low"), DC * t.i)
                for dc in range(DC):
                    for c in range(CT):
                        m = pe.transpose(bank[4 + dc][:, c * P:(c + 1) * P], xg[t.p][:, c, dc * P:(dc + 1) * P], ident[:])
                    m.then_inc(s("xg_T"), 1)

            def hidden(t, hc):
                if hc == 0:
                    pe.wait_ge(s("xgT_low"), DC * (t.i + 1))
                pe.wait_ge(s("w_split"), HC * t.i + hc + 1)
                if not (isinstance(t.i, int) and t.i == 0 and hc < 2):
                    pe.wait_ge(s("gelu"), HC * t.i + hc - 1)
                for dc in range(DC):
                    m = three(bank[6 + hc % 2][:], [w1s[h][:, dc, hc * P:(hc + 1) * P] for h in range(2)],
                              [xgT[h][:, dc] for h in range(2)], dc == 0, dc == DC - 1)
                m.then_inc(s("h_mm"), 1)

            def outputs(t, hc):
                pe.wait_ge(s("hid_low"), HC * t.i + hc + 1)
                for c in range(CT):
                    if hc == 0 and not (isinstance(t.i, int) and t.i == 0):
                        pe.wait_ge(s("yu"), CT * (t.i - 1) + c + 1)
                    h = hs[hc % 2]
                    pe.matmul(bank[c][:], h[0][:, c * P:(c + 1) * P], w2s[:, hc].rearrange("p h d -> p (h d)"),
                              start=hc == 0, stop=False, skip_group_check=True)
                    m = pe.matmul(bank[c][:, 0:D], h[1][:, c * P:(c + 1) * P], w2s[:, hc, 0],
                                  start=False, stop=hc == HC - 1, skip_group_check=True)
                m.then_inc(s("y_mm"), 1)

            def expert(t, last=False):
                hidden(t, 0)
                for hc in range(1, HC):
                    hidden(t, hc)
                    if hc == HC - 1 and not last:
                        transpose_rows(t.ahead(1))
                    outputs(t, hc - 1)
                outputs(t, HC - 1)
            pe.wait_ge(s("counts"), LT)
            transpose_rows(Tile(0, 0, 0))
            expert(Tile(0, 0, 0))
            tiles(pe, 1, 2, expert)
            tiles(pe, 2, E - 2, expert)
            expert(Tile(E - 2, E // 2 - 1, 0))
            expert(Tile(E - 1, E // 2 - 1, 1), last=True)


_INS = ['x', 'ctx_1024', 'g_xattn', 'g_ffn', 'L0_xattn_Wq_c', 'L0_xattn_bq_c', 'L0_xattn_Wk_s', 'L0_xattn_bk_s',
        'L0_xattn_Wv_s', 'L0_xattn_bv_s', 'L0_xattn_Wq_s', 'L0_xattn_bq_s', 'L0_xattn_Wk_c', 'L0_xattn_bk_c',
        'L0_xattn_Wv_c', 'L0_xattn_bv_c', 'L0_xattn_Wg', 'L0_xattn_bg', 'L0_ffn_Wg', 'L0_ffn_W1', 'L0_ffn_b1',
        'L0_ffn_W2', 'L0_ffn_b2']


def kernel(**inputs):
    import numpy as _np
    import concourse.bacc as _bacc
    from concourse import mybir as _mybir
    from concourse.bass_utils import run_bass_kernel_spmd as _run

    nc = _bacc.Bacc("TRN2", target_bir_lowering=False, num_devices=1)
    arrays, args = {}, []
    for name in _INS:
        a = _np.ascontiguousarray(inputs[name])
        arrays[f"in_{name}_dram"] = a
        args.append(nc.dram_tensor(f"in_{name}_dram", a.shape, _mybir.dt.from_np(a.dtype), kind="ExternalInput").ap())
    out = nc.dram_tensor("out_0_dram", (1, L, D), _mybir.dt.float32, kind="ExternalOutput").ap()
    program(nc, *args, out)
    r = _run(nc, [arrays], core_ids=[0])
    return r.results[0]["out_0_dram"]
```

```python
import concourse.bass as bass
from concourse import mybir
from contextlib import ExitStack, contextmanager

P = 128
D = 256
DC = D // P
E = 8
HID = 1024
HC = HID // P
CAP = 512
CT = CAP // P
L = 2048
LT = L // P
C = 1601
CTX = -(-C // P)
CREM = C - (CTX - 1) * P
CKEYS = C + 1
BANK = 512
ROW = D + 3
SKIP = 1 << 20
SCALE = 1.0 / 16
STEP = L // P
LN_EPS = 1e-5


class Tile:

    def __init__(self, i, half, p):
        self.i, self.half, self.p = i, half, p

    def ahead(self, d):
        p = (self.p + d) % 2
        return Tile(self.i + d, self.half + (self.p + d - p) // 2, p)

    def back(self, d):
        p = (self.p - d) % 2
        return Tile(self.i - d, self.half - (d + p - self.p) // 2, p)


def tiles(eng, first, last, body):
    i = first
    if i % 2:
        body(Tile(i, i // 2, 1))
        i += 1
    pairs = (last - i) // 2
    if pairs >= 2:
        with eng.Fori(i // 2, i // 2 + pairs) as half:
            body(Tile(half * 2, half, 0))
            body(Tile(half * 2 + 1, half, 1))
        i += 2 * pairs
    while i < last:
        body(Tile(i, i // 2, i % 2))
        i += 1


def wait(eng, sem, count):
    if isinstance(count, int) and count <= 0:
        return
    eng.wait_ge(sem, count)


def program(nc, x, ctx_in, g_xattn, g_ffn, Wq_c, bq_c, Wk_s, bk_s, Wv_s, bv_s, Wq_s, bq_s, Wk_c, bk_c,
            Wv_c, bv_c, Wgate, bgate, Wroute, W1, b1, W2, b2, out):
    f32, f32r = mybir.dt.float32, mybir.dt.float32r
    i32, u32 = mybir.dt.int32, mybir.dt.uint32
    ALU, ACT, AX = mybir.AluOpType, mybir.ActivationFunctionType, mybir.AxisListType
    stack = ExitStack()
    with stack:
        top = [(nc.sbuf_base + 63) // 64 * 64]

        def size(shape):
            n = 4
            for v in shape[1:]:
                n *= v
            return (n + 31) // 32 * 32

        def at(name, offset, shape, dt=f32):
            return nc.alloc_sbuf_tensor_at(name, shape, dt, offset=offset)

        def region(n):
            top[0] += n
            assert top[0] <= nc.sbuf_usable_end, top[0]
            return top[0] - n

        def sb(name, shape, dt=f32):
            return at(name, region(size(shape)), shape, dt)

        def inside(start, end):
            used = [start]

            def place(name, shape, dt=f32):
                used[0] += size(shape)
                assert used[0] <= end, (name, used[0] - end)
                return at(name, used[0] - size(shape), shape, dt)
            return place

        def sem(name):
            return stack.enter_context(nc.semaphore(name))

        r_kchar = region(2 * DC * L * 4)
        kchar = [at(f"kchar_{s}", r_kchar + n * DC * L * 4, [P, DC, L], f32r) for n, s in enumerate(("high", "low"))]
        r_vchar = region(LT * 2 * D * 4)
        vchar = at("vchar", r_vchar, [P, LT, 2 * D], f32r)
        r_ksub = region(2 * DC * CTX * P * 4)
        ksub = [at(f"ksub_{s}", r_ksub + n * DC * CTX * P * 4, [P, DC, CTX * P], f32r) for n, s in enumerate(("high", "low"))]
        r_vsub = region(CTX * 2 * D * 4)
        vsub = at("vsub", r_vsub, [P, CTX, 2 * D], f32r)
        r_qchar = region(LT * D * 4)
        qchar = at("qchar", r_qchar, [P, LT, DC, P], f32)
        r_qsub = region(CTX * D * 4)
        qsub = at("qsub", r_qsub, [P, CTX, DC, P], f32)

        r_work = region(2 * L * 4 + 2 * LT * P * 4)
        probs = [at(f"probs{p}", r_work + p * L * 4, [P, L], f32) for p in range(2)]
        r_pt = r_work + 2 * L * 4
        pt = [at(f"probsT_{s}", r_pt + n * LT * P * 4, [P, LT, P], f32r) for n, s in enumerate(("high", "low"))]
        wT = [at(f"wT_{n}", r_work + n * DC * 2 * D * 4, [P, DC, 2, D], f32r) for n in range(6)]
        o = r_work + 6 * DC * 2 * D * 4
        tin = [at(f"tin{p}", o + p * D * 4, [P, D], f32) for p in range(2)]
        tT = [[at(f"tT_{s}{p}", o + (2 + 2 * p + n) * D * 4, [P, DC, P], f32r) for n, s in enumerate(("high", "low"))] for p in range(2)]
        assert o + 6 * D * 4 <= r_work + 2 * L * 4 + 2 * LT * P * 4
        x_all = at("x_all", r_vsub, [P, LT, D], f32)
        w_raw = at("w_raw", r_ksub, [P, 6, DC, D], f32)
        wg_raw = at("wg_raw", r_ksub + 6 * DC * D * 4, [P, DC, 2 * D], f32)

        wgT = sb("wgT", [P, 2 * DC, 2, D], f32r)
        ident = sb("ident", [P, P])
        before = sb("before", [P, P])
        ones = sb("ones", [P, P])
        tent = sb("tent", [P, P])
        tdist = sb("tdist", [P, P])
        tabs = sb("tabs", [P, P])
        tidx = at("tidx", r_vchar, [P, P], i32)
        VECS = E * HC + 4 * DC
        vec_rows = at("vec_rows", r_qsub + 1024, [VECS, P])
        vec_cols = sb("vec_cols", [P, VECS])
        b1c = vec_cols[:, 0:E * HC].rearrange("p (e c) -> p e c", c=HC)
        bias_cols = vec_cols[:, E * HC:VECS].rearrange("p (n c) -> p n c", c=DC)
        bias_rows = sb("bias_rows", [P, 3, D])
        gains = sb("gains", [P, 2])
        tgains = sb("tgains", [P, 2])
        thalf = sb("thalf", [P, 1])
        mhalf = sb("mhalf", [P, LT])
        iota_e = sb("iota_e", [P, E])
        base_e = sb("base_e", [P, 2, E])
        full_e = sb("full_e", [P, 2, E])
        ie = sb("ie", [P, 2 * E], i32)
        wroute = sb("wroute", [P, DC, E])
        token = sb("token", [P, 1])
        prow = sb("prow", [P, 1])
        tok_i = sb("tok_i", [P, 1], i32)
        zrow = at("zrow", r_ksub + 16 * D * 4, [P, CT, ROW], f32)
        ztok = sb("ztok", [P, CT], i32)
        stats = at("stats", r_qsub, [P, LT, 6], f32)
        mv = at("mv", r_qsub + LT * 24, [P, LT, 2], f32)
        rstd = at("rstd", r_qsub + LT * 32, [P, LT], f32)
        vpe = at("vpe", r_qsub + LT * 36, [P, LT], f32)

        qs = [[sb(f"q_{s}{p}", [P, DC, P], f32r) for s in ("high", "low")] for p in range(2)]
        mx = sb("mx", [P, 2, 4])
        nmx = sb("nmx", [P, 2])
        nbias = sb("nbias", [P, 2])
        esum = sb("esum", [P, 2, 4])
        zsum = sb("zsum", [P, 1])
        rz = sb("rz", [P, 2])
        att = [sb(f"att{p}", [P, D]) for p in range(2)]

        in_qsub = inside(r_qsub, r_work)
        xres = [sb(f"xres{p}", [P, D]) for p in range(2)]
        subwin = sb("subwin", [P, D])
        sub = in_qsub("sub", [P, D])
        ginT = [in_qsub(f"ginT_{s}", [P, 2 * DC, P], f32r) for s in ("high", "low")]
        zgate = in_qsub("zgate", [P, D])
        tgate = in_qsub("tgate", [P, D])
        diff = in_qsub("diff", [P, D])
        mixed = in_qsub("mixed", [P, D])
        subt = in_qsub("subt", [P, D])
        base = in_qsub("base", [P, D])
        x1 = [in_qsub(f"x1_{p}", [P, D]) for p in range(2)]
        row = [sb(f"row{p}", [P, ROW]) for p in range(2)]
        st1 = sb("st1", [P, 6])
        mv1 = sb("mv1", [P, 2])
        rs1 = sb("rs1", [P, 2])
        xn2T = sb("xn2T", [P, DC, P])
        lg = sb("lg", [P, E])
        lmax = sb("lmax", [P, 2])
        pe_ = sb("pe_", [P, E])
        psm = sb("psm", [P, 2])
        prob = sb("prob", [P, E])
        best = sb("best", [P, 8])
        besti = sb("besti", [P, 8], u32)
        bestf = sb("bestf", [P, 8])
        wsum = sb("wsum", [P, 2])
        oneh = sb("oneh", [P, 2, E])
        counts = sb("counts", [P, 2, E])
        rank = sb("rank", [P, 2, E])
        over = sb("over", [P, 2, E])
        slotf = sb("slotf", [P, 2])
        sloti = [sb(f"sloti{p}", [P, 2], u32) for p in range(2)]

        place = inside(r_kchar, r_ksub)
        w1_raw = [place(f"w1_raw{p}", [P, DC, HID]) for p in range(2)]
        w2_raw = [place("w2_raw0", [P, HC, D])]
        w1s = [place(f"w1_{h}", [P, DC, HID], f32r) for h in ("high", "low")]
        w2s = place("w2s", [P, HC, 2, D], f32r)
        place = inside(r_ksub, r_qchar)
        w2_raw.append(place("w2_raw1", [P, HC, D]))
        b2r = place("b2r", [P, 2, D])
        xg = [place(f"xg{p}", [P, CT, ROW]) for p in range(2)]
        xgT = [place(f"xgT_{h}", [P, DC, CAP], f32r) for h in ("high", "low")]
        hid = [place(f"hid{p}", [P, CAP]) for p in range(2)]
        hs = [[place(f"hid_{h}{p}", [P, CAP], f32r) for h in ("high", "low")] for p in range(2)]
        wt = place("wt", [P, 2, CT])
        wd = place("wd", [P, CT])
        tok = [place(f"tok{p}", [P, CT], u32) for p in range(2)]
        gcur = [place(f"gcur{p}", [P, CT], u32) for p in range(2)]
        yb = place("yb", [P, CT, D])
        yo = place("yo", [P, CT, D])
        cfill = place("cfill", [P, E])
        slot = place("slot", [P, E, CT])
        first_free = place("first_free", [P, E, CT])
        smask = place("smask", [P, E, CT])
        shift = place("shift", [P, E, CT])

        sub_rows = nc.dram_tensor("sub_rows", [CTX * P + 1, D], f32, kind="Internal").ap()
        routed = nc.dram_tensor("routed", [2 * E * CAP, ROW], f32, kind="Internal").ap()
        acc = nc.dram_tensor("acc", [L + CAP, D], f32, kind="Internal").ap()

        bank = [stack.enter_context(nc.psum_tensor(f"bank{b}", [P, BANK], f32)) for b in range(8)]
        scores, ptb, obank, misc = bank[0:4], bank[4:6], bank[6], bank[7]

        names = {}

        def s(name):
            if name not in names:
                names[name] = sem(name)
            return names[name]

        def then_wait(eng, ins, name, count):
            ins.then_inc(s(name), 1)
            eng.wait_ge(s(name), count)

        RANK_STEPS, CHOICE_STEPS, NORM_STEPS = 5, 6, 2

        xv = x[0].rearrange("(t p) d -> p t d", p=P)
        ov = out[0]
        block = stack.enter_context(nc.Block())

        W6 = (Wq_c, Wk_c, Wv_c, Wq_s, Wk_s, Wv_s)
        UNITS = 8
        CONSTS = 11

        def unit_in(u):
            return bank[u][:].rearrange("p (c o) -> p c o", c=DC)

        def unit_out(u, part):
            return wT[u][:, :, part] if u < 6 else wgT[:, (u - 6) * DC:(u - 5) * DC, part]

        GROUPS_A = [range(4 * g, 4 * g + 4) for g in range(4)]
        GROUPS_B = [range(3 * g, 3 * g + 3) for g in range(3)] + [range(9, CTX)]
        CHUNKS_A = [(BANK * c, BANK) for c in range(4)]
        SLICE = CKEYS // 4 // 2 * 2
        CHUNKS_B = [(0, CKEYS - 3 * SLICE)] + [(CKEYS - (4 - c) * SLICE, SLICE) for c in (1, 2, 3)]

        def ysum(c):
            return bank[c][:, 0:D]

        def row_bcast(v):
            return v.rearrange("(a n) -> a n", a=1).broadcast_to([P, v.shape[0]])

        @block.sync
        def _(sp):
            for n, w in enumerate(W6):
                sp.dma_start(w_raw[:, n], w.rearrange("(c p) i -> p c i", p=P)).then_inc(s("weights_in"), 16)
            sp.dma_start(wg_raw[:], Wgate.rearrange("(c p) i -> p c i", p=P)).then_inc(s("weights_in"), 16)

            def load_context(t, rows=P):
                if isinstance(t.i, int) and t.i < 2:
                    sp.wait_ge(s("x_T"), LT)
                else:
                    sp.wait_ge(s("c_T"), t.i - 1)
                sp.dma_start(tin[t.p][0:rows], ctx_in[0, bass.ds(t.i * P, rows)]).then_inc(s(f"tin_in{t.p}"), 16)
            tiles(sp, 0, 2, load_context)
            tiles(sp, 2, CTX - 1, load_context)
            load_context(Tile(CTX - 1, (CTX - 1) // 2, (CTX - 1) % 2), CREM)

            def store_sub(t):
                sp.wait_ge(s("a_att"), t.i + 1)
                sp.dma_start(sub_rows[bass.ds(t.i * P + 1, P)], att[t.p][:]).then_inc(s(f"sub_out{t.p}"), 16)
            store_sub(Tile(0, 0, 0))
            sp.dma_start(sub_rows[0:1], att[0][0:1]).then_inc(s("sub_first"), 16)
            tiles(sp, 1, CTX - 1, store_sub)
            last = (CTX - 1) % 2
            sp.wait_ge(s("a_att"), CTX)
            sp.dma_start(sub_rows[(CTX - 1) * P + 1:C + 1], att[last][0:CREM]).then_inc(s("sub_edge"), 16)
            sp.dma_start(sub_rows[C + 1:C + 2], att[last][CREM - 1:CREM]).then_inc(s("sub_edge"), 16)
            sp.dma_start(sub_rows[C + 2:CTX * P + 1], att[last][CREM + 1:P]).then_inc(s("sub_edge"), 16)

            for name in ("sub_first", "sub_edge"):
                sp.wait_ge(s(name), 16 if name == "sub_first" else 48)
            sp.wait_ge(s("sub_out0"), 16 * ((CTX - 1) // 2))
            sp.wait_ge(s("sub_out1"), 16 * ((CTX - 1) // 2))

            def load_tile(t):
                wait(sp, s("base"), t.i - 1)
                sp.dma_start(xres[t.p][:], x[0, bass.ds(t.i * P, P)]).then_inc(s(f"xres_in{t.p}"), 16)
                wait(sp, s("interp"), t.i)
                sp.dma_start(subwin[:], sub_rows[bass.ds(t.i * (C // STEP), P)]).then_inc(s("subwin_in"), 16)
            load_tile(Tile(0, 0, 0))
            sp.wait_ge(s("a_pv"), CTX)
            sp.dma_start(w1_raw[0][:], W1[0].rearrange("(c p) h -> p c h", p=P)).then_inc(s("w_in0"), 16)
            sp.dma_start(w2_raw[0][:], W2[0].rearrange("(c p) d -> p c d", p=P)).then_inc(s("w_in0"), 16)
            sp.dma_start(w1_raw[1][:], W1[1].rearrange("(c p) h -> p c h", p=P)).then_inc(s("w_in1"), 16)
            load_tile(Tile(1, 0, 1))
            tiles(sp, 2, LT, load_tile)

            def load_bias(t):
                wait(sp, s("yb"), CT * (t.i - 1))
                sp.dma_start(b2r[:, t.p], b2[bass.ds(t.i, 1)].broadcast_to([P, D])).then_inc(s(f"b2_in{t.p}"), 16)

            def load_expert(t):
                sp.wait_ge(s("w1_split"), (t.i - 1) * HC)
                wait(sp, s("w2_split"), (t.i - 2) * HC)
                sp.dma_start(w1_raw[t.p][:], W1[bass.ds(t.i, 1)].rearrange("a (c p) h -> p (a c) h", p=P)).then_inc(s(f"w_in{t.p}"), 16)
                sp.dma_start(w2_raw[t.p][:], W2[bass.ds(t.i, 1)].rearrange("a (c p) d -> p (a c) d", p=P)).then_inc(s(f"w_in{t.p}"), 16)
                load_bias(t)
            sp.wait_ge(s("b_pv"), LT)
            sp.dma_start(w2_raw[1][:], W2[1].rearrange("(c p) d -> p c d", p=P)).then_inc(s("w_in1"), 16)
            load_bias(Tile(0, 0, 0))
            load_bias(Tile(1, 0, 1))
            tiles(sp, 2, 3, load_expert)
            tiles(sp, 3, E, load_expert)

            for p in range(2):
                sp.wait_ge(s(f"y_out{p}"), 16 * CT * E // 2)
            sp.dma_start(ov, acc[0:L]).then_inc(s("out_done"), 16)
            sp.wait_ge(s("out_done"), 16)

        @block.gpsimd
        def _(gp):
            def apart(name, count):
                gp.wait_ge(s(name), count)
                gp.sem_inc(s("g_passed"), 1)

            gp.memset(ident[:], 0.0)
            gp.memset(zrow[:], 0.0)
            gp.memset(ones[:], 1.0).then_inc(s("g_fill"), 1)
            gp.wait_ge(s("g_fill"), 1)
            gp.affine_select(out=ident[:], in_=ident[:], compare_op=ALU.not_equal, fill=1.0, base=0,
                             pattern=[[-1, P]], channel_multiplier=1)
            gp.affine_select(out=before[:], in_=ones[:], compare_op=ALU.is_gt, fill=0.0, base=0,
                             pattern=[[1, P]], channel_multiplier=-1).then_inc(s("ident"), 1)
            gp.memset(mhalf[:], -0.5)
            gp.iota(ztok[:], pattern=[[1, CT]], base=L, channel_multiplier=CT)
            gp.iota(tidx[:], pattern=[[2 * C, P]], base=C + L, channel_multiplier=-2 * L)
            gp.iota(ie[:, 0:E], pattern=[[1, E]], base=0, channel_multiplier=0)
            gp.iota(ie[:, E:2 * E], pattern=[[CAP, E]], base=0, channel_multiplier=0)
            gp.iota(tok_i[:], pattern=[[0, 1]], base=0, channel_multiplier=1).then_inc(s("g_iota"), 1)
            gp.wait_ge(s("g_iota"), 1)
            gp.tensor_copy(zrow[:, :, ROW - 1], ztok[:]).then_inc(s("zrow"), 1)
            for v in (0, 1):
                gp.tensor_scalar(base_e[:, v], ie[:, E:2 * E], float(v * E * CAP), None, ALU.add)
                gp.tensor_scalar(full_e[:, v], ie[:, E:2 * E], float(v * E * CAP + CAP), None, ALU.add)
                gp.tensor_scalar(counts[:, v], ie[:, E:2 * E], float(v * E * CAP), None, ALU.add)
            gp.tensor_copy(iota_e[:], ie[:, 0:E])
            gp.tensor_copy(token[:], tok_i[:])
            gp.tensor_copy(prow[:], tok_i[:])
            gp.tensor_scalar(tdist[:], tidx[:], 1.0 / (2 * L), None, ALU.mult).then_inc(s("g_consts"), 1)
            gp.wait_ge(s("vpe"), 1)
            gp.tensor_tensor(rstd[:], vpe[:], mhalf[:], ALU.pow).then_inc(s("rstd"), 1)

            def split_queries(src, t, ph):
                q = src[:, bass.ds(t.i, 1)].rearrange("p a c l -> p (a c) l")
                if not (isinstance(t.i, int) and t.i < 2):
                    apart(f"{ph}_scores", 4 * (t.i - 1))
                gp.tensor_copy(qs[t.p][0][:], q).then_inc(s(f"{ph}_qh"), 1)
                apart(f"{ph}_qh", t.i + 1)
                gp.tensor_tensor(qs[t.p][1][:], q, qs[t.p][0][:].bitcast(f32), ALU.subtract).then_inc(s(f"{ph}_q"), 1)

            gp.wait_ge(s("consts_in"), CONSTS * 16)
            for name in ("c_high_kqv", "c_low_v"):
                gp.wait_ge(s(name), CTX)
            split_queries(qsub, Tile(0, 0, 0), "a")
            split_queries(qsub, Tile(1, 0, 1), "a")
            tiles(gp, 2, CTX, lambda t: split_queries(qsub, t, "a"))

            def residual_parts(j):
                gp.wait_ge(s("b_att"), j.i + 1)
                gp.wait_ge(s("sub"), j.i + 1)
                if not (isinstance(j.i, int) and j.i < 1):
                    gp.wait_ge(s("x1"), j.i)
                gp.tensor_tensor(diff[:], att[j.p][:], sub[:], ALU.subtract).then_inc(s("diff"), 1)
                gp.wait_ge(s(f"xres_in{j.p}"), 16 * (j.half + 1))
                gp.tensor_tensor(base[:], subt[:], xres[j.p][:], ALU.add).then_inc(s("base"), 1)

            def inverse_deviation(j):
                gp.wait_ge(s("vpe1"), j.i + 1)
                gp.tensor_tensor(rs1[:, 1:2], rs1[:, 0:1], mhalf[:, 0:1], ALU.pow).then_inc(s("rs1"), 1)

            def route(j):
                apart("slots", j.i + 1)
                for v in range(2):
                    gp.indirect_dma_start(out=routed, out_offset=bass.IndirectOffsetOnAxis(ap=sloti[j.p][:, v:v + 1], axis=0),
                                          in_=row[j.p][:], in_offset=None,
                                          bounds_check=2 * E * CAP - 1, oob_is_err=False).then_inc(s(f"routed_out{j.p}"), 16)

            def b_step(t, cur=True, old=True, older=True, weights=False):
                if cur:
                    split_queries(qchar, t.ahead(1), "b")
                if old:
                    residual_parts(t.back(2))
                if weights:
                    split_first_weights(t.i - 4)
                if old:
                    inverse_deviation(t.back(2))
                if older:
                    route(t.back(3))

            def split_first_weights(hc):
                cols, chunk = bass.ds(hc * P, P), bass.ds(hc, 1)
                gp.tensor_copy(w1s[0][:, :, cols], w1_raw[0][:, :, cols])
                gp.tensor_copy(w2s[:, chunk, 0], w2_raw[0][:, chunk]).then_inc(s("w_first_high"), 1)
                gp.wait_ge(s("w_first_high"), hc + 1)
                gp.tensor_tensor(w2s[:, chunk, 1], w2_raw[0][:, chunk], w2s[:, chunk, 0].bitcast(f32), ALU.subtract).then_inc(s("w2_first"), 1)
                gp.tensor_tensor(w1s[1][:, :, cols], w1_raw[0][:, :, cols], w1s[0][:, :, cols].bitcast(f32), ALU.subtract).then_inc(s("w1_split"), 1)

            def w1_low(t, hc):
                cols = slice(hc * P, hc * P + P)
                gp.wait_ge(s("w1_high"), HC * (t.i - 1) + hc + 1)
                gp.tensor_tensor(w1s[1][:, :, cols], w1_raw[t.p][:, :, cols], w1s[0][:, :, cols].bitcast(f32), ALU.subtract).then_inc(s("w1_split"), 1)

            gp.wait_ge(s("a_scores"), 4 * CTX)
            split_queries(qchar, Tile(0, 0, 0), "b")
            tiles(gp, 0, 2, lambda t: b_step(t, old=False, older=False))
            tiles(gp, 2, 3, lambda t: b_step(t, older=False))
            gp.wait_ge(s("empty_in"), 16 * (2 * E + CT))
            tiles(gp, 3, 4, b_step)
            apart("w_in0", 32)
            tiles(gp, 4, 4 + HC, lambda t: b_step(t, weights=True))
            tiles(gp, 4 + HC, LT - 1, b_step)
            tiles(gp, LT - 1, LT + 2, lambda t: b_step(t, cur=False))
            tiles(gp, LT + 2, LT + 3, lambda t: b_step(t, cur=False, old=False))

            def gather(t):
                apart("gcur", t.i + 1)
                for c in range(CT):
                    gp.indirect_dma_start(out=xg[t.p][:, c], out_offset=None, in_=routed,
                                          in_offset=bass.IndirectOffsetOnAxis(ap=gcur[t.p][:, c:c + 1], axis=0),
                                          bounds_check=2 * E * CAP - 1, oob_is_err=False).then_inc(s(f"xg_in{t.p}"), 16)

            def add_rows(t):
                for c in range(CT):
                    apart("yo", CT * t.i + c + 1)
                    if c == 0 and not (isinstance(t.i, int) and t.i == 0):
                        b = t.back(1)
                        apart(f"y_out{b.p}", 16 * CT * (b.half + 1))
                    gp.indirect_dma_start(out=acc, out_offset=bass.IndirectOffsetOnAxis(ap=tok[t.p][:, c:c + 1], axis=0),
                                          in_=yo[:, c], in_offset=None, bounds_check=L + CAP - 1, oob_is_err=True,
                                          compute_op=ALU.add).then_inc(s(f"y_out{t.p}"), 16)

            def expert(t, first=False, last=False):
                if not first:
                    add_rows(t.back(1))
                if not last:
                    n = t.ahead(1)
                    gather(n)
                    for hc in range(HC):
                        w1_low(n, hc)

            for p in range(2):
                gp.wait_ge(s(f"routed_out{p}"), 16 * LT)
            gather(Tile(0, 0, 0))
            for p in range(2):
                gp.wait_ge(s(f"x1_out{p}"), 16 * LT // 2)
            expert(Tile(0, 0, 0), first=True)
            tiles(gp, 1, 2, expert)
            tiles(gp, 2, E - 2, expert)
            expert(Tile(E - 2, E // 2 - 1, 0))
            expert(Tile(E - 1, E // 2 - 1, 1), last=True)
            add_rows(Tile(E - 1, E // 2 - 1, 1))

        @block.scalar
        def _(act):
            act.dma_start(x_all[:], xv).then_inc(s("x_in"), 16)
            for n, b in enumerate((bq_c, bk_c, bq_s, bk_s)):
                act.dma_start(vec_rows[E * HC + n * DC:E * HC + (n + 1) * DC], b.rearrange("(c p) -> c p", p=P)).then_inc(s("consts_in"), 16)
            act.dma_start(vec_rows[0:E * HC], b1.rearrange("e (c p) -> (e c) p", p=P)).then_inc(s("consts_in"), 16)
            for n, b in enumerate((bv_s, bv_c, bgate)):
                act.dma_start(bias_rows[:, n], row_bcast(b)).then_inc(s("consts_in"), 16)
            for n, g in enumerate((g_xattn, g_ffn)):
                act.dma_start(gains[:, n:n + 1], row_bcast(g)).then_inc(s("consts_in"), 16)
            act.dma_start(wroute[:], Wroute.rearrange("(c p) e -> p c e", p=P)).then_inc(s("consts_in"), 16)
            act.wait_ge(s("zrow"), 1)
            for e in range(2 * E):
                act.dma_start(routed[e * CAP:(e + 1) * CAP].rearrange("(p r) n -> p r n", p=P), zrow[:]).then_inc(s("empty_in"), 16)
            for c in range(CT):
                act.dma_start(acc[L + c * P:L + (c + 1) * P], zrow[:, c, 0:D]).then_inc(s("empty_in"), 16)
            act.wait_ge(s("consts_in"), CONSTS * 16)
            act.wait_ge(s("g_consts"), 1)
            act.activation(tgains[:], gains[:], ACT.Tanh).then_inc(s("tgains"), 1)

            for u in range(UNITS):
                act.wait_ge(s("wt_T"), u + 1)
                act.activation(unit_out(u, 0), unit_in(u), ACT.Copy).then_inc(s("wt_high"), 1)

            act.wait_ge(s("vec_T"), 1)
            act.activation(vec_cols[:], bank[6][:, 0:VECS], ACT.Copy).then_inc(s("vec_cols"), 1)
            act.wait_ge(s("vec_cols"), 1)

            def proj_step(t, ph, cur=True, old=True):
                if cur:
                    act.wait_ge(s(f"{ph}_T"), t.i + 1)
                    act.activation(tT[t.p][0][:], bank[t.p][:, 0:D].rearrange("p (c l) -> p c l", c=DC), ACT.Copy).then_inc(s(f"{ph}_tT_high"), 1)
                if old:
                    j = t.back(1)
                    kd, vd, qd, bn = (kchar, vchar, qchar, 0) if ph == "x" else (ksub, vsub, qsub, 2)
                    kq, v = bank[2 + j.p], bank[4 + j.p]
                    act.wait_ge(s(f"{ph}_mm"), j.i + 1)
                    if ph == "c" and isinstance(j.i, int) and j.i == 0:
                        act.wait_ge(s("empty_in"), 16 * (2 * E + CT))
                    for oc in range(DC):
                        act.activation(kd[0][:, oc, bass.ds(j.i * P, P)], kq[:, oc * P:(oc + 1) * P], ACT.Identity,
                                       bias=bias_cols[:, bn + 1, oc:oc + 1])
                    for oc in range(DC):
                        act.activation(qd[:, bass.ds(j.i, 1), oc].rearrange("p a l -> p (a l)"), kq[:, D + oc * P:D + (oc + 1) * P], ACT.Identity,
                                       bias=bias_cols[:, bn, oc:oc + 1])
                    act.activation(vd[:, bass.ds(j.i, 1), 0:D].rearrange("p a d -> p (a d)"), v[:, 0:D], ACT.Copy).then_inc(s(f"{ph}_high_kqv"), 1)

            def proj(ph, n):
                proj_step(Tile(0, 0, 0), ph, old=False)
                tiles(act, 1, n, lambda t: proj_step(t, ph))
                proj_step(Tile(n, n // 2, n % 2), ph, cur=False)
            proj("x", LT)
            proj("c", CTX)

            def high(t, g, ph, groups):
                n = len(groups[g])
                act.wait_ge(s(f"{ph}_T{g % 2}"), 2 * t.i + g // 2 + 1)
                act.activation(pt[0][:, groups[g][0]:groups[g][0] + n], ptb[g % 2][:, 0:n * P].rearrange("p (k l) -> p k l", k=n),
                               ACT.Copy).then_inc(s(f"{ph}_high{g % 2}"), 1)

            def exps(t, c, ph, chunks, keys):
                act.wait_ge(s(f"{ph}_bias"), t.i + 1)
                o, w = chunks[c][0], min(chunks[c][1], keys - chunks[c][0])
                act.activation(probs[t.p][:, o:o + w], scores[c][:, 0:w], ACT.Exp, bias=nbias[:, t.p:t.p + 1], scale=SCALE,
                               accum_out=esum[:, t.p, c:c + 1]).then_inc(s(f"{ph}_exp"), 1)

            def a_step(t, cur=True, prev=True):
                b = t.back(1)
                for g in range(2):
                    if prev:
                        high(b, g, "a", GROUPS_A)
                for g in range(2):
                    if cur:
                        exps(t, 2 * g, "a", CHUNKS_A, L)
                        exps(t, 2 * g + 1, "a", CHUNKS_A, L)
                    if prev:
                        high(b, 2 + g, "a", GROUPS_A)
            a_step(Tile(0, 0, 0), prev=False)
            tiles(act, 1, CTX, a_step)

            def tent_weights(j):
                if isinstance(j.i, int) and j.i == 0:
                    act.wait_ge(s("g_consts"), 1)
                else:
                    act.wait_ge(s("interp"), j.i)
                    act.wait_ge(s("tdist"), j.i)
                act.activation(tabs[:], tdist[:], ACT.Abs).then_inc(s("tabs"), 1)
                act.wait_ge(s("tabs"), j.i + 1)
                act.activation(tent[:], tabs[:], ACT.Relu, scale=-1.0, bias=ones[:, 0:1]).then_inc(s("tent"), 1)

            def rows_transposed(o):
                act.wait_ge(s("xn2_T"), o.i + 1)
                act.activation(xn2T[:], obank[:, 0:D].rearrange("p (c l) -> p c l", c=DC), ACT.Copy).then_inc(s("xn2T"), 1)

            def interpolated(j):
                act.wait_ge(s("interp"), j.i + 1)
                if not (isinstance(j.i, int) and j.i < 1):
                    act.wait_ge(s("base"), j.i)
                act.activation(sub[:], misc[:, 0:D], ACT.Copy)
                act.activation(subt[:], misc[:, 0:D], ACT.Copy, scale=tgains[:, 0:1]).then_inc(s("sub"), 1)

            def logit_exps(o):
                act.wait_ge(s("lmax"), o.i + 1)
                act.activation(pe_[:], obank[:, 0:E], ACT.Exp, bias=lmax[:, 0:1], accum_out=psm[:, 0:1]).then_inc(s("lexp"), 1)

            def gate_high(j):
                act.wait_ge(s("gate_T"), j.i + 1)
                act.activation(ginT[0][:], misc[:].rearrange("p (c l) -> p c l", c=2 * DC), ACT.Copy).then_inc(s("gin_high"), 1)

            def gate_tanh(j):
                act.wait_ge(s("z"), j.i + 1)
                act.activation(tgate[:], zgate[:], ACT.Tanh, scale=0.5).then_inc(s("tgate"), 1)

            def b_step(t, cur=True, prev=True, old=True, older=True):
                b, j, o = t.back(1), t.back(2), t.back(3)
                if old:
                    interpolated(j)
                if older:
                    rows_transposed(o)
                if older:
                    logit_exps(o)
                if old:
                    gate_high(j)
                if prev:
                    high(b, 0, "b", GROUPS_B)
                    high(b, 1, "b", GROUPS_B)
                if cur:
                    exps(t, 0, "b", CHUNKS_B, C)
                    exps(t, 1, "b", CHUNKS_B, C)
                if old:
                    gate_tanh(j)
                if prev:
                    high(b, 2, "b", GROUPS_B)
                if cur:
                    exps(t, 2, "b", CHUNKS_B, C)
                    exps(t, 3, "b", CHUNKS_B, C)
                if prev:
                    high(b, 3, "b", GROUPS_B)
                if old:
                    act.wait_ge(s("x1"), j.i + 1)
                    act.dma_start(acc[bass.ds(j.i * P, P)], x1[j.p][:]).then_inc(s(f"x1_out{j.p}"), 16)
                if prev:
                    tent_weights(b)
            for g in range(4):
                high(Tile(CTX - 1, (CTX - 1) // 2, (CTX - 1) % 2), g, "a", GROUPS_A)
            act.wait_ge(s("a_norm_chain"), NORM_STEPS * CTX)
            act.wait_ge(s("a_T0"), 2 * CTX)
            act.wait_ge(s("a_T1"), 2 * CTX)
            tiles(act, 0, 1, lambda t: b_step(t, prev=False, old=False, older=False))
            tiles(act, 1, 2, lambda t: b_step(t, old=False, older=False))
            tiles(act, 2, 3, lambda t: b_step(t, older=False))
            tiles(act, 3, LT, b_step)
            tiles(act, LT, LT + 1, lambda t: b_step(t, cur=False))
            tiles(act, LT + 1, LT + 2, lambda t: b_step(t, cur=False, prev=False))
            tiles(act, LT + 2, LT + 3, lambda t: b_step(t, cur=False, prev=False, old=False))

            def rows_high(t):
                for dc in range(DC):
                    act.wait_ge(s("xg_T"), DC * t.i + dc + 1)
                    act.activation(xgT[0][:, dc], bank[4 + dc][:], ACT.Copy).then_inc(s("xgT_high"), 1)

            def weighted(t, c):
                act.wait_ge(s("yb"), CT * t.i + c + 1)
                if c == 0 and not (isinstance(t.i, int) and t.i == 0):
                    b = t.back(1)
                    act.wait_ge(s(f"y_out{b.p}"), 16 * CT * (b.half + 1))
                act.activation(yo[:, c], yb[:, c], ACT.Copy, scale=wt[:, t.p, c:c + 1]).then_inc(s("yo"), 1)

            def gelu(t, hc):
                act.wait_ge(s("h_mm"), HC * t.i + hc + 1)
                if not (isinstance(t.i, int) and t.i == 0 and hc < 2):
                    act.wait_ge(s("hid_low"), HC * t.i + hc - 1)
                act.activation(hid[hc % 2][:], bank[6 + hc % 2][:], ACT.Gelu_apprx_tanh,
                               bias=b1c[:, bass.ds(t.i, 1), hc].rearrange("p a -> p a")).then_inc(s("gelu"), 1)

            def w1_high(t, hc):
                if hc == 0:
                    act.wait_ge(s(f"w_in{t.p}"), 32 * (t.half + 1))
                cols = slice(hc * P, hc * P + P)
                act.wait_ge(s("h_mm"), HC * (t.i - 1) + hc + 1)
                act.activation(w1s[0][:, :, cols], w1_raw[t.p][:, :, cols], ACT.Copy).then_inc(s("w1_high"), 1)

            def w2_high(t, hc):
                act.wait_ge(s("y_mm"), HC * (t.i - 1) + hc + 1)
                act.activation(w2s[:, hc, 0], w2_raw[t.p][:, hc], ACT.Copy).then_inc(s("w2_high"), 1)

            def expert(t, first=False, last=False):
                n = t.ahead(1)
                for hc in range(HC):
                    if hc < 2 and not first:
                        weighted(t.back(1), 2 * hc)
                        weighted(t.back(1), 2 * hc + 1)
                    gelu(t, hc)
                    if hc > 0 and not last:
                        w1_high(n, hc - 1)
                    if hc > 1 and not last:
                        w2_high(n, hc - 2)
                if not last:
                    rows_high(n)
                    w1_high(n, HC - 1)
                    w2_high(n, HC - 2)
                    w2_high(n, HC - 1)
            rows_high(Tile(0, 0, 0))
            expert(Tile(0, 0, 0), first=True)
            tiles(act, 1, 2, expert)
            tiles(act, 2, E - 2, expert)
            expert(Tile(E - 2, E // 2 - 1, 0))
            t = Tile(E - 1, E // 2 - 1, 1)
            expert(t, last=True)
            for c in range(CT):
                weighted(t, c)

        @block.vector
        def _(dve):
            dve.wait_ge(s("x_in"), 16)
            for t in range(LT):
                dve.bn_stats(stats[:, t], x_all[:, t]).then_inc(s("stats"), 1)
            for t in range(LT):
                dve.wait_ge(s("stats"), t + 1)
                dve.bn_aggr(mv[:, t], stats[:, t]).then_inc(s("aggr"), 1)
            dve.wait_ge(s("aggr"), LT)
            dve.tensor_scalar(vpe[:], mv[:, :, 1], LN_EPS, None, ALU.add).then_inc(s("vpe"), 1)

            for u in range(UNITS):
                dve.wait_ge(s("wt_high"), u + 1)
                dve.tensor_tensor(unit_out(u, 1), unit_in(u), unit_out(u, 0).bitcast(f32), ALU.subtract).then_inc(s("wt_low"), 1)

            def norm(t):
                if not (isinstance(t.i, int) and t.i < 2):
                    dve.wait_ge(s("x_T"), t.i - 1)
                dve.tensor_scalar(tin[t.p][:], x_all[:, bass.ds(t.i, 1)].rearrange("p a d -> p (a d)"),
                                  mv[:, bass.ds(t.i, 1), 0], rstd[:, bass.ds(t.i, 1)],
                                  ALU.subtract, ALU.mult).then_inc(s("tin_norm"), 1)

            def proj_step(t, ph, cur=True, nxt=True, old=True):
                if cur:
                    dve.wait_ge(s(f"{ph}_tT_high"), t.i + 1)
                    dve.tensor_tensor(tT[t.p][1][:], bank[t.p][:, 0:D].rearrange("p (c l) -> p c l", c=DC), tT[t.p][0][:].bitcast(f32),
                                      ALU.subtract).then_inc(s(f"{ph}_tT_low"), 1)
                if nxt and ph == "x":
                    norm(t.ahead(1))
                if old:
                    j = t.back(1)
                    kd, vd, bn = (kchar, vchar, 0) if ph == "x" else (ksub, vsub, 2)
                    kq, v = bank[2 + j.p], bank[4 + j.p]
                    dve.wait_ge(s(f"{ph}_high_kqv"), j.i + 1)
                    for oc in range(DC):
                        at_ = bass.ds(j.i * P, P)
                        dve.scalar_tensor_tensor(kd[1][:, oc, at_], kq[:, oc * P:(oc + 1) * P], bias_cols[:, bn + 1, oc:oc + 1],
                                                 kd[0][:, oc, at_].bitcast(f32), ALU.add, ALU.subtract)
                    dve.tensor_tensor(vd[:, bass.ds(j.i, 1), D:2 * D].rearrange("p a d -> p (a d)"), v[:, 0:D],
                                      vd[:, bass.ds(j.i, 1), 0:D].rearrange("p a d -> p (a d)").bitcast(f32),
                                      ALU.subtract).then_inc(s(f"{ph}_low_v"), 1)

            def proj(ph, n):
                proj_step(Tile(0, 0, 0), ph, old=False)
                tiles(dve, 1, n - 1, lambda t: proj_step(t, ph))
                proj_step(Tile(n - 1, (n - 1) // 2, (n - 1) % 2), ph, nxt=False)
                proj_step(Tile(n, n // 2, n % 2), ph, cur=False, nxt=False)
            dve.wait_ge(s("rstd"), 1)
            dve.wait_ge(s("vec_cols"), 1)
            dve.wait_ge(s("aggr"), LT)
            norm(Tile(0, 0, 0))
            proj("x", LT)
            proj("c", CTX)

            def maxima(t, c, ph, chunks, keys):
                w = min(chunks[c][1], keys - chunks[c][0])
                dve.wait_ge(s(f"{ph}_scores"), 4 * t.i + c + 1)
                dve.reduce_max(mx[:, t.p, c:c + 1], scores[c][:, 0:w], AX.X).then_inc(s(f"{ph}_max"), 1)

            def softmax_bias(t, ph):
                dve.wait_ge(s(f"{ph}_max"), 4 * t.i + 4)
                dve.tensor_reduce(nmx[:, t.p:t.p + 1], mx[:, t.p], AX.X, ALU.max, negate=True).then_inc(s(f"{ph}_nmx"), 1)
                dve.wait_ge(s(f"{ph}_nmx"), t.i + 1)
                dve.tensor_scalar(nbias[:, t.p:t.p + 1], nmx[:, t.p:t.p + 1], SCALE, None, ALU.mult).then_inc(s(f"{ph}_bias"), 1)

            def low(t, g, ph, groups):
                n, k = len(groups[g]), groups[g][0]
                dve.wait_ge(s(f"{ph}_high{g % 2}"), 2 * t.i + g // 2 + 1)
                dve.tensor_tensor(pt[1][:, k:k + n], ptb[g % 2][:, 0:n * P].rearrange("p (k l) -> p k l", k=n),
                                  pt[0][:, k:k + n].bitcast(f32), ALU.subtract).then_inc(s(f"{ph}_low{g % 2}"), 1)

            def inverse_sums(t, ph):
                dve.wait_ge(s(f"{ph}_exp"), 4 * t.i + 4)
                then_wait(dve, dve.reduce_sum(zsum[:], esum[:, t.p], AX.X), f"{ph}_norm_chain", NORM_STEPS * t.i + 1)
                dve.reciprocal(rz[:, t.p:t.p + 1], zsum[:]).then_inc(s(f"{ph}_norm_chain"), 1)

            def attention_rows(t, ph, n):
                dve.wait_ge(s(f"{ph}_norm_chain"), NORM_STEPS * (t.i + 1))
                if ph == "a" and not (isinstance(t.i, int) and t.i < 2):
                    dve.wait_ge(s(f"sub_out{t.p}"), 16 * t.half)
                if ph == "b" and not (isinstance(t.i, int) and t.i < 2):
                    dve.wait_ge(s("gate_T"), t.i - 1)
                    dve.wait_ge(s("diff"), t.i - 1)
                dve.wait_ge(s(f"{ph}_pv"), t.i + 1)
                dve.scalar_tensor_tensor(att[t.p][:], obank[:, 0:D], rz[:, t.p:t.p + 1], bias_rows[:, n],
                                         ALU.mult, ALU.add).then_inc(s(f"{ph}_att"), 1)

            def a_step(t, cur=True, prev=True, old=True):
                b = t.back(1)
                if old:
                    attention_rows(t.back(2), "a", 1)
                if cur:
                    for c in range(3):
                        maxima(t, c, "a", CHUNKS_A, L)
                if prev:
                    low(b, 0, "a", GROUPS_A)
                if cur:
                    maxima(t, 3, "a", CHUNKS_A, L)
                    softmax_bias(t, "a")
                if prev:
                    for g in (1, 2, 3):
                        low(b, g, "a", GROUPS_A)
                    inverse_sums(b, "a")
            a_step(Tile(0, 0, 0), prev=False, old=False)
            a_step(Tile(1, 0, 1), old=False)
            a_step(Tile(2, 1, 0))
            a_step(Tile(3, 1, 1))
            dve.wait_ge(s("sub_first"), 16)
            tiles(dve, 4, CTX, a_step)

            last, first = Tile(CTX - 1, (CTX - 1) // 2, (CTX - 1) % 2), Tile(0, 0, 0)
            attention_rows(last.back(1), "a", 1)
            inverse_sums(last, "a")
            for c in range(3):
                maxima(first, c, "b", CHUNKS_B, C)
            low(last, 0, "a", GROUPS_A)
            maxima(first, 3, "b", CHUNKS_B, C)
            softmax_bias(first, "b")
            for g in (1, 2, 3):
                low(last, g, "a", GROUPS_A)
            dve.wait_ge(s("a_T0"), 2 * CTX)
            dve.wait_ge(s("a_T1"), 2 * CTX)
            for p in range(2):
                dve.memset(probs[p][:, C:CTX * P], 0.0).then_inc(s("b_pad"), 1)
            attention_rows(last, "a", 1)

            def rank_rows(j):
                dve.wait_ge(s("rank_mm"), j.i + 1)
                then_wait(dve, dve.tensor_tensor(rank[:], misc[:, 0:2 * E].rearrange("p (v e) -> p v e", v=2), counts[:], ALU.add), "rank_chain", RANK_STEPS * j.i + 1)
                then_wait(dve, dve.tensor_tensor(over[:], rank[:], full_e[:], ALU.is_ge), "rank_chain", RANK_STEPS * j.i + 2)
                then_wait(dve, dve.tensor_tensor(counts[:], misc[:, 2 * E:4 * E].rearrange("p (v e) -> p v e", v=2), counts[:], ALU.add), "counts", j.i + 1)
                then_wait(dve, dve.scalar_tensor_tensor(rank[:], over[:], float(SKIP), rank[:], ALU.mult, ALU.add), "rank_chain", RANK_STEPS * j.i + 3)
                then_wait(dve, dve.tensor_tensor(rank[:], rank[:], oneh[:], ALU.mult), "rank_chain", RANK_STEPS * j.i + 4)
                then_wait(dve, dve.reduce_sum(slotf[:], rank[:], AX.X), "rank_chain", RANK_STEPS * j.i + 5)
                dve.tensor_copy(sloti[j.p][:], slotf[:]).then_inc(s("slots"), 1)

            def gate_low(j):
                dve.wait_ge(s("gin_high"), j.i + 1)
                dve.tensor_tensor(ginT[1][:], misc[:].rearrange("p (c l) -> p c l", c=2 * DC), ginT[0][:].bitcast(f32), ALU.subtract).then_inc(s("gin_low"), 1)

            def gate_argument(j):
                dve.wait_ge(s("gate_mm"), j.i + 1)
                dve.tensor_tensor(zgate[:], misc[:, 0:D], bias_rows[:, 2], ALU.add).then_inc(s("z"), 1)

            def mix(j):
                dve.wait_ge(s("tgate"), j.i + 1)
                dve.wait_ge(s("diff"), j.i + 1)
                then_wait(dve, dve.scalar_tensor_tensor(mixed[:], tgate[:], 1.0, diff[:], ALU.add, ALU.mult), "mixed", j.i + 1)
                dve.wait_ge(s("base"), j.i + 1)
                if not (isinstance(j.i, int) and j.i < 2):
                    dve.wait_ge(s(f"x1_out{j.p}"), 16 * j.half)
                then_wait(dve, dve.scalar_tensor_tensor(x1[j.p][:], mixed[:], thalf[:], base[:], ALU.mult, ALU.add), "x1", j.i + 1)
                then_wait(dve, dve.bn_stats(st1[:], x1[j.p][:]), "st1", j.i + 1)
                dve.sem_inc(s("v_passed"), 1)
                then_wait(dve, dve.bn_aggr(mv1[:], st1[:]), "mv1", j.i + 1)
                dve.tensor_scalar(rs1[:, 0:1], mv1[:, 1:2], LN_EPS, None, ALU.add).then_inc(s("vpe1"), 1)

            def norm_rows(j):
                dve.wait_ge(s("rs1"), j.i + 1)
                if not (isinstance(j.i, int) and j.i < 2):
                    dve.wait_ge(s(f"routed_out{j.p}"), 32 * j.half)
                dve.tensor_scalar(row[j.p][:, 0:D], x1[j.p][:], mv1[:, 0:1], rs1[:, 1:2], ALU.subtract, ALU.mult).then_inc(s("xn2"), 1)

            def logit_maxima(o):
                dve.wait_ge(s("logits"), o.i + 1)
                dve.tensor_reduce(lmax[:, 0:1], obank[:, 0:E], AX.X, ALU.max, negate=True).then_inc(s("lmax"), 1)

            def choose(o):
                n = CHOICE_STEPS * o.i
                dve.wait_ge(s("lexp"), o.i + 1)
                then_wait(dve, dve.reciprocal(psm[:, 1:2], psm[:, 0:1]), "choice_chain", n + 1)
                then_wait(dve, dve.tensor_scalar(prob[:], pe_[:], psm[:, 1:2], None, ALU.mult), "choice_chain", n + 2)
                dve.sem_inc(s("v_passed"), 1)
                then_wait(dve, dve.max(best[:], prob[:]), "choice_chain", n + 3)
                dve.sem_inc(s("v_passed"), 1)
                dve.max_index(besti[:], best[:], prob[:]).then_inc(s("besti"), 1)
                dve.tensor_scalar(wsum[:, 0:1], best[:, 0:1], best[:, 1:2], 1e-9, ALU.add, ALU.add).then_inc(s("choice_chain"), 1)

            def choice_weights(o):
                n = CHOICE_STEPS * o.i
                dve.wait_ge(s("choice_chain"), n + 4)
                dve.reciprocal(wsum[:, 1:2], wsum[:, 0:1]).then_inc(s("choice_chain"), 1)
                dve.wait_ge(s("besti"), o.i + 1)
                dve.tensor_copy(bestf[:, 0:2], besti[:, 0:2]).then_inc(s("choice_chain"), 1)
                wait(dve, s("token"), o.i)
                dve.tensor_copy(row[o.p][:, D + 2:D + 3], token[:])
                dve.tensor_scalar(token[:], token[:], float(P), None, ALU.add).then_inc(s("token"), 1)
                dve.wait_ge(s("choice_chain"), n + 6)
                dve.tensor_scalar(row[o.p][:, D:D + 2], best[:, 0:2], wsum[:, 1:2], tgains[:, 1:2], ALU.mult, ALU.mult)
                for v in range(2):
                    dve.tensor_scalar(oneh[:, v], iota_e[:], bestf[:, v:v + 1], None, ALU.is_equal).then_inc(s("oneh"), 1)

            def b_step(t, cur=True, prev=True, old=True, older=True):
                b, j, o = t.back(1), t.back(2), t.back(3)
                if old:
                    attention_rows(j, "b", 0)
                if cur:
                    maxima(t, 0, "b", CHUNKS_B, C)
                if older:
                    logit_maxima(o)
                if cur:
                    maxima(t, 1, "b", CHUNKS_B, C)
                if older:
                    choose(o)
                if old:
                    gate_low(j)
                if cur:
                    maxima(t, 2, "b", CHUNKS_B, C)
                if older:
                    choice_weights(o)
                if prev:
                    low(b, 0, "b", GROUPS_B)
                if cur:
                    maxima(t, 3, "b", CHUNKS_B, C)
                    softmax_bias(t, "b")
                if old:
                    gate_argument(j)
                if prev:
                    low(b, 1, "b", GROUPS_B)
                if old:
                    mix(j)
                if prev:
                    low(b, 2, "b", GROUPS_B)
                    inverse_sums(b, "b")
                if old:
                    dve.wait_ge(s("tabs"), j.i + 1)
                    dve.tensor_scalar(tdist[:], tdist[:], C / STEP - C // STEP, None, ALU.add).then_inc(s("tdist"), 1)
                    norm_rows(j)
                if prev:
                    low(b, 3, "b", GROUPS_B)
                if older:
                    rank_rows(o)
            dve.wait_ge(s("g_consts"), 1)
            dve.wait_ge(s("tgains"), 1)
            dve.tensor_scalar(thalf[:], tgains[:, 0:1], 0.5, None, ALU.mult).then_inc(s("thalf"), 1)
            dve.wait_ge(s("sub_edge"), 48)
            dve.wait_ge(s("sub_out1"), 16 * ((CTX - 1) // 2))
            dve.wait_ge(s("thalf"), 1)
            tiles(dve, 1, 2, lambda t: b_step(t, old=False, older=False))
            tiles(dve, 2, 3, lambda t: b_step(t, older=False))
            tiles(dve, 3, LT, b_step)
            tiles(dve, LT, LT + 1, lambda t: b_step(t, cur=False))
            tiles(dve, LT + 1, LT + 2, lambda t: b_step(t, cur=False, prev=False))
            tiles(dve, LT + 2, LT + 3, lambda t: b_step(t, cur=False, prev=False, old=False))

            dve.wait_ge(s("b_pv"), LT)
            dve.wait_ge(s("counts"), LT)
            then_wait(dve, dve.tensor_tensor(cfill[:], counts[:, 0], base_e[:, 0], ALU.subtract), "e_chain", 1)
            then_wait(dve, dve.tensor_scalar(cfill[:], cfill[:], float(CAP), None, ALU.min), "e_chain", 2)
            for c in range(CT):
                dve.tensor_scalar(slot[:, :, c], base_e[:, 0], prow[:], float(c * P), ALU.add, ALU.add)
                then_wait(dve, dve.tensor_tensor(first_free[:, :, c], base_e[:, 0], cfill[:], ALU.add), "e_chain", 3 + c)
            then_wait(dve, dve.tensor_tensor(smask[:], slot[:], first_free[:], ALU.is_lt), "e_chain", 3 + CT)
            for c in range(CT):
                then_wait(dve, dve.tensor_scalar(shift[:, :, c], cfill[:], -1.0, float(E * CAP), ALU.mult, ALU.add), "e_chain", 4 + CT + c)
            then_wait(dve, dve.tensor_tensor(slot[:], slot[:], shift[:], ALU.add), "e_chain", 4 + 2 * CT)
            then_wait(dve, dve.tensor_tensor(shift[:], shift[:], smask[:], ALU.mult), "e_chain", 5 + 2 * CT)
            then_wait(dve, dve.tensor_tensor(slot[:], slot[:], shift[:], ALU.subtract), "e_chain", 6 + 2 * CT)

            def places(t):
                if not (isinstance(t.i, int) and t.i < 2):
                    dve.wait_ge(s(f"xg_in{t.p}"), 16 * CT * t.half)
                dve.tensor_copy(gcur[t.p][:], slot[:, bass.ds(t.i, 1)].rearrange("p a c -> p (a c)")).then_inc(s("gcur"), 1)

            def rows_low(t):
                for dc in range(DC):
                    dve.wait_ge(s("xgT_high"), DC * t.i + dc + 1)
                    dve.tensor_tensor(xgT[1][:, dc], bank[4 + dc][:], xgT[0][:, dc].bitcast(f32), ALU.subtract).then_inc(s("xgT_low"), 1)

            def weights_and_tokens(t):
                dve.wait_ge(s(f"xg_in{t.p}"), 16 * CT * (t.half + 1))
                m = smask[:, bass.ds(t.i, 1)].rearrange("p a c -> p (a c)")
                then_wait(dve, dve.tensor_tensor(wd[:], xg[t.p][:, :, D], xg[t.p][:, :, D + 1], ALU.subtract), "wd", 2 * t.i + 1)
                then_wait(dve, dve.tensor_tensor(wd[:], wd[:], m, ALU.mult), "wd", 2 * t.i + 2)
                dve.tensor_tensor(wt[:, t.p], wd[:], xg[t.p][:, :, D + 1], ALU.add)
                if not (isinstance(t.i, int) and t.i < 2):
                    dve.wait_ge(s(f"y_out{t.p}"), 16 * CT * t.half)
                dve.tensor_copy(tok[t.p][:], xg[t.p][:, :, D + 2]).then_inc(s("wt"), 1)

            def output_rows(t, c):
                if c == 0:
                    dve.wait_ge(s("y_mm"), HC * (t.i + 1))
                    dve.wait_ge(s(f"b2_in{t.p}"), 16 * (t.half + 1))
                    if not (isinstance(t.i, int) and t.i == 0):
                        dve.wait_ge(s("yo"), CT * t.i)
                dve.tensor_tensor(yb[:, c], ysum(c), b2r[:, t.p], ALU.add).then_inc(s("yb"), 1)

            def split_hidden(t, hc):
                dve.wait_ge(s("gelu"), HC * t.i + hc + 1)
                if not (isinstance(t.i, int) and t.i == 0 and hc < 2):
                    dve.wait_ge(s("y_mm"), HC * t.i + hc - 1)
                dve.tensor_copy(hs[hc % 2][0][:], hid[hc % 2][:]).then_inc(s("hid_high"), 1)
                dve.wait_ge(s("hid_high"), HC * t.i + hc + 1)
                dve.tensor_tensor(hs[hc % 2][1][:], hid[hc % 2][:], hs[hc % 2][0][:].bitcast(f32), ALU.subtract).then_inc(s("hid_low"), 1)

            def w2_low(t, hc):
                dve.wait_ge(s("w2_high"), HC * (t.i - 1) + hc + 1)
                dve.tensor_tensor(w2s[:, hc, 1], w2_raw[t.p][:, hc], w2s[:, hc, 0].bitcast(f32), ALU.subtract).then_inc(s("w2_split"), 1)

            def expert(t, first=False, last=False):
                if not last:
                    places(t.ahead(1))
                for hc in range(HC):
                    if hc < 2 and not first:
                        output_rows(t.back(1), 2 * hc)
                        output_rows(t.back(1), 2 * hc + 1)
                    split_hidden(t, hc)
                    if hc > 1 and not last:
                        w2_low(t.ahead(1), hc - 2)
                if not last:
                    rows_low(t.ahead(1))
                    weights_and_tokens(t.ahead(1))
                    w2_low(t.ahead(1), HC - 2)
                    w2_low(t.ahead(1), HC - 1)
            places(Tile(0, 0, 0))
            rows_low(Tile(0, 0, 0))
            weights_and_tokens(Tile(0, 0, 0))
            expert(Tile(0, 0, 0), first=True)
            tiles(dve, 1, 2, expert)
            tiles(dve, 2, E - 2, expert)
            expert(Tile(E - 2, E // 2 - 1, 0))
            t = Tile(E - 1, E // 2 - 1, 1)
            expert(t, last=True)
            for c in range(CT):
                output_rows(t, c)

        @block.tensor
        def _(pe):
            def three(dst, lhs, rhs, start, stop):
                pe.matmul(dst, lhs[0], rhs[0], start=start, stop=False)
                pe.matmul(dst, lhs[0], rhs[1], start=False, stop=False)
                return pe.matmul(dst, lhs[1], rhs[0], start=False, stop=stop)

            pe.wait_ge(s("ident"), 1)
            pe.wait_ge(s("weights_in"), 7 * 16)
            for u in range(UNITS):
                for ic in range(DC):
                    for oc in range(DC):
                        raw = w_raw[:, u, oc, ic * P:(ic + 1) * P] if u < 6 else wg_raw[:, oc, ((u - 6) * DC + ic) * P:((u - 6) * DC + ic + 1) * P]
                        m = pe.transpose(bank[u][:, ic * D + oc * P:ic * D + (oc + 1) * P], raw, ident[:])
                m.then_inc(s("wt_T"), 1)
            pe.wait_ge(s("wt_low"), UNITS)
            pe.wait_ge(s("consts_in"), CONSTS * 16)
            pe.transpose(bank[6][:, 0:VECS], vec_rows[:], ident[0:VECS, 0:VECS]).then_inc(s("vec_T"), 1)

            def proj_step(t, ph, cur=True, old=True):
                if cur:
                    if ph == "x":
                        pe.wait_ge(s("tin_norm"), t.i + 1)
                    else:
                        pe.wait_ge(s(f"tin_in{t.p}"), 16 * (t.half + 1))
                        if isinstance(t.i, int) and t.i < 2:
                            pe.wait_ge(s("x_tT_low"), LT)
                    if not (isinstance(t.i, int) and t.i < 2):
                        pe.wait_ge(s(f"{ph}_tT_low"), t.i - 1)
                    for dc in range(DC):
                        m = pe.transpose(bank[t.p][:, dc * P:(dc + 1) * P], tin[t.p][:, dc * P:(dc + 1) * P], ident[:])
                    m.then_inc(s(f"{ph}_T"), 1)
                if old:
                    j = t.back(1)
                    w0 = 0 if ph == "x" else 3
                    kq, v = bank[2 + j.p], bank[4 + j.p]
                    pe.wait_ge(s(f"{ph}_tT_low"), j.i + 1)
                    if isinstance(j.i, int) and j.i < 2:
                        if ph == "c":
                            pe.wait_ge(s("x_low_v"), LT)
                    else:
                        pe.wait_ge(s(f"{ph}_low_v"), j.i - 1)
                    for n, w in enumerate((wT[w0 + 1], wT[w0])):
                        for oc in range(DC):
                            for dc in range(DC):
                                three(kq[:, n * D + oc * P:n * D + (oc + 1) * P],
                                      [w[:, dc, h, oc * P:(oc + 1) * P] for h in range(2)],
                                      [tT[j.p][h][:, dc] for h in range(2)], dc == 0, dc == DC - 1)
                    for dc in range(DC):
                        m = three(v[:, 0:D], [tT[j.p][h][:, dc] for h in range(2)],
                                  [wT[w0 + 2][:, dc, h] for h in range(2)], dc == 0, dc == DC - 1)
                    m.then_inc(s(f"{ph}_mm"), 1)

            def proj(ph, n):
                proj_step(Tile(0, 0, 0), ph, old=False)
                tiles(pe, 1, 3, lambda t: proj_step(t, ph))
                tiles(pe, 3, n - 1, lambda t: proj_step(t, ph))
                proj_step(Tile(n - 1, (n - 1) // 2, (n - 1) % 2), ph)
                proj_step(Tile(n, n // 2, n % 2), ph, cur=False)
            proj("x", LT)
            proj("c", CTX)

            def score(t, c, ph, k, chunks):
                if c == 0:
                    pe.wait_ge(s(f"{ph}_q"), t.i + 1)
                if not (isinstance(t.i, int) and t.i == 0):
                    pe.wait_ge(s(f"{ph}_exp"), 4 * (t.i - 1) + c + 1)
                elif ph == "b":
                    pe.wait_ge(s("a_exp"), 4 * (CTX - 1) + c + 1)
                o, w = chunks[c]
                for dc in range(DC):
                    m = three(scores[c][:, 0:w], [qs[t.p][h][:, dc] for h in range(2)],
                              [k[h][:, dc, o:o + w] for h in range(2)], dc == 0, dc == DC - 1)
                m.then_inc(s(f"{ph}_scores"), 1)

            def transpose_probs(t, g, ph, groups):
                pe.wait_ge(s(f"{ph}_exp"), 4 * t.i + g + 1)
                if not (isinstance(t.i, int) and t.i == 0 and g < 2):
                    pe.wait_ge(s(f"{ph}_low{g % 2}"), 2 * t.i + g // 2)
                elif ph == "b":
                    pe.wait_ge(s(f"a_low{g}"), 2 * CTX)
                if ph == "b" and isinstance(t.i, int) and t.i == 0 and g == 3:
                    pe.wait_ge(s("b_pad"), 2)
                for n, k in enumerate(groups[g]):
                    m = pe.transpose(ptb[g % 2][:, n * P:(n + 1) * P], probs[t.p][:, k * P:(k + 1) * P], ident[:])
                m.then_inc(s(f"{ph}_T{g % 2}"), 1)

            def values(t, g, ph, v, groups):
                pe.wait_ge(s(f"{ph}_low{g % 2}"), 2 * t.i + g // 2 + 1)
                if g == 0 and not (isinstance(t.i, int) and t.i == 0):
                    pe.wait_ge(s(f"{ph}_att"), t.i)
                elif g == 0 and ph == "b":
                    pe.wait_ge(s("a_att"), CTX)
                for k in groups[g]:
                    m = three(obank[:, 0:D], [pt[h][:, k] for h in range(2)],
                              [v[:, k, 0:D], v[:, k, D:2 * D]], k == 0, k == groups[-1][-1])
                if g == 3:
                    m.then_inc(s(f"{ph}_pv"), 1)

            def a_step(t, cur=True, prev=True):
                b = t.back(1)
                if cur:
                    for c in range(3):
                        score(t, c, "a", kchar, CHUNKS_A)
                if prev:
                    transpose_probs(b, 0, "a", GROUPS_A)
                if cur:
                    score(t, 3, "a", kchar, CHUNKS_A)
                if prev:
                    transpose_probs(b, 1, "a", GROUPS_A)
                    values(b, 0, "a", vchar, GROUPS_A)
                    transpose_probs(b, 2, "a", GROUPS_A)
                    values(b, 1, "a", vchar, GROUPS_A)
                    transpose_probs(b, 3, "a", GROUPS_A)
                    values(b, 2, "a", vchar, GROUPS_A)
                    values(b, 3, "a", vchar, GROUPS_A)
            pe.wait_ge(s("c_low_v"), CTX)
            a_step(Tile(0, 0, 0), prev=False)
            tiles(pe, 1, 2, a_step)
            tiles(pe, 2, CTX, a_step)
            last, first = Tile(CTX - 1, (CTX - 1) // 2, (CTX - 1) % 2), Tile(0, 0, 0)
            for c in range(3):
                score(first, c, "b", ksub, CHUNKS_B)
            transpose_probs(last, 0, "a", GROUPS_A)
            score(first, 3, "b", ksub, CHUNKS_B)
            transpose_probs(last, 1, "a", GROUPS_A)
            for g in (2, 3):
                values(last, g - 2, "a", vchar, GROUPS_A)
                transpose_probs(last, g, "a", GROUPS_A)
            for g in (2, 3):
                values(last, g, "a", vchar, GROUPS_A)

            def norm_transposes(o):
                pe.wait_ge(s("xn2"), o.i + 1)
                if isinstance(o.i, int) and o.i == LT - 1:
                    pe.wait_ge(s("b_att"), LT)
                else:
                    pe.wait_ge(s("b_att"), o.i + 2)
                for dc in range(DC):
                    m = pe.transpose(obank[:, dc * P:(dc + 1) * P], row[o.p][:, dc * P:(dc + 1) * P], ident[:])
                m.then_inc(s("xn2_T"), 1)

            def logit_products(o):
                pe.wait_ge(s("xn2T"), o.i + 1)
                for dc in range(DC):
                    m = pe.matmul(obank[:, 0:E], xn2T[:, dc], wroute[:, dc], start=dc == 0, stop=dc == DC - 1)
                m.then_inc(s("logits"), 1)

            def interpolate(j):
                pe.wait_ge(s("tent"), j.i + 1)
                pe.wait_ge(s("subwin_in"), 16 * (j.i + 1))
                if not (isinstance(j.i, int) and j.i < 2):
                    pe.wait_ge(s("counts"), j.i - 1)
                elif isinstance(j.i, int) and j.i == 1:
                    pe.wait_ge(s("z"), 1)
                pe.matmul(misc[:, 0:D], tent[:], subwin[:], start=True, stop=True).then_inc(s("interp"), 1)

            def gate_transposes(j):
                pe.wait_ge(s("b_att"), j.i + 1)
                pe.wait_ge(s("sub"), j.i + 1)
                for n, part in enumerate((att[j.p], sub)):
                    for dc in range(DC):
                        m = pe.transpose(misc[:, (n * DC + dc) * P:(n * DC + dc + 1) * P], part[:, dc * P:(dc + 1) * P], ident[:])
                m.then_inc(s("gate_T"), 1)

            def gate_products(j):
                pe.wait_ge(s("gin_low"), j.i + 1)
                for k in range(2 * DC):
                    m = three(misc[:, 0:D], [ginT[h][:, k] for h in range(2)], [wgT[:, k, h] for h in range(2)], k == 0, k == 2 * DC - 1)
                m.then_inc(s("gate_mm"), 1)

            def rank_products(o):
                pe.wait_ge(s("oneh"), 2 * (o.i + 1))
                if isinstance(o.i, int) and o.i == LT - 1:
                    pe.wait_ge(s("counts"), LT - 1)
                else:
                    pe.wait_ge(s("z"), o.i + 2)
                pe.matmul(misc[:, 0:2 * E], before[:], oneh[:].rearrange("p v e -> p (v e)"), start=True, stop=True)
                pe.matmul(misc[:, 2 * E:4 * E], ones[:], oneh[:].rearrange("p v e -> p (v e)"), start=True, stop=True).then_inc(s("rank_mm"), 1)

            def b_step(t, cur=True, prev=True, old=True, older=True):
                b, j, o = t.back(1), t.back(2), t.back(3)
                if old:
                    interpolate(j)
                if cur:
                    score(t, 0, "b", ksub, CHUNKS_B)
                if older:
                    norm_transposes(o)
                if cur:
                    score(t, 1, "b", ksub, CHUNKS_B)
                if older:
                    logit_products(o)
                if old:
                    gate_transposes(j)
                if cur:
                    score(t, 2, "b", ksub, CHUNKS_B)
                if prev:
                    transpose_probs(b, 0, "b", GROUPS_B)
                if cur:
                    score(t, 3, "b", ksub, CHUNKS_B)
                if old:
                    gate_products(j)
                if prev:
                    transpose_probs(b, 1, "b", GROUPS_B)
                    if older:
                        pe.wait_ge(s("lexp"), o.i + 1)
                    values(b, 0, "b", vsub, GROUPS_B)
                    transpose_probs(b, 2, "b", GROUPS_B)
                    values(b, 1, "b", vsub, GROUPS_B)
                    transpose_probs(b, 3, "b", GROUPS_B)
                if older:
                    rank_products(o)
                if prev:
                    values(b, 2, "b", vsub, GROUPS_B)
                    values(b, 3, "b", vsub, GROUPS_B)
            tiles(pe, 1, 2, lambda t: b_step(t, old=False, older=False))
            tiles(pe, 2, 3, lambda t: b_step(t, older=False))
            tiles(pe, 3, LT, b_step)
            tiles(pe, LT, LT + 1, lambda t: b_step(t, cur=False))
            tiles(pe, LT + 1, LT + 2, lambda t: b_step(t, cur=False, prev=False))
            tiles(pe, LT + 2, LT + 3, lambda t: b_step(t, cur=False, prev=False, old=False))

            def transpose_rows(t):
                pe.wait_ge(s(f"xg_in{t.p}"), 16 * CT * (t.half + 1))
                if not (isinstance(t.i, int) and t.i == 0):
                    pe.wait_ge(s("xgT_low"), DC * t.i)
                for dc in range(DC):
                    for c in range(CT):
                        m = pe.transpose(bank[4 + dc][:, c * P:(c + 1) * P], xg[t.p][:, c, dc * P:(dc + 1) * P], ident[:])
                    m.then_inc(s("xg_T"), 1)

            def hidden(t, hc):
                if hc == 0:
                    pe.wait_ge(s("xgT_low"), DC * (t.i + 1))
                pe.wait_ge(s("w1_split"), HC * t.i + hc + 1)
                if not (isinstance(t.i, int) and t.i == 0 and hc < 2):
                    pe.wait_ge(s("gelu"), HC * t.i + hc - 1)
                for dc in range(DC):
                    m = three(bank[6 + hc % 2][:], [w1s[h][:, dc, hc * P:(hc + 1) * P] for h in range(2)],
                              [xgT[h][:, dc] for h in range(2)], dc == 0, dc == DC - 1)
                m.then_inc(s("h_mm"), 1)

            def outputs(t, hc):
                if isinstance(t.i, int) and t.i == 0:
                    pe.wait_ge(s("w2_first"), hc + 1)
                else:
                    pe.wait_ge(s("w2_split"), HC * (t.i - 1) + hc + 1)
                pe.wait_ge(s("hid_low"), HC * t.i + hc + 1)
                for c in range(CT):
                    if hc == 0 and not (isinstance(t.i, int) and t.i == 0):
                        pe.wait_ge(s("yb"), CT * (t.i - 1) + c + 1)
                    h = hs[hc % 2]
                    m = three(ysum(c), [h[n][:, c * P:(c + 1) * P] for n in range(2)],
                              [w2s[:, hc, n] for n in range(2)], hc == 0, hc == HC - 1)
                m.then_inc(s("y_mm"), 1)

            def expert(t, last=False):
                hidden(t, 0)
                for hc in range(1, HC):
                    hidden(t, hc)
                    if hc == HC - 1 and not last:
                        transpose_rows(t.ahead(1))
                    outputs(t, hc - 1)
                outputs(t, HC - 1)
            pe.wait_ge(s("counts"), LT)
            transpose_rows(Tile(0, 0, 0))
            expert(Tile(0, 0, 0))
            tiles(pe, 1, 2, expert)
            tiles(pe, 2, E - 2, expert)
            expert(Tile(E - 2, E // 2 - 1, 0))
            expert(Tile(E - 1, E // 2 - 1, 1), last=True)


_INS = ['x', 'ctx_1024', 'g_xattn', 'g_ffn', 'L0_xattn_Wq_c', 'L0_xattn_bq_c', 'L0_xattn_Wk_s', 'L0_xattn_bk_s',
        'L0_xattn_Wv_s', 'L0_xattn_bv_s', 'L0_xattn_Wq_s', 'L0_xattn_bq_s', 'L0_xattn_Wk_c', 'L0_xattn_bk_c',
        'L0_xattn_Wv_c', 'L0_xattn_bv_c', 'L0_xattn_Wg', 'L0_xattn_bg', 'L0_ffn_Wg', 'L0_ffn_W1', 'L0_ffn_b1',
        'L0_ffn_W2', 'L0_ffn_b2']


def kernel(**inputs):
    import numpy as _np
    import concourse.bacc as _bacc
    from concourse import mybir as _mybir
    from concourse.bass_utils import run_bass_kernel_spmd as _run

    nc = _bacc.Bacc("TRN2", target_bir_lowering=False, num_devices=1)
    arrays, args = {}, []
    for name in _INS:
        a = _np.ascontiguousarray(inputs[name])
        arrays[f"in_{name}_dram"] = a
        args.append(nc.dram_tensor(f"in_{name}_dram", a.shape, _mybir.dt.from_np(a.dtype), kind="ExternalInput").ap())
    out = nc.dram_tensor("out_0_dram", (1, L, D), _mybir.dt.float32, kind="ExternalOutput").ap()
    program(nc, *args, out)
    r = _run(nc, [arrays], core_ids=[0])
    return r.results[0]["out_0_dram"]
```

```python
import concourse.bass as bass
from concourse import mybir
from contextlib import ExitStack

P = 128
D = 256
DC = D // P
E = 8
HID = 1024
HC = HID // P
CAP = 512
CT = CAP // P
L = 2048
LT = L // P
C = 1601
CTX = -(-C // P)
CREM = C - (CTX - 1) * P
XPAIRS, CPAIRS = LT // 2, -(-CTX // 2)
CKEYS = C + 1
BANK = 512
ROW = D + 3
SKIP = 1 << 20
SCALE = 1.0 / 16
STEP = L // P
LN_EPS = 1e-5


class Tile:

    def __init__(self, i, half, p):
        self.i, self.half, self.p = i, half, p

    def ahead(self, d):
        p = (self.p + d) % 2
        return Tile(self.i + d, self.half + (self.p + d - p) // 2, p)

    def back(self, d):
        p = (self.p - d) % 2
        return Tile(self.i - d, self.half - (d + p - self.p) // 2, p)


def tiles(eng, first, last, body):
    i = first
    if i % 2:
        body(Tile(i, i // 2, 1))
        i += 1
    pairs = (last - i) // 2
    if pairs >= 2:
        with eng.Fori(i // 2, i // 2 + pairs) as half:
            body(Tile(half * 2, half, 0))
            body(Tile(half * 2 + 1, half, 1))
        i += 2 * pairs
    while i < last:
        body(Tile(i, i // 2, i % 2))
        i += 1


def wait(eng, sem, count):
    if isinstance(count, int) and count <= 0:
        return
    eng.wait_ge(sem, count)


def program(nc, x, ctx_in, g_xattn, g_ffn, Wq_c, bq_c, Wk_s, bk_s, Wv_s, bv_s, Wq_s, bq_s, Wk_c, bk_c,
            Wv_c, bv_c, Wgate, bgate, Wroute, W1, b1, W2, b2, out):
    f32, f32r = mybir.dt.float32, mybir.dt.float32r
    i32, u32 = mybir.dt.int32, mybir.dt.uint32
    ALU, ACT, AX = mybir.AluOpType, mybir.ActivationFunctionType, mybir.AxisListType
    stack = ExitStack()
    with stack:
        top = [(nc.sbuf_base + 63) // 64 * 64]

        def size(shape):
            n = 4
            for v in shape[1:]:
                n *= v
            return (n + 31) // 32 * 32

        def at(name, offset, shape, dt=f32):
            return nc.alloc_sbuf_tensor_at(name, shape, dt, offset=offset)

        def region(n):
            top[0] += n
            assert top[0] <= nc.sbuf_usable_end, top[0]
            return top[0] - n

        def sb(name, shape, dt=f32):
            return at(name, region(size(shape)), shape, dt)

        def inside(start, end):
            used = [start]

            def place(name, shape, dt=f32):
                used[0] += size(shape)
                assert used[0] <= end, (name, used[0] - end)
                return at(name, used[0] - size(shape), shape, dt)
            return place

        def sem(name):
            return stack.enter_context(nc.semaphore(name))

        r_kchar = region(2 * DC * L * 4)
        kchar = [at(f"kchar_{s}", r_kchar + n * DC * L * 4, [P, DC, L], f32r) for n, s in enumerate(("high", "low"))]
        r_vchar = region(LT * 2 * D * 4)
        vchar = at("vchar", r_vchar, [P, LT, 2 * D], f32r)
        r_ksub = region(2 * DC * CTX * P * 4)
        ksub = [at(f"ksub_{s}", r_ksub + n * DC * CTX * P * 4, [P, DC, CTX * P], f32r) for n, s in enumerate(("high", "low"))]
        r_vsub = region(CTX * 2 * D * 4)
        vsub = at("vsub", r_vsub, [P, CTX, 2 * D], f32r)
        r_qchar = region(LT * D * 4)
        qchar = at("qchar", r_qchar, [P, LT, DC, P], f32)
        r_qsub = region(CTX * D * 4)
        qsub = at("qsub", r_qsub, [P, CTX, DC, P], f32)

        r_work = region(2 * L * 4 + 2 * LT * P * 4)
        probs = [at(f"probs{p}", r_work + p * L * 4, [P, L], f32) for p in range(2)]
        r_pt = r_work + 2 * L * 4
        pt = [at(f"probsT_{s}", r_pt + n * LT * P * 4, [P, LT, P], f32r) for n, s in enumerate(("high", "low"))]
        wT = [at(f"wT_{n}", r_work + n * DC * 2 * D * 4, [P, DC, 2, D], f32r) for n in range(6)]
        o = r_work + 6 * DC * 2 * D * 4
        tT = [[at(f"tT_{s}{p}", o + (2 * p + n) * 2 * D * 4, [P, DC, 2 * P], f32r) for n, s in enumerate(("high", "low"))] for p in range(2)]
        assert o + 8 * D * 4 <= r_work + 2 * L * 4 + 2 * LT * P * 4
        r_xres = region(2 * D * 4)
        tin = [sb("tin0", [P, 2, D]), at("tin1", r_xres, [P, 2, D])]
        x_all = at("x_all", r_vsub, [P, LT, D], f32)
        w_raw = at("w_raw", r_ksub, [P, 6, DC, D], f32)
        wg_raw = at("wg_raw", r_ksub + 6 * DC * D * 4, [P, DC, 2 * D], f32)

        wgT = sb("wgT", [P, 2 * DC, 2, D], f32r)
        ident = sb("ident", [P, P])
        before, every = sb("before", [P, P], f32r), sb("every", [P, P], f32r)
        upper = at("upper", r_vchar + 2048, [P, P])
        ones = at("ones", r_vchar + 1024 + 512, [P, P])
        one = sb("one", [P, 1])
        tent = sb("tent", [P, P])
        tdist = sb("tdist", [P, P])
        tabs = sb("tabs", [P, P])
        tidx = at("tidx", r_vchar, [P, P], i32)
        VECS = E * HC + 4 * DC
        vec_rows = at("vec_rows", r_qsub + 1024, [VECS, P])
        vec_cols = sb("vec_cols", [P, VECS])
        b1c = vec_cols[:, 0:E * HC].rearrange("p (e c) -> p e c", c=HC)
        bias_cols = vec_cols[:, E * HC:VECS].rearrange("p (n c) -> p n c", c=DC)
        bias_rows = sb("bias_rows", [P, 3, D])
        gains = sb("gains", [P, 2])
        tgains = sb("tgains", [P, 2])
        thalf = sb("thalf", [P, 1])
        mhalf = sb("mhalf", [P, LT])
        iota_e = sb("iota_e", [P, E])
        base_e = sb("base_e", [P, 2, E])
        full_e = sb("full_e", [P, 2, E])
        ie = sb("ie", [P, 2 * E], i32)
        slot_i = at("slot_i", r_vchar + 1024, [P, E, CT], i32)
        wroute = sb("wroute", [P, DC, E])
        token = sb("token", [P, 1])
        tok_i = sb("tok_i", [P, 1], i32)
        ztok = sb("ztok", [P, CT], i32)
        stats = at("stats", r_qsub, [P, 2, 2, 6])
        mv = at("mv", r_qsub + 96, [P, 2, 2, 2])
        rstd = at("rstd", r_qsub + 128, [P, 2, 2])
        vpe = at("vpe", r_qsub + 160, [P, 2, 2])

        qs = [[sb(f"q_{s}{p}", [P, DC, P], f32r) for s in ("high", "low")] for p in range(2)]
        mx = sb("mx", [P, 2, 4])
        nmx = sb("nmx", [P, 2])
        nbias = sb("nbias", [P, 2])
        esum = sb("esum", [P, 2, 4])
        zsum = sb("zsum", [P, 1])
        rz = sb("rz", [P, 2])
        att = [sb(f"att{p}", [P, D]) for p in range(2)]

        in_qsub = inside(r_qsub, r_work)
        xres = [at(f"xres{p}", r_xres + p * D * 4, [P, D]) for p in range(2)]
        r_late = region(2 * size([P, ROW]) + 2 * size([P, D]))
        place = inside(r_late, top[0])
        zrow = at("zrow", r_late, [P, CT, ROW])
        assert size([P, CT * ROW]) <= top[0] - r_late
        subwin = place("subwin", [P, D])
        sub = in_qsub("sub", [P, D])
        ginT = [in_qsub(f"ginT_{s}", [P, 2 * DC, P], f32r) for s in ("high", "low")]
        zgate = in_qsub("zgate", [P, D])
        tgate = in_qsub("tgate", [P, D])
        diff = in_qsub("diff", [P, D])
        mixed = in_qsub("mixed", [P, D])
        subt = in_qsub("subt", [P, D])
        base = in_qsub("base", [P, D])
        x1 = [in_qsub(f"x1_{p}", [P, D]) for p in range(2)]
        row = [place(f"row{p}", [P, ROW]) for p in range(2)]
        st1 = sb("st1", [P, 6])
        mv1 = sb("mv1", [P, 2])
        rs1 = sb("rs1", [P, 2])
        xn2T = place("xn2T", [P, DC, P])
        lmax = sb("lmax", [P, 2])
        pe_ = sb("pe_", [P, E])
        psm = sb("psm", [P, 2])
        prob = sb("prob", [P, E])
        best = sb("best", [P, 8])
        besti = sb("besti", [P, 8], u32)
        bestf = sb("bestf", [P, 8])
        wsum = sb("wsum", [P, 2])
        oneh = sb("oneh", [P, 2, E], f32r)
        slot0 = sb("slot0", [P, E, CT])
        counts = sb("counts", [P, 2, E])
        rank = sb("rank", [P, 2, E])
        over = sb("over", [P, 2, E])
        slotf = sb("slotf", [P, 2])
        sloti = [sb(f"sloti{p}", [P, 2], u32) for p in range(2)]

        place = inside(r_kchar, r_ksub)
        w1_raw = [place(f"w1_raw{p}", [P, DC, HID]) for p in range(2)]
        w2_raw = [place(f"w2_raw{p}", [P, HC, D]) for p in range(2)]
        w1s = [place(f"w1_{h}", [P, DC, HID], f32r) for h in ("high", "low")]
        w2s = place("w2s", [P, HC, 2, D], f32r)
        place = inside(r_ksub, r_qchar)
        b2r = place("b2r", [P, 2, D])
        xg = [place(f"xg{p}", [P, CT, ROW]) for p in range(2)]
        xgT = [[place(f"xgT_{h}{p}", [P, DC, CAP], f32r) for h in ("high", "low")] for p in range(2)]
        hid = [place(f"hid{p}", [P, CAP]) for p in range(2)]
        hs = [[place(f"hid_{h}{p}", [P, CAP], f32r) for h in ("high", "low")] for p in range(2)]
        wt = place("wt", [P, 2, CT])
        wd = place("wd", [P, CT])
        tok = [place(f"tok{p}", [P, CT], u32) for p in range(2)]
        gcur = [place(f"gcur{p}", [P, CT], u32) for p in range(2)]
        yb = place("yb", [P, CT, D])
        yo = place("yo", [P, CT, D])
        slot = place("slot", [P, E, CT])
        first_free = place("first_free", [P, E])
        second = place("second", [P, E, CT])
        shift = place("shift", [P, E])

        sub_rows = nc.dram_tensor("sub_rows", [CTX * P + 1, D], f32, kind="Internal").ap()
        routed = nc.dram_tensor("routed", [2 * E * CAP, ROW], f32, kind="Internal").ap()

        bank = [stack.enter_context(nc.psum_tensor(f"bank{b}", [P, BANK], f32)) for b in range(8)]
        scores, ptb, obank, misc = bank[0:4], bank[4:6], bank[6], bank[7]

        names = {}

        def s(name):
            if name not in names:
                names[name] = sem(name)
            return names[name]

        def then_wait(eng, ins, name, count):
            ins.then_inc(s(name), 1)
            eng.wait_ge(s(name), count)

        RANK_STEPS, CHOICE_STEPS, NORM_STEPS = 5, 6, 2

        xv = x[0].rearrange("(t p) d -> p t d", p=P)
        ov = out[0]
        block = stack.enter_context(nc.Block())

        W6 = (Wq_c, Wk_c, Wv_c, Wq_s, Wk_s, Wv_s)
        XFIRST = 4
        UNITS = 8
        VEC_LOADS, CONSTS = 5, 6

        def unit_bank(u):
            return bank[(u + 4) % 8]

        def unit_in(u):
            return unit_bank(u)[:].rearrange("p (c o) -> p c o", c=DC)

        def unit_out(u, part):
            return wT[u][:, :, part] if u < 6 else wgT[:, (u - 6) * DC:(u - 5) * DC, part]

        T_BANK, K_BANK, Q_BANK, V_BANK = ((bank[4 + n], bank[n]) for n in range(4))

        def pairs(eng, body):
            def pair(ph, u):
                return ph, u, 1 if ph == "c" and isinstance(u.i, int) and u.i == CPAIRS - 1 else 2
            def steps(ph, first, last):
                tiles(eng, first, last, lambda u: body(pair(ph, u), pair(ph, u.back(1))))
            body(pair("x", Tile(0, 0, 0)), None)
            steps("x", 1, 2)
            steps("x", 2, XPAIRS - 2)
            steps("x", XPAIRS - 2, XPAIRS - 1)
            steps("x", XPAIRS - 1, XPAIRS)
            x_last = pair("x", Tile(XPAIRS - 1, (XPAIRS - 1) // 2, (XPAIRS - 1) % 2))
            body(pair("c", Tile(0, 0, 0)), x_last)
            steps("c", 1, 3)
            steps("c", 3, CPAIRS - 1)
            steps("c", CPAIRS - 1, CPAIRS)
            body(None, pair("c", Tile(CPAIRS - 1, (CPAIRS - 1) // 2, (CPAIRS - 1) % 2)))

        def wait_pair_of_two_before(eng, name, ph, u):
            if not (isinstance(u.i, int) and u.i < 2):
                eng.wait_ge(s(f"{ph}_{name}"), u.i - 1)
            elif ph == "c":
                eng.wait_ge(s(f"x_{name}"), XPAIRS - 1 + u.i)

        GROUPS_A = [range(4 * g, 4 * g + 4) for g in range(4)]
        GROUPS_B = [range(3 * g, 3 * g + 3) for g in range(3)] + [range(9, CTX)]
        CHUNKS_A = [(BANK * c, BANK) for c in range(4)]
        SLICE = CKEYS // 4 // 2 * 2
        CHUNKS_B = [(0, CKEYS - 3 * SLICE)] + [(CKEYS - (4 - c) * SLICE, SLICE) for c in (1, 2, 3)]

        AHEAD = HC - 2

        def ysum(c):
            return bank[c][:, 0:D]

        def row_bcast(v):
            return v.rearrange("(a n) -> a n", a=1).broadcast_to([P, v.shape[0]])

        @block.sync
        def _(sp):
            def load_weights(n):
                sp.dma_start(w_raw[:, n], W6[n].rearrange("(c p) i -> p c i", p=P)).then_inc(s(f"weight_in{n}"), 16)
            for n in range(6):
                load_weights(n)
            sp.dma_start(wg_raw[:], Wgate.rearrange("(c p) i -> p c i", p=P)).then_inc(s("weight_in6"), 16)
            for n, b in enumerate((bq_c, bk_c, bq_s, bk_s)):
                sp.dma_start(vec_rows[E * HC + n * DC:E * HC + (n + 1) * DC], b.rearrange("(c p) -> c p", p=P)).then_inc(s("vecs_in"), 16)
            sp.dma_start(vec_rows[0:E * HC], b1.rearrange("e (c p) -> (e c) p", p=P)).then_inc(s("vecs_in"), 16)
            sp.dma_start(x_all[:, XFIRST:LT], xv[:, XFIRST:LT]).then_inc(s("x_rest"), 16)
            for n, b in enumerate((bv_s, bv_c, bgate)):
                sp.dma_start(bias_rows[:, n], row_bcast(b)).then_inc(s("consts_in"), 16)
            for n, g in enumerate((g_xattn, g_ffn)):
                sp.dma_start(gains[:, n:n + 1], row_bcast(g)).then_inc(s("consts_in"), 16)
            sp.dma_start(wroute[:], Wroute.rearrange("(c p) e -> p c e", p=P)).then_inc(s("consts_in"), 16)
            sp.wait_ge(s("zrow"), 1)
            for e in range(2 * E):
                sp.dma_start(routed[e * CAP:(e + 1) * CAP].rearrange("(p r) n -> p r n", p=P), zrow[:]).then_inc(s("empty_in"), 16)

            def store_sub(t):
                sp.wait_ge(s("a_att"), t.i + 1)
                sp.dma_start(sub_rows[bass.ds(t.i * P + 1, P)], att[t.p][:]).then_inc(s(f"sub_out{t.p}"), 16)
            store_sub(Tile(0, 0, 0))
            sp.dma_start(sub_rows[0:1], att[0][0:1]).then_inc(s("sub_first"), 16)
            tiles(sp, 1, CTX - 1, store_sub)
            last = (CTX - 1) % 2
            sp.wait_ge(s("a_att"), CTX)
            sp.dma_start(sub_rows[(CTX - 1) * P + 1:C + 1], att[last][0:CREM]).then_inc(s("sub_edge"), 16)
            sp.dma_start(sub_rows[C + 1:C + 2], att[last][CREM - 1:CREM]).then_inc(s("sub_edge"), 16)
            sp.dma_start(sub_rows[C + 2:CTX * P + 1], att[last][CREM + 1:P]).then_inc(s("sub_edge"), 16)

            for name in ("sub_first", "sub_edge"):
                sp.wait_ge(s(name), 16 if name == "sub_first" else 48)
            sp.wait_ge(s("sub_out0"), 16 * ((CTX - 1) // 2))
            sp.wait_ge(s("sub_out1"), 16 * ((CTX - 1) // 2))

            def load_tile(t):
                wait(sp, s("base"), t.i - 1)
                sp.dma_start(xres[t.p][:], x[0, bass.ds(t.i * P, P)]).then_inc(s(f"xres_in{t.p}"), 16)
                wait(sp, s("interp"), t.i)
                sp.dma_start(subwin[:], sub_rows[bass.ds(t.i * (C // STEP), P)]).then_inc(s("subwin_in"), 16)
            sp.wait_ge(s("empty_in"), 16 * 2 * E)
            load_tile(Tile(0, 0, 0))
            sp.wait_ge(s("a_pv"), CTX)
            sp.dma_start(w1_raw[0][:], W1[0].rearrange("(c p) h -> p c h", p=P)).then_inc(s("w_in0"), 16)
            sp.dma_start(w2_raw[0][:], W2[0].rearrange("(c p) d -> p c d", p=P)).then_inc(s("w_in0"), 16)
            sp.dma_start(w1_raw[1][:], W1[1].rearrange("(c p) h -> p c h", p=P)).then_inc(s("w_in1"), 16)
            sp.dma_start(w2_raw[1][:], W2[1].rearrange("(c p) d -> p c d", p=P)).then_inc(s("w_in1"), 16)
            load_tile(Tile(1, 0, 1))
            tiles(sp, 2, LT, load_tile)

            def load_bias(t):
                wait(sp, s("yb"), CT * (t.i - 1))
                sp.dma_start(b2r[:, t.p], b2[bass.ds(t.i, 1)].broadcast_to([P, D])).then_inc(s(f"b2_in{t.p}"), 16)

            def load_expert(t):
                sp.wait_ge(s("w1_split"), (t.i - 1) * HC)
                wait(sp, s("w2_split"), (t.i - 2) * HC)
                sp.dma_start(w1_raw[t.p][:], W1[bass.ds(t.i, 1)].rearrange("a (c p) h -> p (a c) h", p=P)).then_inc(s(f"w_in{t.p}"), 16)
                sp.dma_start(w2_raw[t.p][:], W2[bass.ds(t.i, 1)].rearrange("a (c p) d -> p (a c) d", p=P)).then_inc(s(f"w_in{t.p}"), 16)
                load_bias(t)
            sp.wait_ge(s("b_pv"), LT)
            load_bias(Tile(0, 0, 0))
            load_bias(Tile(1, 0, 1))
            sp.wait_ge(s("xg_in0"), 16 * CT)
            tiles(sp, 2, 3, load_expert)
            tiles(sp, 3, E, load_expert)

            for p in range(2):
                sp.wait_ge(s(f"y_out{p}"), 16 * CT * E // 2)

        @block.gpsimd
        def _(gp):
            def apart(name, count):
                gp.wait_ge(s(name), count)
                gp.sem_inc(s("g_passed"), 1)

            gp.memset(ident[:], 0.0)
            gp.memset(zrow[:], 0.0)
            gp.memset(one[:], 1.0)
            gp.memset(ones[:], 1.0).then_inc(s("g_fill"), 1)
            gp.wait_ge(s("g_fill"), 1)
            gp.affine_select(out=ident[:], in_=ident[:], compare_op=ALU.not_equal, fill=1.0, base=0,
                             pattern=[[-1, P]], channel_multiplier=1)
            gp.affine_select(out=upper[:], in_=ones[:], compare_op=ALU.is_gt, fill=0.0, base=0,
                             pattern=[[1, P]], channel_multiplier=-1).then_inc(s("ident"), 1)
            gp.memset(mhalf[:], -0.5)
            gp.iota(ztok[:], pattern=[[1, CT]], base=L, channel_multiplier=CT)
            gp.iota(tidx[:], pattern=[[2 * C, P]], base=C + L, channel_multiplier=-2 * L)
            gp.iota(ie[:, 0:E], pattern=[[1, E]], base=0, channel_multiplier=0)
            gp.iota(ie[:, E:2 * E], pattern=[[CAP, E]], base=0, channel_multiplier=0)
            gp.iota(slot_i[:], pattern=[[CAP, E], [P, CT]], base=0, channel_multiplier=1)
            gp.iota(tok_i[:], pattern=[[0, 1]], base=0, channel_multiplier=1).then_inc(s("g_iota"), 1)
            gp.wait_ge(s("g_iota"), 1)
            gp.tensor_copy(zrow[:, :, ROW - 1], ztok[:]).then_inc(s("zrow"), 1)
            for v in (0, 1):
                gp.tensor_scalar(base_e[:, v], ie[:, E:2 * E], float(v * E * CAP), None, ALU.add)
                gp.tensor_scalar(full_e[:, v], ie[:, E:2 * E], float(v * E * CAP + CAP), None, ALU.add)
                gp.tensor_scalar(counts[:, v], ie[:, E:2 * E], float(v * E * CAP), None, ALU.add)
            gp.tensor_copy(iota_e[:], ie[:, 0:E])
            gp.tensor_copy(slot0[:], slot_i[:])
            gp.tensor_copy(every[:], ones[:])
            gp.wait_ge(s("ident"), 1)
            gp.tensor_copy(before[:], upper[:])
            gp.tensor_copy(token[:], tok_i[:])
            gp.tensor_scalar(tdist[:], tidx[:], 1.0 / (2 * L), None, ALU.mult).then_inc(s("g_consts"), 1)
            def deviations(u):
                gp.wait_ge(s("vpe"), u.i + 1)
                gp.tensor_tensor(rstd[:, u.p], vpe[:, u.p], mhalf[:, 0:2], ALU.pow).then_inc(s("rstd"), 1)
            tiles(gp, 0, XPAIRS, deviations)

            def split_queries(src, t, ph):
                q = src[:, bass.ds(t.i, 1)].rearrange("p a c l -> p (a c) l")
                if not (isinstance(t.i, int) and t.i < 2):
                    apart(f"{ph}_scores", 4 * (t.i - 1))
                gp.tensor_copy(qs[t.p][0][:], q).then_inc(s(f"{ph}_qh"), 1)
                apart(f"{ph}_qh", t.i + 1)
                gp.tensor_tensor(qs[t.p][1][:], q, qs[t.p][0][:].bitcast(f32), ALU.subtract).then_inc(s(f"{ph}_q"), 1)

            gp.wait_ge(s("c_high_kqv"), 1)
            gp.wait_ge(s("x_high_kqv"), XPAIRS)
            split_queries(qsub, Tile(0, 0, 0), "a")
            split_queries(qsub, Tile(1, 0, 1), "a")
            gp.wait_ge(s("c_high_kqv"), CPAIRS)
            tiles(gp, 2, CTX, lambda t: split_queries(qsub, t, "a"))

            def residual_parts(j):
                gp.wait_ge(s("b_att"), j.i + 1)
                gp.wait_ge(s("sub"), j.i + 1)
                if not (isinstance(j.i, int) and j.i < 1):
                    gp.wait_ge(s("x1"), j.i)
                gp.tensor_tensor(diff[:], att[j.p][:], sub[:], ALU.subtract).then_inc(s("diff"), 1)
                gp.wait_ge(s(f"xres_in{j.p}"), 16 * (j.half + 1))
                gp.wait_ge(s("subt"), j.i + 1)
                gp.tensor_tensor(base[:], subt[:], xres[j.p][:], ALU.add).then_inc(s("base"), 1)

            def inverse_deviation(j):
                gp.wait_ge(s("vpe1"), j.i + 1)
                gp.tensor_tensor(rs1[:, 1:2], rs1[:, 0:1], mhalf[:, 0:1], ALU.pow).then_inc(s("rs1"), 1)

            def route(j):
                apart("slots", j.i + 1)
                for v in range(2):
                    gp.indirect_dma_start(out=routed, out_offset=bass.IndirectOffsetOnAxis(ap=sloti[j.p][:, v:v + 1], axis=0),
                                          in_=row[j.p][:], in_offset=None,
                                          bounds_check=2 * E * CAP - 1, oob_is_err=False).then_inc(s(f"routed_out{j.p}"), 16)

            def b_step(t, cur=True, old=True, older=True, weights=False):
                if cur:
                    split_queries(qchar, t.ahead(1), "b")
                if old:
                    residual_parts(t.back(2))
                if weights:
                    split_first_weights(t.i - 4)
                if old:
                    inverse_deviation(t.back(2))
                if older:
                    route(t.back(3))

            def split_first_weights(hc):
                cols, chunk = bass.ds(hc * P, P), bass.ds(hc, 1)
                gp.tensor_copy(w1s[0][:, :, cols], w1_raw[0][:, :, cols])
                gp.tensor_copy(w2s[:, chunk, 0], w2_raw[0][:, chunk]).then_inc(s("w_first_high"), 1)
                gp.wait_ge(s("w_first_high"), hc + 1)
                gp.tensor_tensor(w2s[:, chunk, 1], w2_raw[0][:, chunk], w2s[:, chunk, 0].bitcast(f32), ALU.subtract).then_inc(s("w2_first"), 1)
                gp.tensor_tensor(w1s[1][:, :, cols], w1_raw[0][:, :, cols], w1s[0][:, :, cols].bitcast(f32), ALU.subtract).then_inc(s("w1_split"), 1)

            def w1_low(t, hc):
                cols = slice(hc * P, hc * P + P)
                gp.wait_ge(s("w1_high"), HC * (t.i - 1) + hc + 1)
                gp.tensor_tensor(w1s[1][:, :, cols], w1_raw[t.p][:, :, cols], w1s[0][:, :, cols].bitcast(f32), ALU.subtract).then_inc(s("w1_split"), 1)

            gp.wait_ge(s("a_scores"), 4 * CTX)
            split_queries(qchar, Tile(0, 0, 0), "b")
            tiles(gp, 0, 2, lambda t: b_step(t, old=False, older=False))
            tiles(gp, 2, 3, lambda t: b_step(t, older=False))
            gp.wait_ge(s("empty_in"), 16 * 2 * E)
            tiles(gp, 3, 4, b_step)
            apart("w_in0", 32)
            tiles(gp, 4, 4 + HC, lambda t: b_step(t, weights=True))
            tiles(gp, 4 + HC, LT - 1, b_step)
            tiles(gp, LT - 1, LT + 2, lambda t: b_step(t, cur=False))
            tiles(gp, LT + 2, LT + 3, lambda t: b_step(t, cur=False, old=False))

            def gather(t):
                apart("gcur", t.i + 1)
                for c in range(CT):
                    gp.indirect_dma_start(out=xg[t.p][:, c], out_offset=None, in_=routed,
                                          in_offset=bass.IndirectOffsetOnAxis(ap=gcur[t.p][:, c:c + 1], axis=0),
                                          bounds_check=2 * E * CAP - 1, oob_is_err=False).then_inc(s(f"xg_in{t.p}"), 16)

            def add_rows(t):
                for c in range(CT):
                    apart("yo", CT * t.i + c + 1)
                    if c == 0 and not (isinstance(t.i, int) and t.i == 0):
                        b = t.back(1)
                        apart(f"y_out{b.p}", 16 * CT * (b.half + 1))
                    gp.indirect_dma_start(out=ov, out_offset=bass.IndirectOffsetOnAxis(ap=tok[t.p][:, c:c + 1], axis=0),
                                          in_=yo[:, c], in_offset=None, bounds_check=L - 1, oob_is_err=False,
                                          compute_op=ALU.add).then_inc(s(f"y_out{t.p}"), 16)

            def expert(t, first=False, last=False):
                if not last:
                    gather(t.ahead(1))
                if not first:
                    w1_low(t, HC - 1)
                for hc in range(HC - 1):
                    if hc == 1 and not first:
                        add_rows(t.back(1))
                    if not last:
                        w1_low(t.ahead(1), hc)

            for p in range(2):
                gp.wait_ge(s(f"routed_out{p}"), 16 * LT)
            gather(Tile(0, 0, 0))
            for p in range(2):
                gp.wait_ge(s(f"x1_out{p}"), 16 * LT // 2)
            expert(Tile(0, 0, 0), first=True)
            tiles(gp, 1, 2, expert)
            tiles(gp, 2, E - 2, expert)
            expert(Tile(E - 2, E // 2 - 1, 0))
            expert(Tile(E - 1, E // 2 - 1, 1), last=True)
            add_rows(Tile(E - 1, E // 2 - 1, 1))

        @block.scalar
        def _(act):
            act.dma_start(x_all[:, 0:XFIRST], xv[:, 0:XFIRST]).then_inc(s("x_first"), 16)

            def weights_high(u):
                act.wait_ge(s("wt_T"), u + 1)
                act.activation(unit_out(u, 0), unit_in(u), ACT.Copy).then_inc(s("wt_high"), 1)
            for u in range(4):
                weights_high(u)
            act.wait_ge(s("g_consts"), 1)

            def load_context(u, last=False):
                if last:
                    act.dma_start(tin[u.p][0:CREM, 0], ctx_in[0, C - CREM:C]).then_inc(s(f"tin_in{u.p}"), 16)
                else:
                    act.dma_start(tin[u.p][:], ctx_in[0, bass.ds(u.i * 2 * P, 2 * P)].rearrange("(a p) d -> p a d", p=P)).then_inc(s(f"tin_in{u.p}"), 16)

            def proj_step(cur, old):
                if cur:
                    ph, u, n = cur
                    act.wait_ge(s(f"{ph}_T"), u.i + 1)
                    if isinstance(u.i, int):
                        after = u.i + 2 if ph == "c" else u.i + 2 - XPAIRS
                        if 0 <= after < CPAIRS:
                            load_context(Tile(after, after // 2, u.p), after == CPAIRS - 1)
                    act.activation(tT[u.p][0][:, :, 0:n * P], T_BANK[u.p][:].rearrange("p (c l) -> p c l", c=DC)[:, :, 0:n * P],
                                   ACT.Copy).then_inc(s(f"{ph}_tT_high"), 1)
                    if not old:
                        for u in range(4, UNITS):
                            weights_high(u)
                if old:
                    ph, j, n = old
                    kd, vd, qd, bn = (kchar, vchar, qchar, 0) if ph == "x" else (ksub, vsub, qsub, 2)
                    if ph == "x" and isinstance(j.i, int) and j.i == 0:
                        act.wait_ge(s("vec_T"), 1)
                        act.activation(vec_cols[:], V_BANK[1][:, 0:VECS], ACT.Copy).then_inc(s("vec_cols"), 1)
                        act.wait_ge(s("vec_cols"), 1)
                    act.wait_ge(s(f"{ph}_mm"), j.i + 1)
                    for oc in range(DC):
                        cols = slice(oc * 2 * P, oc * 2 * P + n * P)
                        m = act.activation(kd[0][:, oc, bass.ds(j.i * 2 * P, n * P)], K_BANK[j.p][:, cols], ACT.Identity,
                                           bias=bias_cols[:, bn + 1, oc:oc + 1])
                    m.then_inc(s(f"{ph}_high_k"), 1)
                    for oc in range(DC):
                        cols = slice(oc * 2 * P, oc * 2 * P + n * P)
                        act.activation(qd[:, bass.ds(j.i * 2, n), oc], Q_BANK[j.p][:, cols].rearrange("p (a l) -> p a l", a=n), ACT.Identity,
                                       bias=bias_cols[:, bn, oc:oc + 1])
                    act.activation(vd[:, bass.ds(j.i * 2, n), 0:D], V_BANK[j.p][:, 0:n * D].rearrange("p (a d) -> p a d", a=n),
                                   ACT.Copy).then_inc(s(f"{ph}_high_kqv"), 1)
            pairs(act, proj_step)
            act.wait_ge(s("consts_in"), CONSTS * 16)
            act.activation(tgains[:], gains[:], ACT.Tanh).then_inc(s("tgains"), 1)

            def high(t, g, ph, groups):
                n = len(groups[g])
                act.wait_ge(s(f"{ph}_T{g % 2}"), 2 * t.i + g // 2 + 1)
                act.activation(pt[0][:, groups[g][0]:groups[g][0] + n], ptb[g % 2][:, 0:n * P].rearrange("p (k l) -> p k l", k=n),
                               ACT.Copy).then_inc(s(f"{ph}_high{g % 2}"), 1)

            def exps(t, c, ph, chunks, keys):
                act.wait_ge(s(f"{ph}_bias"), t.i + 1)
                o, w = chunks[c][0], min(chunks[c][1], keys - chunks[c][0])
                act.activation(probs[t.p][:, o:o + w], scores[c][:, 0:w], ACT.Exp, bias=nbias[:, t.p:t.p + 1], scale=SCALE,
                               accum_out=esum[:, t.p, c:c + 1]).then_inc(s(f"{ph}_exp"), 1)

            def a_step(t, cur=True, prev=True):
                b = t.back(1)
                for g in range(2):
                    if prev:
                        high(b, g, "a", GROUPS_A)
                for g in range(2):
                    if cur:
                        exps(t, g, "a", CHUNKS_A, L)
                    if prev:
                        high(b, 2 + g, "a", GROUPS_A)
                if cur:
                    exps(t, 2, "a", CHUNKS_A, L)
                    exps(t, 3, "a", CHUNKS_A, L)
            a_step(Tile(0, 0, 0), prev=False)
            tiles(act, 1, CTX, a_step)

            def tent_weights(j):
                if isinstance(j.i, int) and j.i == 0:
                    act.wait_ge(s("g_consts"), 1)
                else:
                    act.wait_ge(s("interp"), j.i)
                    act.wait_ge(s("tdist"), j.i)
                act.activation(tabs[:], tdist[:], ACT.Abs).then_inc(s("tabs"), 1)
                act.wait_ge(s("tabs"), j.i + 1)
                act.activation(tent[:], tabs[:], ACT.Relu, scale=-1.0, bias=one[:]).then_inc(s("tent"), 1)

            def rows_transposed(o):
                act.wait_ge(s("xn2_T"), o.i + 1)
                act.activation(xn2T[:], obank[:, 0:D].rearrange("p (c l) -> p c l", c=DC), ACT.Copy).then_inc(s("xn2T"), 1)

            def interpolated(j):
                act.wait_ge(s("interp"), j.i + 1)
                if not (isinstance(j.i, int) and j.i < 1):
                    act.wait_ge(s("base"), j.i)
                act.activation(sub[:], misc[:, 0:D], ACT.Copy).then_inc(s("sub"), 1)

            def scaled(j):
                act.wait_ge(s("sub"), j.i + 1)
                act.activation(subt[:], sub[:], ACT.Copy, scale=tgains[:, 0:1]).then_inc(s("subt"), 1)

            def logit_exps(o):
                act.wait_ge(s("lmax"), o.i + 1)
                act.activation(pe_[:], obank[:, 0:E], ACT.Exp, bias=lmax[:, 0:1], accum_out=psm[:, 0:1]).then_inc(s("lexp"), 1)

            def gate_high(j):
                act.wait_ge(s("gate_T"), j.i + 1)
                act.activation(ginT[0][:], misc[:].rearrange("p (c l) -> p c l", c=2 * DC), ACT.Copy).then_inc(s("gin_high"), 1)

            def gate_tanh(j):
                act.wait_ge(s("z"), j.i + 1)
                act.activation(tgate[:], zgate[:], ACT.Tanh, scale=0.5).then_inc(s("tgate"), 1)

            def b_step(t, cur=True, prev=True, old=True, older=True):
                b, j, o = t.back(1), t.back(2), t.back(3)
                if old:
                    interpolated(j)
                if older:
                    rows_transposed(o)
                if old:
                    gate_high(j)
                    scaled(j)
                if older:
                    logit_exps(o)
                if prev:
                    high(b, 0, "b", GROUPS_B)
                    high(b, 1, "b", GROUPS_B)
                    high(b, 2, "b", GROUPS_B)
                if cur:
                    exps(t, 0, "b", CHUNKS_B, C)
                if old:
                    gate_tanh(j)
                if prev:
                    high(b, 3, "b", GROUPS_B)
                if cur:
                    exps(t, 1, "b", CHUNKS_B, C)
                    exps(t, 2, "b", CHUNKS_B, C)
                    exps(t, 3, "b", CHUNKS_B, C)
                if prev:
                    tent_weights(b)
                if old:
                    act.wait_ge(s("x1"), j.i + 1)
                    act.dma_start(ov[bass.ds(j.i * P, P)], x1[j.p][:]).then_inc(s(f"x1_out{j.p}"), 16)
            act.wait_ge(s("empty_in"), 16 * 2 * E)
            for g in range(4):
                high(Tile(CTX - 1, (CTX - 1) // 2, (CTX - 1) % 2), g, "a", GROUPS_A)
            act.wait_ge(s("a_norm_chain"), NORM_STEPS * CTX)
            act.wait_ge(s("a_T0"), 2 * CTX)
            act.wait_ge(s("a_T1"), 2 * CTX)
            tiles(act, 0, 1, lambda t: b_step(t, prev=False, old=False, older=False))
            tiles(act, 1, 2, lambda t: b_step(t, old=False, older=False))
            tiles(act, 2, 3, lambda t: b_step(t, older=False))
            tiles(act, 3, LT, b_step)
            tiles(act, LT, LT + 1, lambda t: b_step(t, cur=False))
            tiles(act, LT + 1, LT + 2, lambda t: b_step(t, cur=False, prev=False))
            tiles(act, LT + 2, LT + 3, lambda t: b_step(t, cur=False, prev=False, old=False))

            def rows_high(t):
                for dc in range(DC):
                    act.wait_ge(s("xg_T"), DC * t.i + dc + 1)
                    act.activation(xgT[t.p][0][:, dc], bank[4 + dc][:], ACT.Copy).then_inc(s("xgT_high"), 1)

            def weighted(t, c):
                act.wait_ge(s("yb"), CT * t.i + c + 1)
                if c == 0 and not (isinstance(t.i, int) and t.i == 0):
                    b = t.back(1)
                    act.wait_ge(s(f"y_out{b.p}"), 16 * CT * (b.half + 1))
                act.activation(yo[:, c], yb[:, c], ACT.Copy, scale=wt[:, t.p, c:c + 1]).then_inc(s("yo"), 1)

            def gelu(t, hc):
                act.wait_ge(s("h_mm"), HC * t.i + hc + 1)
                if not (isinstance(t.i, int) and t.i == 0 and hc < 2):
                    act.wait_ge(s("hid_low"), HC * t.i + hc - 1)
                act.activation(hid[hc % 2][:], bank[6 + hc % 2][:], ACT.Gelu_apprx_tanh,
                               bias=b1c[:, bass.ds(t.i, 1), hc].rearrange("p a -> p a")).then_inc(s("gelu"), 1)

            def w1_high(t, hc):
                if hc == 0:
                    act.wait_ge(s(f"w_in{t.p}"), 32 * (t.half + 1))
                cols = slice(hc * P, hc * P + P)
                act.wait_ge(s("h_mm"), HC * (t.i - 1) + hc + 1)
                act.activation(w1s[0][:, :, cols], w1_raw[t.p][:, :, cols], ACT.Copy).then_inc(s("w1_high"), 1)

            def w2_high(t, hc):
                act.wait_ge(s("y_mm"), CT * (HC * (t.i - 1) + hc + 1))
                act.activation(w2s[:, hc, 0], w2_raw[t.p][:, hc], ACT.Copy).then_inc(s("w2_high"), 1)

            def chunk_before(t, hc, lag, first, last, body):
                if hc >= lag and not last:
                    body(t.ahead(1), hc - lag)
                elif hc < lag and not first:
                    body(t, hc - lag + HC)

            def expert(t, first=False, last=False):
                for hc in range(HC):
                    gelu(t, hc)
                    chunk_before(t, hc, 1, first, last, w1_high)
                    chunk_before(t, hc, 2, first, last, w2_high)
                    if hc == 1 and not first:
                        for c in range(CT):
                            weighted(t.back(1), c)
                    if hc == AHEAD and not last:
                        rows_high(t.ahead(1))
            rows_high(Tile(0, 0, 0))
            expert(Tile(0, 0, 0), first=True)
            tiles(act, 1, 2, expert)
            tiles(act, 2, E - 2, expert)
            expert(Tile(E - 2, E // 2 - 1, 0))
            t = Tile(E - 1, E // 2 - 1, 1)
            expert(t, last=True)
            for c in range(CT):
                weighted(t, c)

        @block.vector
        def _(dve):
            def x_moments(u):
                for n in range(2):
                    tile = bass.ds(u.i * 2 + n, 1)
                    dve.bn_stats(stats[:, u.p, n], x_all[:, tile].rearrange("p a d -> p (a d)")).then_inc(s("stats"), 1)
                dve.wait_ge(s("stats"), 2 * (u.i + 1))
                dve.sem_inc(s("v_passed"), 1)
                for n in range(2):
                    dve.bn_aggr(mv[:, u.p, n], stats[:, u.p, n]).then_inc(s("aggr"), 1)
                dve.wait_ge(s("aggr"), 2 * (u.i + 1))
                dve.tensor_scalar(vpe[:, u.p], mv[:, u.p, :, 1], LN_EPS, None, ALU.add).then_inc(s("vpe"), 1)

            dve.wait_ge(s("x_first"), 16)
            for u in range(XFIRST // 2):
                x_moments(Tile(u, u // 2, u % 2))

            def weights_low(u):
                dve.wait_ge(s("wt_high"), u + 1)
                dve.tensor_tensor(unit_out(u, 1), unit_in(u), unit_out(u, 0).bitcast(f32), ALU.subtract).then_inc(s("wt_low"), 1)

            def norm(u):
                wait_pair_of_two_before(dve, "T", "x", u)
                dve.wait_ge(s("rstd"), u.i + 1)
                for n in range(2):
                    tile = bass.ds(u.i * 2 + n, 1)
                    m = dve.tensor_scalar(tin[u.p][:, n], x_all[:, tile].rearrange("p a d -> p (a d)"),
                                          mv[:, u.p, n, 0:1], rstd[:, u.p, n:n + 1], ALU.subtract, ALU.mult)
                m.then_inc(s("tin_norm"), 1)

            def proj_step(cur, old):
                if cur:
                    ph, u, n = cur
                    if ph == "x" and not (isinstance(u.i, int) and u.i in (0, XPAIRS - 1)):
                        norm(u.ahead(1))
                    dve.wait_ge(s(f"{ph}_tT_high"), u.i + 1)
                    dve.tensor_tensor(tT[u.p][1][:, :, 0:n * P], T_BANK[u.p][:].rearrange("p (c l) -> p c l", c=DC)[:, :, 0:n * P],
                                      tT[u.p][0][:, :, 0:n * P].bitcast(f32), ALU.subtract).then_inc(s(f"{ph}_tT_low"), 1)
                    if not old:
                        for w in range(4, UNITS):
                            weights_low(w)
                    if ph == "x" and isinstance(u.i, int) and u.i == 0:
                        dve.wait_ge(s("x_rest"), 16)
                    if ph == "x" and not (isinstance(u.i, int) and u.i >= XPAIRS - 2):
                        x_moments(u.ahead(2))
                if old:
                    ph, j, n = old
                    kd, vd, bn = (kchar, vchar, 0) if ph == "x" else (ksub, vsub, 2)
                    if ph == "x" and isinstance(j.i, int) and j.i == 0:
                        dve.wait_ge(s("vec_cols"), 1)
                    dve.wait_ge(s(f"{ph}_high_k"), j.i + 1)
                    for oc in range(DC):
                        at_ = bass.ds(j.i * 2 * P, n * P)
                        dve.scalar_tensor_tensor(kd[1][:, oc, at_], K_BANK[j.p][:, oc * 2 * P:oc * 2 * P + n * P], bias_cols[:, bn + 1, oc:oc + 1],
                                                 kd[0][:, oc, at_].bitcast(f32), ALU.add, ALU.subtract)
                    dve.wait_ge(s(f"{ph}_high_kqv"), j.i + 1)
                    dve.tensor_tensor(vd[:, bass.ds(j.i * 2, n), D:2 * D], V_BANK[j.p][:, 0:n * D].rearrange("p (a d) -> p a d", a=n),
                                      vd[:, bass.ds(j.i * 2, n), 0:D].bitcast(f32), ALU.subtract).then_inc(s(f"{ph}_low_v"), 1)

            norm(Tile(0, 0, 0))
            norm(Tile(1, 0, 1))
            for u in range(4):
                weights_low(u)
            pairs(dve, proj_step)
            dve.wait_ge(s("consts_in"), CONSTS * 16)

            def maxima(t, c, ph, chunks, keys):
                w = min(chunks[c][1], keys - chunks[c][0])
                dve.wait_ge(s(f"{ph}_scores"), 4 * t.i + c + 1)
                dve.reduce_max(mx[:, t.p, c:c + 1], scores[c][:, 0:w], AX.X).then_inc(s(f"{ph}_max"), 1)

            def row_maxima(t, ph):
                dve.wait_ge(s(f"{ph}_max"), 4 * t.i + 4)
                dve.tensor_reduce(nmx[:, t.p:t.p + 1], mx[:, t.p], AX.X, ALU.max, negate=True).then_inc(s(f"{ph}_nmx"), 1)

            def softmax_bias(t, ph):
                dve.wait_ge(s(f"{ph}_nmx"), t.i + 1)
                dve.tensor_scalar(nbias[:, t.p:t.p + 1], nmx[:, t.p:t.p + 1], SCALE, None, ALU.mult).then_inc(s(f"{ph}_bias"), 1)

            def low(t, g, ph, groups):
                n, k = len(groups[g]), groups[g][0]
                dve.wait_ge(s(f"{ph}_high{g % 2}"), 2 * t.i + g // 2 + 1)
                dve.tensor_tensor(pt[1][:, k:k + n], ptb[g % 2][:, 0:n * P].rearrange("p (k l) -> p k l", k=n),
                                  pt[0][:, k:k + n].bitcast(f32), ALU.subtract).then_inc(s(f"{ph}_low{g % 2}"), 1)

            def inverse_sums(t, ph):
                dve.wait_ge(s(f"{ph}_exp"), 4 * t.i + 4)
                then_wait(dve, dve.reduce_sum(zsum[:], esum[:, t.p], AX.X), f"{ph}_norm_chain", NORM_STEPS * t.i + 1)
                dve.reciprocal(rz[:, t.p:t.p + 1], zsum[:]).then_inc(s(f"{ph}_norm_chain"), 1)

            def attention_rows(t, ph, n):
                dve.wait_ge(s(f"{ph}_norm_chain"), NORM_STEPS * (t.i + 1))
                if ph == "a" and not (isinstance(t.i, int) and t.i < 2):
                    dve.wait_ge(s(f"sub_out{t.p}"), 16 * t.half)
                if ph == "b" and not (isinstance(t.i, int) and t.i < 2):
                    dve.wait_ge(s("gate_T"), t.i - 1)
                    dve.wait_ge(s("diff"), t.i - 1)
                dve.wait_ge(s(f"{ph}_pv"), t.i + 1)
                dve.scalar_tensor_tensor(att[t.p][:], obank[:, 0:D], rz[:, t.p:t.p + 1], bias_rows[:, n],
                                         ALU.mult, ALU.add).then_inc(s(f"{ph}_att"), 1)

            def a_step(t, cur=True, prev=True, old=True):
                b = t.back(1)
                if old:
                    attention_rows(t.back(2), "a", 1)
                if cur:
                    for c in range(3):
                        maxima(t, c, "a", CHUNKS_A, L)
                if prev:
                    low(b, 0, "a", GROUPS_A)
                if cur:
                    maxima(t, 3, "a", CHUNKS_A, L)
                    row_maxima(t, "a")
                    softmax_bias(t, "a")
                if prev:
                    for g in (1, 2, 3):
                        low(b, g, "a", GROUPS_A)
                    inverse_sums(b, "a")
            a_step(Tile(0, 0, 0), prev=False, old=False)
            a_step(Tile(1, 0, 1), old=False)
            a_step(Tile(2, 1, 0))
            a_step(Tile(3, 1, 1))
            dve.wait_ge(s("sub_first"), 16)
            tiles(dve, 4, CTX, a_step)

            last, first = Tile(CTX - 1, (CTX - 1) // 2, (CTX - 1) % 2), Tile(0, 0, 0)
            attention_rows(last.back(1), "a", 1)
            inverse_sums(last, "a")
            for c in range(3):
                maxima(first, c, "b", CHUNKS_B, C)
            low(last, 0, "a", GROUPS_A)
            maxima(first, 3, "b", CHUNKS_B, C)
            row_maxima(first, "b")
            softmax_bias(first, "b")
            for g in (1, 2, 3):
                low(last, g, "a", GROUPS_A)
            dve.wait_ge(s("a_T0"), 2 * CTX)
            dve.wait_ge(s("a_T1"), 2 * CTX)
            for p in range(2):
                dve.memset(probs[p][:, C:CTX * P], 0.0).then_inc(s("b_pad"), 1)
            attention_rows(last, "a", 1)

            def rank_rows(j):
                dve.wait_ge(s("rank_mm"), j.i + 1)
                wait(dve, s("counts"), j.i)
                dve.tensor_tensor(rank[:], misc[:, 0:2 * E].rearrange("p (v e) -> p v e", v=2), counts[:], ALU.add).then_inc(s("rank_chain"), 1)
                dve.tensor_tensor(counts[:], misc[:, 2 * E:4 * E].rearrange("p (v e) -> p v e", v=2), counts[:], ALU.add).then_inc(s("counts"), 1)

            def slots(j):
                dve.wait_ge(s("rank_chain"), RANK_STEPS * j.i + 1)
                then_wait(dve, dve.tensor_tensor(over[:], rank[:], full_e[:], ALU.is_ge), "rank_chain", RANK_STEPS * j.i + 2)
                then_wait(dve, dve.scalar_tensor_tensor(rank[:], over[:], float(SKIP), rank[:], ALU.mult, ALU.add), "rank_chain", RANK_STEPS * j.i + 3)
                then_wait(dve, dve.tensor_tensor(rank[:], rank[:], oneh[:].bitcast(f32), ALU.mult), "rank_chain", RANK_STEPS * j.i + 4)
                then_wait(dve, dve.reduce_sum(slotf[:], rank[:], AX.X), "rank_chain", RANK_STEPS * j.i + 5)
                dve.tensor_copy(sloti[j.p][:], slotf[:]).then_inc(s("slots"), 1)

            def gate_low(j):
                dve.wait_ge(s("gin_high"), j.i + 1)
                dve.tensor_tensor(ginT[1][:], misc[:].rearrange("p (c l) -> p c l", c=2 * DC), ginT[0][:].bitcast(f32), ALU.subtract).then_inc(s("gin_low"), 1)

            def gate_argument(j):
                dve.wait_ge(s("gate_mm"), j.i + 1)
                dve.tensor_tensor(zgate[:], misc[:, 0:D], bias_rows[:, 2], ALU.add).then_inc(s("z"), 1)

            def mix(j):
                dve.wait_ge(s("tgate"), j.i + 1)
                dve.wait_ge(s("diff"), j.i + 1)
                then_wait(dve, dve.scalar_tensor_tensor(mixed[:], tgate[:], 1.0, diff[:], ALU.add, ALU.mult), "mixed", j.i + 1)
                dve.wait_ge(s("base"), j.i + 1)
                if not (isinstance(j.i, int) and j.i < 2):
                    dve.wait_ge(s(f"x1_out{j.p}"), 16 * j.half)
                dve.scalar_tensor_tensor(x1[j.p][:], mixed[:], thalf[:], base[:], ALU.mult, ALU.add).then_inc(s("x1"), 1)

            def moments(j):
                dve.wait_ge(s("x1"), j.i + 1)
                then_wait(dve, dve.bn_stats(st1[:], x1[j.p][:]), "st1", j.i + 1)
                dve.sem_inc(s("v_passed"), 1)
                then_wait(dve, dve.bn_aggr(mv1[:], st1[:]), "mv1", j.i + 1)
                dve.tensor_scalar(rs1[:, 0:1], mv1[:, 1:2], LN_EPS, None, ALU.add).then_inc(s("vpe1"), 1)

            def norm_rows(j):
                dve.wait_ge(s("rs1"), j.i + 1)
                if not (isinstance(j.i, int) and j.i < 2):
                    dve.wait_ge(s(f"routed_out{j.p}"), 32 * j.half)
                dve.tensor_scalar(row[j.p][:, 0:D], x1[j.p][:], mv1[:, 0:1], rs1[:, 1:2], ALU.subtract, ALU.mult).then_inc(s("xn2"), 1)

            def logit_maxima(o):
                dve.wait_ge(s("logits"), o.i + 1)
                dve.tensor_reduce(lmax[:, 0:1], obank[:, 0:E], AX.X, ALU.max, negate=True).then_inc(s("lmax"), 1)

            def choose(o):
                n = CHOICE_STEPS * o.i
                dve.wait_ge(s("lexp"), o.i + 1)
                then_wait(dve, dve.reciprocal(psm[:, 1:2], psm[:, 0:1]), "choice_chain", n + 1)
                then_wait(dve, dve.tensor_scalar(prob[:], pe_[:], psm[:, 1:2], None, ALU.mult), "choice_chain", n + 2)
                dve.sem_inc(s("v_passed"), 1)
                then_wait(dve, dve.max(best[:], prob[:]), "choice_chain", n + 3)
                dve.sem_inc(s("v_passed"), 1)
                dve.max_index(besti[:], best[:], prob[:]).then_inc(s("besti"), 1)
                dve.tensor_scalar(wsum[:, 0:1], best[:, 0:1], best[:, 1:2], 1e-9, ALU.add, ALU.add).then_inc(s("choice_chain"), 1)

            def choice_weights(o):
                n = CHOICE_STEPS * o.i
                dve.wait_ge(s("choice_chain"), n + 4)
                dve.reciprocal(wsum[:, 1:2], wsum[:, 0:1]).then_inc(s("choice_chain"), 1)
                dve.wait_ge(s("besti"), o.i + 1)
                dve.tensor_copy(bestf[:, 0:2], besti[:, 0:2]).then_inc(s("choice_chain"), 1)
                wait(dve, s("token"), o.i)
                dve.tensor_copy(row[o.p][:, D + 2:D + 3], token[:])
                dve.tensor_scalar(token[:], token[:], float(P), None, ALU.add).then_inc(s("token"), 1)
                dve.wait_ge(s("choice_chain"), n + 6)
                dve.tensor_scalar(row[o.p][:, D:D + 2], best[:, 0:2], wsum[:, 1:2], tgains[:, 1:2], ALU.mult, ALU.mult)
                for v in range(2):
                    dve.tensor_scalar(oneh[:, v], iota_e[:], bestf[:, v:v + 1], None, ALU.is_equal).then_inc(s("oneh"), 1)

            def b_step(t, cur=True, prev=True, old=True, older=True):
                b, j, o = t.back(1), t.back(2), t.back(3)
                if cur:
                    maxima(t, 0, "b", CHUNKS_B, C)
                if old:
                    dve.wait_ge(s("tabs"), j.i + 1)
                    dve.tensor_scalar(tdist[:], tdist[:], C / STEP - C // STEP, None, ALU.add).then_inc(s("tdist"), 1)
                if cur:
                    maxima(t, 1, "b", CHUNKS_B, C)
                if old:
                    gate_low(j)
                if cur:
                    maxima(t, 2, "b", CHUNKS_B, C)
                if older:
                    logit_maxima(o)
                if prev:
                    low(b, 0, "b", GROUPS_B)
                if older:
                    choose(o)
                if cur:
                    maxima(t, 3, "b", CHUNKS_B, C)
                    row_maxima(t, "b")
                if prev:
                    low(b, 1, "b", GROUPS_B)
                if cur:
                    softmax_bias(t, "b")
                if old:
                    gate_argument(j)
                if prev:
                    low(b, 2, "b", GROUPS_B)
                if older:
                    choice_weights(o)
                if prev:
                    low(b, 3, "b", GROUPS_B)
                if old:
                    mix(j)
                if prev:
                    inverse_sums(b, "b")
                if old:
                    moments(j)
                if older:
                    rank_rows(o)
                if prev and not cur:
                    attention_rows(b, "b", 0)
                if old:
                    norm_rows(j)
                if prev and cur:
                    attention_rows(b, "b", 0)
                if older:
                    slots(o)
            dve.wait_ge(s("g_consts"), 1)
            dve.wait_ge(s("tgains"), 1)
            dve.tensor_scalar(thalf[:], tgains[:, 0:1], 0.5, None, ALU.mult).then_inc(s("thalf"), 1)
            dve.wait_ge(s("empty_in"), 16 * 2 * E)
            dve.wait_ge(s("sub_edge"), 48)
            dve.wait_ge(s("sub_out1"), 16 * ((CTX - 1) // 2))
            dve.wait_ge(s("thalf"), 1)
            tiles(dve, 1, 2, lambda t: b_step(t, old=False, older=False))
            tiles(dve, 2, 3, lambda t: b_step(t, older=False))
            tiles(dve, 3, LT, b_step)
            tiles(dve, LT, LT + 1, lambda t: b_step(t, cur=False))
            tiles(dve, LT + 1, LT + 2, lambda t: b_step(t, cur=False, prev=False))
            tiles(dve, LT + 2, LT + 3, lambda t: b_step(t, cur=False, prev=False, old=False))

            dve.wait_ge(s("b_pv"), LT)
            dve.wait_ge(s("counts"), LT)
            by_chunk = lambda v: v.rearrange("p (e a) -> p e a", a=1).broadcast_to([P, E, CT])
            then_wait(dve, dve.tensor_tensor(first_free[:], counts[:, 0], full_e[:, 0], ALU.min), "e_chain", 1)
            dve.tensor_tensor(second[:], slot0[:], by_chunk(first_free[:]), ALU.is_ge)
            then_wait(dve, dve.scalar_tensor_tensor(shift[:], base_e[:, 0], float(E * CAP), first_free[:], ALU.add, ALU.subtract), "e_chain", 2)
            then_wait(dve, dve.tensor_tensor(slot[:], second[:], by_chunk(shift[:]), ALU.mult), "e_chain", 3)
            then_wait(dve, dve.tensor_tensor(slot[:], slot[:], slot0[:], ALU.add), "e_chain", 4)

            def places(t):
                if not (isinstance(t.i, int) and t.i < 2):
                    dve.wait_ge(s(f"xg_in{t.p}"), 16 * CT * t.half)
                dve.tensor_copy(gcur[t.p][:], slot[:, bass.ds(t.i, 1)].rearrange("p a c -> p (a c)")).then_inc(s("gcur"), 1)

            def rows_low(t):
                for dc in range(DC):
                    dve.wait_ge(s("xgT_high"), DC * t.i + dc + 1)
                    dve.tensor_tensor(xgT[t.p][1][:, dc], bank[4 + dc][:], xgT[t.p][0][:, dc].bitcast(f32), ALU.subtract).then_inc(s("xgT_low"), 1)

            def weights_and_tokens(t):
                dve.wait_ge(s(f"xg_in{t.p}"), 16 * CT * (t.half + 1))
                m = second[:, bass.ds(t.i, 1)].rearrange("p a c -> p (a c)")
                then_wait(dve, dve.tensor_tensor(wd[:], xg[t.p][:, :, D + 1], xg[t.p][:, :, D], ALU.subtract), "wd", 2 * t.i + 1)
                then_wait(dve, dve.tensor_tensor(wd[:], wd[:], m, ALU.mult), "wd", 2 * t.i + 2)
                dve.tensor_tensor(wt[:, t.p], wd[:], xg[t.p][:, :, D], ALU.add)
                if not (isinstance(t.i, int) and t.i < 2):
                    dve.wait_ge(s(f"y_out{t.p}"), 16 * CT * t.half)
                dve.tensor_copy(tok[t.p][:], xg[t.p][:, :, D + 2]).then_inc(s("wt"), 1)

            def output_rows(t, c):
                dve.wait_ge(s("y_mm"), CT * (HC * t.i + HC - 1) + c + 1)
                if c == 0:
                    dve.wait_ge(s(f"b2_in{t.p}"), 16 * (t.half + 1))
                    if not (isinstance(t.i, int) and t.i == 0):
                        dve.wait_ge(s("yo"), CT * t.i)
                dve.tensor_tensor(yb[:, c], ysum(c), b2r[:, t.p], ALU.add).then_inc(s("yb"), 1)

            def split_hidden(t, hc):
                dve.wait_ge(s("gelu"), HC * t.i + hc + 1)
                if not (isinstance(t.i, int) and t.i == 0 and hc < 2):
                    dve.wait_ge(s("y_mm"), CT * (HC * t.i + hc - 1))
                dve.tensor_copy(hs[hc % 2][0][:], hid[hc % 2][:]).then_inc(s("hid_high"), 1)
                dve.wait_ge(s("hid_high"), HC * t.i + hc + 1)
                dve.tensor_tensor(hs[hc % 2][1][:], hid[hc % 2][:], hs[hc % 2][0][:].bitcast(f32), ALU.subtract).then_inc(s("hid_low"), 1)

            def w2_low(t, hc):
                dve.wait_ge(s("w2_high"), HC * (t.i - 1) + hc + 1)
                dve.tensor_tensor(w2s[:, hc, 1], w2_raw[t.p][:, hc], w2s[:, hc, 0].bitcast(f32), ALU.subtract).then_inc(s("w2_split"), 1)

            def expert(t, first=False, last=False):
                if not last:
                    places(t.ahead(1))
                for hc in range(HC):
                    split_hidden(t, hc)
                    if hc == 0 and not first:
                        for c in range(CT):
                            output_rows(t.back(1), c)
                    if hc >= 2 and not last:
                        w2_low(t.ahead(1), hc - 2)
                    elif hc < 2 and not first:
                        w2_low(t, hc - 2 + HC)
                    if hc == AHEAD and not last:
                        rows_low(t.ahead(1))
                        weights_and_tokens(t.ahead(1))
            places(Tile(0, 0, 0))
            rows_low(Tile(0, 0, 0))
            weights_and_tokens(Tile(0, 0, 0))
            expert(Tile(0, 0, 0), first=True)
            tiles(dve, 1, 2, expert)
            tiles(dve, 2, E - 2, expert)
            expert(Tile(E - 2, E // 2 - 1, 0))
            t = Tile(E - 1, E // 2 - 1, 1)
            expert(t, last=True)
            for c in range(CT):
                output_rows(t, c)

        @block.tensor
        def _(pe):
            def three(dst, lhs, rhs, start, stop):
                pe.matmul(dst, lhs[0], rhs[0], start=start, stop=False)
                pe.matmul(dst, lhs[0], rhs[1], start=False, stop=False)
                return pe.matmul(dst, lhs[1], rhs[0], start=False, stop=stop)

            pe.wait_ge(s("ident"), 1)
            def weight_transposes(u):
                pe.wait_ge(s(f"weight_in{min(u, 6)}"), 16)
                for ic in range(DC):
                    for oc in range(DC):
                        raw = w_raw[:, u, oc, ic * P:(ic + 1) * P] if u < 6 else wg_raw[:, oc, ((u - 6) * DC + ic) * P:((u - 6) * DC + ic + 1) * P]
                        m = pe.transpose(unit_bank(u)[:, ic * D + oc * P:ic * D + (oc + 1) * P], raw, ident[:])
                m.then_inc(s("wt_T"), 1)
            for u in range(4):
                weight_transposes(u)

            def proj_step(cur, old):
                if cur:
                    ph, u, n = cur
                    if ph == "x" and isinstance(u.i, int) and u.i < 2:
                        pe.wait_ge(s("wt_low"), 4 * u.i + 1)
                    if ph == "x":
                        pe.wait_ge(s("tin_norm"), u.i + 1)
                    else:
                        pe.wait_ge(s(f"tin_in{u.p}"), 16 * (u.half + 1))
                    wait_pair_of_two_before(pe, "tT_low", ph, u)
                    for dc in range(DC):
                        for a in range(n):
                            m = pe.transpose(T_BANK[u.p][:, (dc * 2 + a) * P:(dc * 2 + a + 1) * P], tin[u.p][:, a, dc * P:(dc + 1) * P], ident[:])
                    m.then_inc(s(f"{ph}_T"), 1)
                    if not old:
                        for u in range(4, UNITS):
                            weight_transposes(u)
                if old:
                    ph, j, n = old
                    w0 = 0 if ph == "x" else 3
                    pe.wait_ge(s(f"{ph}_tT_low"), j.i + 1)
                    wait_pair_of_two_before(pe, "low_v", ph, j)
                    if ph == "x" and isinstance(j.i, int) and j.i == 0:
                        pe.wait_ge(s("wt_low"), 4)
                    if ph == "x" and j.p == 1:
                        pe.wait_ge(s("vec_cols"), 1)
                    for dst, w in ((K_BANK, wT[w0 + 1]), (Q_BANK, wT[w0])):
                        for oc in range(DC):
                            for dc in range(DC):
                                three(dst[j.p][:, oc * 2 * P:oc * 2 * P + n * P],
                                      [w[:, dc, h, oc * P:(oc + 1) * P] for h in range(2)],
                                      [tT[j.p][h][:, dc, 0:n * P] for h in range(2)], dc == 0, dc == DC - 1)
                    for a in range(n):
                        for dc in range(DC):
                            m = three(V_BANK[j.p][:, a * D:(a + 1) * D], [tT[j.p][h][:, dc, a * P:(a + 1) * P] for h in range(2)],
                                      [wT[w0 + 2][:, dc, h] for h in range(2)], dc == 0, dc == DC - 1)
                    m.then_inc(s(f"{ph}_mm"), 1)
                    if ph == "x" and isinstance(j.i, int) and j.i == 0:
                        pe.wait_ge(s("wt_low"), UNITS)
                        pe.wait_ge(s("vecs_in"), VEC_LOADS * 16)
                        pe.transpose(V_BANK[1][:, 0:VECS], vec_rows[:], ident[0:VECS, 0:VECS]).then_inc(s("vec_T"), 1)
            pairs(pe, proj_step)

            def score(t, c, ph, k, chunks):
                if c == 0:
                    pe.wait_ge(s(f"{ph}_q"), t.i + 1)
                if not (isinstance(t.i, int) and t.i == 0):
                    pe.wait_ge(s(f"{ph}_exp"), 4 * (t.i - 1) + c + 1)
                elif ph == "b":
                    pe.wait_ge(s("a_exp"), 4 * (CTX - 1) + c + 1)
                elif c == 0:
                    pe.wait_ge(s("c_low_v"), CPAIRS - 1)
                o, w = chunks[c]
                for dc in range(DC):
                    m = three(scores[c][:, 0:w], [qs[t.p][h][:, dc] for h in range(2)],
                              [k[h][:, dc, o:o + w] for h in range(2)], dc == 0, dc == DC - 1)
                m.then_inc(s(f"{ph}_scores"), 1)

            def transpose_probs(t, g, ph, groups):
                pe.wait_ge(s(f"{ph}_exp"), 4 * t.i + g + 1)
                if not (isinstance(t.i, int) and t.i == 0 and g < 2):
                    pe.wait_ge(s(f"{ph}_low{g % 2}"), 2 * t.i + g // 2)
                elif ph == "b":
                    pe.wait_ge(s(f"a_low{g}"), 2 * CTX)
                elif g == 0:
                    pe.wait_ge(s("c_low_v"), CPAIRS)
                if ph == "b" and isinstance(t.i, int) and t.i == 0 and g == 3:
                    pe.wait_ge(s("b_pad"), 2)
                for n, k in enumerate(groups[g]):
                    m = pe.transpose(ptb[g % 2][:, n * P:(n + 1) * P], probs[t.p][:, k * P:(k + 1) * P], ident[:])
                m.then_inc(s(f"{ph}_T{g % 2}"), 1)

            def values(t, g, ph, v, groups):
                pe.wait_ge(s(f"{ph}_low{g % 2}"), 2 * t.i + g // 2 + 1)
                if g == 0 and not (isinstance(t.i, int) and t.i == 0):
                    pe.wait_ge(s(f"{ph}_att"), t.i)
                elif g == 0 and ph == "b":
                    pe.wait_ge(s("a_att"), CTX)
                for k in groups[g]:
                    m = three(obank[:, 0:D], [pt[h][:, k] for h in range(2)],
                              [v[:, k, 0:D], v[:, k, D:2 * D]], k == 0, k == groups[-1][-1])
                if g == 3:
                    m.then_inc(s(f"{ph}_pv"), 1)

            def a_step(t, cur=True, prev=True):
                b = t.back(1)
                if cur:
                    for c in range(3):
                        score(t, c, "a", kchar, CHUNKS_A)
                if prev:
                    transpose_probs(b, 0, "a", GROUPS_A)
                if cur:
                    score(t, 3, "a", kchar, CHUNKS_A)
                if prev:
                    transpose_probs(b, 1, "a", GROUPS_A)
                    transpose_probs(b, 2, "a", GROUPS_A)
                    values(b, 0, "a", vchar, GROUPS_A)
                    transpose_probs(b, 3, "a", GROUPS_A)
                    values(b, 1, "a", vchar, GROUPS_A)
                    values(b, 2, "a", vchar, GROUPS_A)
                    values(b, 3, "a", vchar, GROUPS_A)
            a_step(Tile(0, 0, 0), prev=False)
            tiles(pe, 1, 2, a_step)
            tiles(pe, 2, CTX, a_step)
            last, first = Tile(CTX - 1, (CTX - 1) // 2, (CTX - 1) % 2), Tile(0, 0, 0)
            for c in range(3):
                score(first, c, "b", ksub, CHUNKS_B)
            transpose_probs(last, 0, "a", GROUPS_A)
            score(first, 3, "b", ksub, CHUNKS_B)
            transpose_probs(last, 1, "a", GROUPS_A)
            for g in (2, 3):
                transpose_probs(last, g, "a", GROUPS_A)
                values(last, g - 2, "a", vchar, GROUPS_A)
            for g in (2, 3):
                values(last, g, "a", vchar, GROUPS_A)

            def norm_transposes(o):
                pe.wait_ge(s("xn2"), o.i + 1)
                if isinstance(o.i, int) and o.i == LT - 1:
                    pe.wait_ge(s("b_att"), LT)
                else:
                    pe.wait_ge(s("b_att"), o.i + 2)
                for dc in range(DC):
                    m = pe.transpose(obank[:, dc * P:(dc + 1) * P], row[o.p][:, dc * P:(dc + 1) * P], ident[:])
                m.then_inc(s("xn2_T"), 1)

            def logit_products(o):
                pe.wait_ge(s("xn2T"), o.i + 1)
                for dc in range(DC):
                    m = pe.matmul(obank[:, 0:E], xn2T[:, dc], wroute[:, dc], start=dc == 0, stop=dc == DC - 1)
                m.then_inc(s("logits"), 1)

            def interpolate(j):
                pe.wait_ge(s("tent"), j.i + 1)
                pe.wait_ge(s("subwin_in"), 16 * (j.i + 1))
                if not (isinstance(j.i, int) and j.i < 2):
                    pe.wait_ge(s("counts"), j.i - 1)
                elif isinstance(j.i, int) and j.i == 1:
                    pe.wait_ge(s("z"), 1)
                pe.matmul(misc[:, 0:D], tent[:], subwin[:], start=True, stop=True).then_inc(s("interp"), 1)

            def gate_transposes(j):
                pe.wait_ge(s("b_att"), j.i + 1)
                pe.wait_ge(s("sub"), j.i + 1)
                for n, part in enumerate((att[j.p], sub)):
                    for dc in range(DC):
                        m = pe.transpose(misc[:, (n * DC + dc) * P:(n * DC + dc + 1) * P], part[:, dc * P:(dc + 1) * P], ident[:])
                m.then_inc(s("gate_T"), 1)

            def gate_products(j):
                pe.wait_ge(s("gin_high"), j.i + 1)
                pe.wait_ge(s("gin_low"), j.i + 1)
                for k in range(2 * DC):
                    m = three(misc[:, 0:D], [ginT[h][:, k] for h in range(2)], [wgT[:, k, h] for h in range(2)], k == 0, k == 2 * DC - 1)
                m.then_inc(s("gate_mm"), 1)

            def rank_products(o):
                pe.wait_ge(s("oneh"), 2 * (o.i + 1))
                if isinstance(o.i, int) and o.i == LT - 1:
                    pe.wait_ge(s("counts"), LT - 1)
                else:
                    pe.wait_ge(s("z"), o.i + 2)
                pe.matmul(misc[:, 0:2 * E], before[:], oneh[:].rearrange("p v e -> p (v e)"), start=True, stop=True)
                pe.matmul(misc[:, 2 * E:4 * E], every[:], oneh[:].rearrange("p v e -> p (v e)"), start=True, stop=True).then_inc(s("rank_mm"), 1)

            def b_step(t, cur=True, prev=True, old=True, older=True):
                b, j, o = t.back(1), t.back(2), t.back(3)
                if cur:
                    score(t, 0, "b", ksub, CHUNKS_B)
                if old:
                    interpolate(j)
                if cur:
                    score(t, 1, "b", ksub, CHUNKS_B)
                if older:
                    norm_transposes(o)
                if old:
                    gate_transposes(j)
                if cur:
                    score(t, 2, "b", ksub, CHUNKS_B)
                if older:
                    logit_products(o)
                if prev:
                    transpose_probs(b, 0, "b", GROUPS_B)
                if cur:
                    score(t, 3, "b", ksub, CHUNKS_B)
                if old:
                    gate_products(j)
                if prev:
                    transpose_probs(b, 1, "b", GROUPS_B)
                    transpose_probs(b, 2, "b", GROUPS_B)
                    if older:
                        pe.wait_ge(s("lexp"), o.i + 1)
                    values(b, 0, "b", vsub, GROUPS_B)
                    transpose_probs(b, 3, "b", GROUPS_B)
                    values(b, 1, "b", vsub, GROUPS_B)
                    values(b, 2, "b", vsub, GROUPS_B)
                if older:
                    rank_products(o)
                if prev:
                    values(b, 3, "b", vsub, GROUPS_B)
            tiles(pe, 1, 2, lambda t: b_step(t, old=False, older=False))
            tiles(pe, 2, 3, lambda t: b_step(t, older=False))
            tiles(pe, 3, LT, b_step)
            tiles(pe, LT, LT + 1, lambda t: b_step(t, cur=False))
            tiles(pe, LT + 1, LT + 2, lambda t: b_step(t, cur=False, prev=False))
            tiles(pe, LT + 2, LT + 3, lambda t: b_step(t, cur=False, prev=False, old=False))

            def transpose_rows(t):
                pe.wait_ge(s(f"xg_in{t.p}"), 16 * CT * (t.half + 1))
                if not (isinstance(t.i, int) and t.i == 0):
                    pe.wait_ge(s("xgT_low"), DC * t.i)
                for dc in range(DC):
                    for c in range(CT):
                        m = pe.transpose(bank[4 + dc][:, c * P:(c + 1) * P], xg[t.p][:, c, dc * P:(dc + 1) * P], ident[:])
                    m.then_inc(s("xg_T"), 1)

            def hidden(t, hc):
                if hc == 0:
                    pe.wait_ge(s("xgT_low"), DC * (t.i + 1))
                pe.wait_ge(s("w1_split"), HC * t.i + hc + 1)
                if not (isinstance(t.i, int) and t.i == 0 and hc < 2):
                    pe.wait_ge(s("gelu"), HC * t.i + hc - 1)
                for dc in range(DC):
                    m = three(bank[6 + hc % 2][:], [w1s[h][:, dc, hc * P:(hc + 1) * P] for h in range(2)],
                              [xgT[t.p][h][:, dc] for h in range(2)], dc == 0, dc == DC - 1)
                m.then_inc(s("h_mm"), 1)

            def outputs(t, hc):
                if isinstance(t.i, int) and t.i == 0:
                    pe.wait_ge(s("w2_first"), hc + 1)
                else:
                    pe.wait_ge(s("w2_split"), HC * (t.i - 1) + hc + 1)
                pe.wait_ge(s("hid_low"), HC * t.i + hc + 1)
                for c in range(CT):
                    if hc == 0 and not (isinstance(t.i, int) and t.i == 0):
                        pe.wait_ge(s("yb"), CT * (t.i - 1) + c + 1)
                    h = hs[hc % 2]
                    m = three(ysum(c), [h[n][:, c * P:(c + 1) * P] for n in range(2)],
                              [w2s[:, hc, n] for n in range(2)], hc == 0, hc == HC - 1)
                    m.then_inc(s("y_mm"), 1)

            def expert(t, first=False, last=False):
                for hc in range(HC):
                    hidden(t, hc)
                    if hc == AHEAD and not last:
                        transpose_rows(t.ahead(1))
                    if hc > 0:
                        outputs(t, hc - 1)
                    elif not first:
                        outputs(t.back(1), HC - 1)
            pe.wait_ge(s("counts"), LT)
            transpose_rows(Tile(0, 0, 0))
            expert(Tile(0, 0, 0), first=True)
            tiles(pe, 1, 2, expert)
            tiles(pe, 2, E - 2, expert)
            expert(Tile(E - 2, E // 2 - 1, 0))
            t = Tile(E - 1, E // 2 - 1, 1)
            expert(t, last=True)
            outputs(t, HC - 1)


_INS = ['x', 'ctx_1024', 'g_xattn', 'g_ffn', 'L0_xattn_Wq_c', 'L0_xattn_bq_c', 'L0_xattn_Wk_s', 'L0_xattn_bk_s',
        'L0_xattn_Wv_s', 'L0_xattn_bv_s', 'L0_xattn_Wq_s', 'L0_xattn_bq_s', 'L0_xattn_Wk_c', 'L0_xattn_bk_c',
        'L0_xattn_Wv_c', 'L0_xattn_bv_c', 'L0_xattn_Wg', 'L0_xattn_bg', 'L0_ffn_Wg', 'L0_ffn_W1', 'L0_ffn_b1',
        'L0_ffn_W2', 'L0_ffn_b2']


def kernel(**inputs):
    import numpy as _np
    import concourse.bacc as _bacc
    from concourse import mybir as _mybir
    from concourse.bass_utils import run_bass_kernel_spmd as _run

    nc = _bacc.Bacc("TRN2", target_bir_lowering=False, num_devices=1)
    arrays, args = {}, []
    for name in _INS:
        a = _np.ascontiguousarray(inputs[name])
        arrays[f"in_{name}_dram"] = a
        args.append(nc.dram_tensor(f"in_{name}_dram", a.shape, _mybir.dt.from_np(a.dtype), kind="ExternalInput").ap())
    out = nc.dram_tensor("out_0_dram", (1, L, D), _mybir.dt.float32, kind="ExternalOutput").ap()
    program(nc, *args, out)
    r = _run(nc, [arrays], core_ids=[0])
    return r.results[0]["out_0_dram"]
```
